# Optimizing a Trainium2 kernel written in Bass

```python
import numpy as np
import jax
import jax.numpy as jnp

def _softmax(x, axis=-1):
    return jax.nn.softmax(x, axis=axis)

def _gelu(x):
    return jax.nn.gelu(x, approximate=True)

def _silu(x):
    return jax.nn.silu(x)

def _sigmoid(x):
    return jax.nn.sigmoid(x)

def _layernorm(x, axis=-1, eps=1e-05):
    m = jnp.mean(x, axis=axis, keepdims=True)
    v = jnp.var(x, axis=axis, keepdims=True)
    return (x - m) / jnp.sqrt(v + eps)

def _scatter_add(tgt, idx, src, axis=0):
    return tgt.at[idx].add(src)

def _segment_sum(src, seg, n):
    return jax.ops.segment_sum(src, seg, n)
kernel_name = 'mk_xattn_seq_d2_seqx_r4_0f86f0'

def setup_inputs(seed: int=0):
    np.random.seed(seed)
    _w = jnp.asarray

    def _rec_inputs():
        import jax
        import jax.numpy as jnp
        _rk = jax.random.key(seed)
        x = 7.22e-05 + 1 * jax.random.normal(jax.random.fold_in(_rk, 1), (4, 512, 512), jnp.float32)
        _lenS = 512 - jax.random.randint(jax.random.fold_in(_rk, 7), (4,), 0, max(1, 512 // 4) + 1, jnp.int32)
        _lenS2 = 64 - jax.random.randint(jax.random.fold_in(_rk, 8), (4,), 0, max(1, 64 // 4) + 1, jnp.int32)
        _ctx_2048P = jax.random.normal(jax.random.fold_in(_rk, 11), (4, 16, 512), jnp.float32)
        _ctx_2048c = jax.random.dirichlet(jax.random.fold_in(_rk, 511), 0.3 * jnp.ones((16,), jnp.float32), (4, 64))
        _ctx_2048t = jnp.einsum('bsk,bkd->bsd', _ctx_2048c, _ctx_2048P)
        _ctx_2048t = _ctx_2048t * jax.lax.rsqrt(jnp.mean(jnp.square(_ctx_2048t)) + 1e-12) * 0.953939
        ctx_2048 = 2.81802e-05 + 1.00001 * (_ctx_2048t + 0.3 * jax.random.normal(jax.random.fold_in(_rk, 611), (4, 64, 512), jnp.float32))
        _validS = jnp.arange(512)[None, :] < _lenS[:, None]
        _validS2 = jnp.arange(64)[None, :] < _lenS2[:, None]
        _causal = jnp.tril(jnp.ones((512, 512), dtype=bool))
        mask_BxS2_bf1 = jnp.ones((4, 64), dtype=bool)
        mask_BxS2_ik0 = jnp.where(jnp.broadcast_to(_validS2[:, :], (4, 64)), 0, 1).astype(jnp.int32)
        return (x, ctx_2048, mask_BxS2_bf1, mask_BxS2_ik0)
    x, ctx_2048, mask_BxS2_bf1, mask_BxS2_ik0 = _rec_inputs()

    def _L0_xattn_setup():
        import jax, jax.numpy as jnp
        import numpy as np
        D = 512
        H = 16
        HD = D // H
        INNER = 4 * D
        EPS = 1e-05

        def layer_norm(x, w, b):
            mu = jnp.mean(x, axis=-1, keepdims=True)
            var = jnp.mean(jnp.square(x - mu), axis=-1, keepdims=True)
            return (x - mu) * jax.lax.rsqrt(var + EPS) * w + b
        key = jax.random.key(seed)
        ks = jax.random.split(key, 12)
        B, LQ, LK = (4, 256, 512)
        std = 0.02
        inp = {'hidden_states': jax.random.normal(ks[0], (B, LQ, D), jnp.float32), 'encoder_hidden_states': jax.random.normal(ks[1], (B, LK, D), jnp.float32), 'encoder_attention_mask': jnp.ones((B, LK), dtype=bool), 'ln1_w': jnp.ones((D,), jnp.float32), 'ln1_b': jnp.zeros((D,), jnp.float32), 'q_w': jax.random.normal(ks[2], (D, D), jnp.float32) * std, 'q_b': jnp.zeros((D,), jnp.float32), 'k_w': jax.random.normal(ks[3], (D, D), jnp.float32) * std, 'k_b': jnp.zeros((D,), jnp.float32), 'v_w': jax.random.normal(ks[4], (D, D), jnp.float32) * std, 'v_b': jnp.zeros((D,), jnp.float32), 'cproj_w': jax.random.normal(ks[5], (D, D), jnp.float32) * std, 'cproj_b': jnp.zeros((D,), jnp.float32), 'ln2_w': jnp.ones((D,), jnp.float32), 'ln2_b': jnp.zeros((D,), jnp.float32), 'fc_w': jax.random.normal(ks[6], (D, INNER), jnp.float32) * std, 'fc_b': jnp.zeros((INNER,), jnp.float32), 'proj_w': jax.random.normal(ks[7], (INNER, D), jnp.float32) * std, 'proj_b': jnp.zeros((D,), jnp.float32)}
        return inp
    _L0_xattn_all = _L0_xattn_setup()
    _L0_xattn_in = {k: v for k, v in _L0_xattn_all.items() if k in ('ln1_w', 'ln1_b', 'q_w', 'q_b', 'k_w', 'k_b', 'v_w', 'v_b', 'cproj_w', 'cproj_b', 'ln2_w', 'ln2_b', 'fc_w', 'fc_b', 'proj_w', 'proj_b')}
    del _L0_xattn_all

    def _L1_xattn_setup():
        import jax, jax.numpy as jnp
        import numpy as np
        B, P, K, H, NH = (4, 512, 64, 512, 16)
        DH = H // NH
        EPS = 1e-06

        def rmsnorm(x, w):
            var = jnp.mean(jnp.square(x), axis=-1, keepdims=True)
            return x * jax.lax.rsqrt(var + EPS) * w
        key = jax.random.key(seed)
        ks = jax.random.split(key, 12)
        s = 0.02
        return {'x': jax.random.normal(ks[0], (B, P, H), jnp.float32), 'latents': jax.random.normal(ks[1], (B, K, H), jnp.float32), 'attention_mask': jax.random.randint(ks[2], (B, P), 0, 2, jnp.int32), 'q_w': s * jax.random.normal(ks[3], (H, H), jnp.float32), 'q_b': jnp.zeros((H,), jnp.float32), 'kv_w': s * jax.random.normal(ks[4], (H, 2 * H), jnp.float32), 'kv_b': jnp.zeros((2 * H,), jnp.float32), 'out_w': s * jax.random.normal(ks[5], (H, H), jnp.float32), 'out_b': jnp.zeros((H,), jnp.float32), 'postnorm_w': jnp.ones((H,), jnp.float32), 'mlp_w1': s * jax.random.normal(ks[6], (H, 4 * H), jnp.float32), 'mlp_b1': jnp.zeros((4 * H,), jnp.float32), 'mlp_w2': s * jax.random.normal(ks[7], (4 * H, H), jnp.float32), 'mlp_b2': jnp.zeros((H,), jnp.float32)}
    _L1_xattn_all = _L1_xattn_setup()
    _L1_xattn_in = {k: v for k, v in _L1_xattn_all.items() if k in ('q_w', 'q_b', 'kv_w', 'kv_b', 'out_w', 'out_b', 'postnorm_w', 'mlp_w1', 'mlp_b1', 'mlp_w2', 'mlp_b2')}
    del _L1_xattn_all
    return {'x': x, 'ctx_2048': ctx_2048, 'mask_BxS2_bf1': mask_BxS2_bf1, 'mask_BxS2_ik0': mask_BxS2_ik0, 'L0_xattn_ln1_w': _L0_xattn_in['ln1_w'], 'L0_xattn_ln1_b': _L0_xattn_in['ln1_b'], 'L0_xattn_q_w': _L0_xattn_in['q_w'], 'L0_xattn_q_b': _L0_xattn_in['q_b'], 'L0_xattn_k_w': _L0_xattn_in['k_w'], 'L0_xattn_k_b': _L0_xattn_in['k_b'], 'L0_xattn_v_w': _L0_xattn_in['v_w'], 'L0_xattn_v_b': _L0_xattn_in['v_b'], 'L0_xattn_cproj_w': _L0_xattn_in['cproj_w'], 'L0_xattn_cproj_b': _L0_xattn_in['cproj_b'], 'L0_xattn_ln2_w': _L0_xattn_in['ln2_w'], 'L0_xattn_ln2_b': _L0_xattn_in['ln2_b'], 'L0_xattn_fc_w': _L0_xattn_in['fc_w'], 'L0_xattn_fc_b': _L0_xattn_in['fc_b'], 'L0_xattn_proj_w': _L0_xattn_in['proj_w'], 'L0_xattn_proj_b': _L0_xattn_in['proj_b'], 'L1_xattn_q_w': _L1_xattn_in['q_w'], 'L1_xattn_q_b': _L1_xattn_in['q_b'], 'L1_xattn_kv_w': _L1_xattn_in['kv_w'], 'L1_xattn_kv_b': _L1_xattn_in['kv_b'], 'L1_xattn_out_w': _L1_xattn_in['out_w'], 'L1_xattn_out_b': _L1_xattn_in['out_b'], 'L1_xattn_postnorm_w': _L1_xattn_in['postnorm_w'], 'L1_xattn_mlp_w1': _L1_xattn_in['mlp_w1'], 'L1_xattn_mlp_b1': _L1_xattn_in['mlp_b1'], 'L1_xattn_mlp_w2': _L1_xattn_in['mlp_w2'], 'L1_xattn_mlp_b2': _L1_xattn_in['mlp_b2']}

def reference(x, ctx_2048, mask_BxS2_bf1, mask_BxS2_ik0, L0_xattn_ln1_w, L0_xattn_ln1_b, L0_xattn_q_w, L0_xattn_q_b, L0_xattn_k_w, L0_xattn_k_b, L0_xattn_v_w, L0_xattn_v_b, L0_xattn_cproj_w, L0_xattn_cproj_b, L0_xattn_ln2_w, L0_xattn_ln2_b, L0_xattn_fc_w, L0_xattn_fc_b, L0_xattn_proj_w, L0_xattn_proj_b, L1_xattn_q_w, L1_xattn_q_b, L1_xattn_kv_w, L1_xattn_kv_b, L1_xattn_out_w, L1_xattn_out_b, L1_xattn_postnorm_w, L1_xattn_mlp_w1, L1_xattn_mlp_b1, L1_xattn_mlp_w2, L1_xattn_mlp_b2):
    import jax
    import jax.numpy as jnp

    def _L0_xattn_ref(hidden_states, encoder_hidden_states, encoder_attention_mask, ln1_w, ln1_b, q_w, q_b, k_w, k_b, v_w, v_b, cproj_w, cproj_b, ln2_w, ln2_b, fc_w, fc_b, proj_w, proj_b):
        import jax, jax.numpy as jnp
        import numpy as np
        D = 512
        H = 16
        HD = D // H
        INNER = 4 * D
        EPS = 1e-05

        def layer_norm(x, w, b):
            mu = jnp.mean(x, axis=-1, keepdims=True)
            var = jnp.mean(jnp.square(x - mu), axis=-1, keepdims=True)
            return (x - mu) * jax.lax.rsqrt(var + EPS) * w + b
        B, LQ, _ = hidden_states.shape
        LK = encoder_hidden_states.shape[1]
        residual = hidden_states
        x = layer_norm(hidden_states, ln1_w, ln1_b)
        q = (x @ q_w + q_b).reshape(B, LQ, H, HD).transpose(0, 2, 1, 3)
        k = (encoder_hidden_states @ k_w + k_b).reshape(B, LK, H, HD).transpose(0, 2, 1, 3)
        v = (encoder_hidden_states @ v_w + v_b).reshape(B, LK, H, HD).transpose(0, 2, 1, 3)
        scale = 1.0 / np.sqrt(HD).astype(np.float32)
        scores = jnp.einsum('bhqd,bhkd->bhqk', q, k) * scale
        mask = encoder_attention_mask[:, None, None, :]
        mask_value = jnp.finfo(scores.dtype).min
        scores = jnp.where(mask, scores, mask_value)
        attn = jax.nn.softmax(scores, axis=-1)
        out = jnp.einsum('bhqk,bhkd->bhqd', attn, v)
        out = out.transpose(0, 2, 1, 3).reshape(B, LQ, D)
        out = out @ cproj_w + cproj_b
        hidden = out + residual
        residual = hidden
        y = layer_norm(hidden, ln2_w, ln2_b)
        y = jax.nn.gelu(y @ fc_w + fc_b, approximate=True)
        y = y @ proj_w + proj_b
        return residual + y

    def _L1_xattn_ref(x, latents, attention_mask, q_w, q_b, kv_w, kv_b, out_w, out_b, postnorm_w, mlp_w1, mlp_b1, mlp_w2, mlp_b2):
        import jax, jax.numpy as jnp
        import numpy as np
        B, P, K, H, NH = (4, 512, 64, 512, 16)
        DH = H // NH
        EPS = 1e-06

        def rmsnorm(x, w):
            var = jnp.mean(jnp.square(x), axis=-1, keepdims=True)
            return x * jax.lax.rsqrt(var + EPS) * w
        b, p, _ = x.shape
        k_len = latents.shape[1]
        residual = latents
        h = jnp.concatenate([x, latents], axis=1)
        q = (latents @ q_w + q_b).reshape(b, k_len, NH, DH)
        kv = (h @ kv_w + kv_b).reshape(b, p + k_len, NH, DH, 2)
        kmat, v = (kv[..., 0], kv[..., 1])
        attn = jnp.einsum('bkhd,bnhd->bhkn', q, kmat) / DH
        full_mask = jnp.concatenate([attention_mask.astype(bool), jnp.ones((b, k_len), bool)], axis=-1)
        attn = jnp.where(full_mask[:, None, None, :], attn, -jnp.inf)
        attn = jax.nn.softmax(attn.astype(jnp.float32), axis=-1).astype(q.dtype)
        attn_out = jnp.einsum('bhkn,bnhd->bkhd', attn, v).reshape(b, k_len, H)
        attn_out = attn_out @ out_w + out_b + residual
        out = rmsnorm(attn_out, postnorm_w)
        out = jax.nn.gelu(out @ mlp_w1 + mlp_b1) @ mlp_w2 + mlp_b2
        return out + residual
    x = _L0_xattn_ref(x, ctx_2048, mask_BxS2_bf1, L0_xattn_ln1_w, L0_xattn_ln1_b, L0_xattn_q_w, L0_xattn_q_b, L0_xattn_k_w, L0_xattn_k_b, L0_xattn_v_w, L0_xattn_v_b, L0_xattn_cproj_w, L0_xattn_cproj_b, L0_xattn_ln2_w, L0_xattn_ln2_b, L0_xattn_fc_w, L0_xattn_fc_b, L0_xattn_proj_w, L0_xattn_proj_b)
    x = _L1_xattn_ref(ctx_2048, x, mask_BxS2_ik0, L1_xattn_q_w, L1_xattn_q_b, L1_xattn_kv_w, L1_xattn_kv_b, L1_xattn_out_w, L1_xattn_out_b, L1_xattn_postnorm_w, L1_xattn_mlp_w1, L1_xattn_mlp_b1, L1_xattn_mlp_w2, L1_xattn_mlp_b2)
    return x

_drawn_inputs = setup_inputs


def setup_inputs(seed=0):
    import zlib

    import numpy as np

    out = dict(_drawn_inputs(seed))
    spreads = {'L0_xattn_ln1_w': (1.0, 0.6),
     'L0_xattn_ln1_b': (0.0, 0.8),
     'L0_xattn_q_b': (0.0, 0.8),
     'L0_xattn_k_b': (0.0, 2.0),
     'L0_xattn_v_b': (0.0, 0.1),
     'L0_xattn_cproj_b': (0.0, 0.1),
     'L0_xattn_ln2_w': (1.0, 0.2),
     'L0_xattn_ln2_b': (0.0, 0.361),
     'L0_xattn_fc_b': (0.0, 0.1),
     'L0_xattn_proj_b': (0.0, 0.1),
     'L1_xattn_q_b': (0.0, 0.8),
     'L1_xattn_kv_b': (0.0, 0.8),
     'L1_xattn_out_b': (0.0, 1.068),
     'L1_xattn_postnorm_w': (1.0, 0.2),
     'L1_xattn_mlp_b1': (0.0, 0.1),
     'L1_xattn_mlp_b2': (0.0, 0.1)}
    factors = {'L0_xattn_q_w': 6.58,
     'L0_xattn_k_w': 6.552,
     'L1_xattn_q_w': 8.0,
     'L1_xattn_kv_w': 6.268,
     'L1_xattn_out_w': 4.798}
    for name, (base, spread) in spreads.items():
        noise = np.random.default_rng([zlib.crc32(name.encode()), seed]).standard_normal(out[name].shape)
        drawn = base * np.exp(spread * noise) if base else spread * noise
        out[name] = jnp.asarray(drawn.astype(out[name].dtype))
    for name, factor in factors.items():
        out[name] = (out[name] * factor).astype(out[name].dtype)
    return out
```

```python
from contextlib import ExitStack

import concourse.bass as bass
from concourse import mybir

F32 = mybir.dt.float32
F32R = mybir.dt.float32r
U8 = mybir.dt.uint8
I32 = mybir.dt.int32
ACT = mybir.ActivationFunctionType
ALU = mybir.AluOpType
AX_X = mybir.AxisListType.X
ds = bass.ds

P = 128
B, S, D = 4, 512, 512
C = 64
H, HD = 16, 32
INNER = 4 * D
KT = D // P
TT = S // P
HG = P // HD
G = H // HG
NK = S + C
CT = TT
ROWMASK, ROWMAX = 3 * HD, 3 * HD + 1
VW = 2 * HD + 2
BIG = 2.0 ** 126
PRING = 3
LAG = 2
STK = 16 * (6 * HG + 1)
NGRP = INNER // D
NCH = D // P


class Layer:

    def __init__(self, index):
        self.index = index
        self.tiles = [CT] if index == 0 else list(range(TT + 1))
        self.main = index == 1
        self.scale = HD ** -0.5 if index == 0 else 1.0 / HD
        self.eps = 1e-5 if index == 0 else 1e-6
        v = [f"V{t}" for t in self.tiles]

        def key(c):
            return ([f"K{c}"] if self.main else []) + [f"KC{c}"]
        uses = [f"T{k}" for k in range(KT)] + ["C"] + v
        uses += ["Q0"] + key(0) + ["Q1"] + key(1) + ["R0"]
        for c in range(G):
            uses += [f"Q{c + 2}"] if c + 2 < G else []
            uses += [f"R{c + 1}"] if c + 1 < G else []
            uses += key(c + 2) if c + 2 < G else []
        uses += [f"O{t}" for t in range(TT)]
        self.uses = uses
        by_act = [u for u in uses if u[0] not in "RO"]
        self.use = {u: n for n, u in enumerate(uses)}
        self.act = {u: n for n, u in enumerate(by_act)}
        self.n_use, self.n_act = len(uses), len(by_act)
        self.n_step = H * len(self.tiles)
        self.steps = [(j, t) for j in range(HG) for t in self.tiles]


LAYERS = [Layer(0), Layer(1)]


def at(base, b, per, n):
    return b * per + (base + max(n, 0))


def program(nc, x, ctx, mask_bool, mask_int, w, x1, xm, x2, out):
    es = ExitStack()
    with es:
        def sb(name, shape, dt):
            return es.enter_context(nc.sbuf_tensor(name, shape, dt))

        def sem(name):
            return es.enter_context(nc.semaphore(name))

        bank = [es.enter_context(nc.psum_tensor(f"bank{i}", [P, 512], F32)) for i in range(8)]

        W = sb("W", [P, 4, 2, KT, D], F32R)
        raw = sb("raw", [P, 2, D], F32)
        ident = sb("ident", [P, P], F32)
        cols = sb("cols", [P, 80], F32)
        brow = sb("brow", [P, D], F32)
        stats = sb("stats", [P, TT, 6], F32)
        mv = sb("mv", [P, TT, 2], F32)
        sdev = sb("sdev", [P, TT], F32)
        rstd = sb("rstd", [P, TT], F32)
        anyk = sb("anyk", [P, B], F32)
        kbias = sb("kbias", [1, 2, B * C], F32R)
        zero = sb("zero", [1, 8], F32)

        NR_ATT = (2 * KT * S + 2 * KT * C + 2 * HG * S + 2 * HG * NK + 5 * H * VW
                  + 2 * PRING * S + 2 * S + 2 * NK + 2 * P)
        NR_MLP = 2 * KT * B * S + 2 * 4 * S
        RA = sb("RA", [P, max(NR_ATT, NR_MLP)], F32R)
        NF_ATT = PRING * S + 2 * S + KT * S + KT * S + D + 2 * S + 4 * 16
        NF_MLP = B * TT * D + TT * D
        FA = sb("FA", [P, max(NF_ATT, NF_MLP)], F32)

        def cut(arena, sizes):
            o, parts = 0, []
            for n in sizes:
                parts.append(arena[:, o:o + n])
                o += n
            return parts

        xT_, cT_, QS_, KS_, VP_, ph_, pl_, qt_, kt_, nT_ = cut(RA, [
            2 * KT * S, 2 * KT * C, 2 * HG * S, 2 * HG * NK, 5 * H * VW,
            PRING * S, PRING * S, 2 * S, 2 * NK, 2 * P])
        xT = xT_.rearrange("p (h k n) -> p h k n", h=2, k=KT)
        cT = cT_.rearrange("p (h k n) -> p h k n", h=2, k=KT)
        QS = QS_.rearrange("p (s j n) -> p s j n", s=2, j=HG)
        KS = KS_.rearrange("p (s j n) -> p s j n", s=2, j=HG)
        VP = VP_.rearrange("p (t h n) -> p t h n", t=5, h=H)
        ph = ph_.rearrange("p (r n) -> p r n", r=PRING)
        pl = pl_.rearrange("p (r n) -> p r n", r=PRING)
        qt = qt_.rearrange("p (h n) -> p h n", h=2)
        kt = kt_.rearrange("p (h n) -> p h n", h=2)
        nT = nT_.rearrange("p (s n) -> p s n", s=2)
        pf_, sg_, oa_, tok_, ct_, sr_, nm_ = cut(FA, [
            PRING * S, 2 * S, KT * S, KT * S, D, 2 * S, 4 * 16])
        pf = pf_.rearrange("p (r n) -> p r n", r=PRING)
        sg = sg_.rearrange("p (r n) -> p r n", r=2)
        oa = oa_.rearrange("p (k n) -> p k n", k=KT)
        tok = tok_.rearrange("p (t n) -> p t n", t=TT)
        rb = tok
        ctok = ct_
        s16, r16 = sr_[:, 0:S], sr_[:, S:2 * S]
        nm_main, nm_ctx, nm = nm_[:, 0:16], nm_[:, 16:32], nm_[:, 32:48]
        yT_, g_ = cut(RA, [2 * KT * B * S, 2 * 4 * S])
        yT = yT_.rearrange("p (h k n) -> p h k n", h=2, k=KT)
        gs = g_.rearrange("p (h r n) -> p h r n", h=2, r=4)
        acc_, nt_ = cut(FA, [B * TT * D, TT * D])
        nt = nt_.rearrange("p (t n) -> p t n", t=TT)
        gf = nt[:, 0:2, :]

        ident_ready = sem("ident_ready")
        par_loaded = sem("par_loaded")
        par_turned = sem("par_turned")
        consts = sem("consts")
        dve_own = sem("dve_own")
        brow_loaded = sem("brow_loaded")
        x_loaded = sem("x_loaded")
        c_loaded = sem("c_loaded")
        var_ready = sem("var_ready")
        sd_ready = sem("sd_ready")
        normed = sem("normed")
        pb_full = sem("pb_full")
        pb_free = sem("pb_free")
        act_out = sem("act_out")
        act_own = sem("act_own")
        stacked = [sem("stacked0"), sem("stacked1")]
        maxed = [sem("maxed0"), sem("maxed1")]
        mm_full = sem("mm_full")
        mm_free = sem("mm_free")
        mc_full = sem("mc_full")
        mc_free = sem("mc_free")
        nm_ready = sem("nm_ready")
        s_full = sem("s_full")
        p_exp = sem("p_exp")
        p_hi = sem("p_hi")
        p_lo = sem("p_lo")
        pv_step = sem("pv_step")
        sg_ready = sem("sg_ready")
        o_free = sem("o_free")
        o_moved = [sem("o_moved0"), sem("o_moved1")]
        r_ready = sem("r_ready")
        r_spread = sem("r_spread")
        scaled = sem("scaled")
        att_ready = sem("att_ready")
        x_again = sem("x_again")
        xb_ready = sem("xb_ready")
        stored = sem("stored")
        raw_loaded = [sem("raw_loaded0"), sem("raw_loaded1")]
        w_hi = sem("w_hi")
        w_lo = sem("w_lo")
        w_ready = sem("w_ready")
        acc_loaded = sem("acc_loaded")
        nt_loaded = sem("nt_loaded")
        t_full = sem("t_full")
        y_hi = sem("y_hi")
        y_ready = sem("y_ready")
        f_full = sem("f_full")
        g_act = sem("g_act")
        g_hi = sem("g_hi")
        g_lo = sem("g_lo")
        a_full = sem("a_full")
        acc_added = sem("acc_added")
        biased = sem("biased")

        order = ["ln1_w", "ln1_b", "q_b", "v_b", "k_b", "ln2_w", "ln2_b", "fc_b",
                 "q_b1", "k_b1", "v_b1", "post_w", "mlp_b1"]
        col, at_row = {}, 0
        for name in order:
            col[name] = at_row
            at_row += (4 * D if name in ("fc_b", "mlp_b1") else D) // P
        NPAR = at_row

        def par(name, k):
            return cols[:, col[name] + k:col[name] + k + 1]

        par_rows = tok_[0:NPAR, 0:P]
        maskf = oa_[:, 0:B * C]
        maskr = pf_[:, 0:B * C // 4].bitcast(U8)
        mask2 = sg_[0:1, 0:B * C].bitcast(I32)
        mask2f = sg_[0:1, 512:512 + B * C]

        def tokens(t):
            return t.rearrange("b (t p) d -> p b t d", p=P)

        src_of = [x, xm]
        mid_of = [x1, x2]
        dst_of = [xm, out]

        def base(L, per0):
            return B * per0 if L.index else 0

        passed = sem("passed")

        def wait_apart(eng, *waits):
            for sem_, v in waits:
                eng.wait_ge(sem_, v)
            eng.sem_inc(passed, 1)

        block = es.enter_context(nc.Block())

        @block.sync
        def _(sp):
            n = 0
            for name in order:
                rows = (4 * D if name in ("fc_b", "mlp_b1") else D) // P
                if name in ("k_b1", "v_b1"):
                    two = w["kv_b"].rearrange("(c n two) -> two c n", n=P, two=2)
                    with nc.allow_non_contiguous_dma(reason="kv_b interleaves k and v"):
                        sp.dma_start(par_rows[col[name]:col[name] + rows, :],
                                     two[int(name == "v_b1")]).then_inc(par_loaded, 16)
                else:
                    sp.dma_start(par_rows[col[name]:col[name] + rows, :],
                                 w[name].rearrange("(c n) -> c n", n=P)).then_inc(par_loaded, 16)
                n += 1
            sp.dma_start(maskr, mask_bool.rearrange("b c -> (b c)").partition_broadcast(P))\
                .then_inc(par_loaded, 16)
            sp.dma_start(mask2, mask_int.rearrange("(o b) c -> o (b c)", o=1)).then_inc(par_loaded, 16)
            sp.wait_ge(consts, 3)

            def attention(L):
                src, dst = tokens(src_of[L.index]), tokens(mid_of[L.index])
                if L.index:
                    sp.wait_ge(stored, 16 * 4 * B * 2)
                sp.dma_start(brow[:, :], w["cproj_b" if L.index == 0 else "out_b"].partition_broadcast(P))\
                    .then_inc(brow_loaded, 16)
                U = L.n_use
                ub = base(L, LAYERS[0].n_use)
                sb_ = base(L, LAYERS[0].n_step)
                nS = len(L.steps)
                k0 = 0 if L.main else S
                with sp.Fori(0, B) as b:
                    wait_apart(sp, (stored, at(16 * 4 * B * 2 * L.index, b, 64, 0)))
                    sp.dma_start(tok, src[:, ds(b, 1), :, :]).then_inc(x_loaded, 16)
                    sp.dma_start(ctok[0:C, :], ctx[ds(b, 1), :, :].rearrange("o c d -> (o c) d"))\
                        .then_inc(c_loaded, 16)

                    def q_stack(c):
                        wait_apart(sp, (pb_free, at(ub, b, U, L.use[f"Q{c}"] + 1)))
                        if c >= 2:
                            wait_apart(sp, (s_full, at(sb_, b, L.n_step, (c - 1) * nS)))
                        for r, half in ((0, 0), (HD, 0), (2 * HD, 1)):
                            for j in range(HG):
                                sp.dma_start(QS[r:r + HD, c % 2, j, :].bitcast(F32), qt[HD * j:HD * j + HD, half, :].bitcast(F32))\
                                    .then_inc(stacked[c % 2], 16)

                    def k_stack(c):
                        sp.wait_ge(pb_free, at(ub, b, U, L.use[f"KC{c}"] + 1))
                        for r, half in ((0, 0), (HD, 1), (2 * HD, 0)):
                            for j in range(HG):
                                sp.dma_start(KS[r:r + HD, c % 2, j, k0:].bitcast(F32), kt[HD * j:HD * j + HD, half, k0:].bitcast(F32))\
                                    .then_inc(stacked[c % 2], 16)
                        sp.dma_start(KS[ROWMASK:ROWMASK + 1, c % 2, :, S:NK].bitcast(F32),
                                     kbias[0:1, L.index, ds(b * C, C)].bitcast(F32).unsqueeze(1).to_broadcast([1, HG, C]))\
                            .then_inc(stacked[c % 2], 16)

                    def max_row(c):
                        sp.wait_ge(pb_free, at(ub, b, U, L.use[f"R{c}"] + 1))
                        sp.dma_start(QS[ROWMAX:ROWMAX + 1, c % 2, :, :].rearrange("o j (q n) -> o (j q) n", n=P).bitcast(F32),
                                     nT[0:16, c % 2, :].bitcast(F32)).then_inc(maxed[c % 2], 16)

                    def o_move(c, j):
                        h = HG * c + j
                        hb = base(L, H)
                        sp.wait_ge(o_free, at(hb, b, H, h + 1))
                        sp.dma_start(oa[HD * j:HD * j + HD, c, :], sg[0:HD, h % 2, :])\
                            .then_inc(o_moved[h % 2], 16)
                        sp.dma_start(s16[4 * j + c:4 * j + c + 1, :], sg[2 * HD:2 * HD + 1, h % 2, :])\
                            .then_inc(o_moved[h % 2], 16)

                    q_stack(0)
                    k_stack(0)
                    q_stack(1)
                    k_stack(1)
                    max_row(0)
                    for c in range(G):
                        for j in range(HG - 1):
                            o_move(c, j)
                        if c + 2 < G:
                            q_stack(c + 2)
                        if c + 1 < G:
                            max_row(c + 1)
                        if c + 2 < G:
                            k_stack(c + 2)
                        o_move(c, HG - 1)
                    sp.wait_ge(r_ready, at(base(L, 1), b, 1, 1))
                    for j in range(HG):
                        for c in range(G):
                            row = r16[4 * j + c:4 * j + c + 1, :]
                            sp.dma_start(rb[HD * j:HD * j + HD, c, :],
                                         row.unsqueeze(1).to_broadcast([1, HD, S])).then_inc(r_spread, 16)
                    wait_apart(sp, (scaled, at(base(L, KT), b, KT, KT)))
                    sp.dma_start(tok, src[:, ds(b, 1), :, :]).then_inc(x_again, 16)
                    for t in range(TT):
                        sp.wait_ge(pb_free, at(ub, b, U, L.use[f"O{t}"] + 1))
                        sp.dma_start(dst[:, ds(b, 1), t:t + 1, :], tok[:, t:t + 1, :]).then_inc(stored, 16)

            def mlp(L):
                st = 16 * 4 * B * (2 * L.index + 1)
                sp.wait_ge(stored, st)
                sp.dma_start(brow[:, :], w["proj_b" if L.index == 0 else "mlp_b2"].partition_broadcast(P))\
                    .then_inc(brow_loaded, 16)
                res = tokens(x1 if L.index == 0 else xm)
                mid, dst = tokens(mid_of[L.index]), tokens(dst_of[L.index])
                with sp.Fori(0, B) as b:
                    sp.dma_start(acc_[:, ds(b * TT * D, TT * D)].rearrange("p (t d) -> p t d", d=D),
                                 res[:, ds(b, 1), :, :]).then_inc(acc_loaded, 16)
                    wait_apart(sp, (t_full, at(base(L, KT), b, KT, 0)))
                    sp.dma_start(nt, mid[:, ds(b, 1), :, :]).then_inc(nt_loaded, 16)
                with sp.Fori(0, B) as b:
                    sp.wait_ge(acc_added, at(base(L, NGRP * TT) + (NGRP - 1) * B * TT, b, TT, TT))
                    sp.dma_start(dst[:, ds(b, 1), :, :],
                                 acc_[:, ds(b * TT * D, TT * D)].rearrange("p (t d) -> p t d", d=D))\
                        .then_inc(stored, 64)

            for L in LAYERS:
                attention(L)
                mlp(L)
            sp.wait_ge(stored, 16 * 4 * B * 4)

        @block.gpsimd
        def _(pool):
            pool.memset(ident[:], 0.0).then_inc(ident_ready, 1)
            pool.wait_ge(ident_ready, 1)
            pool.affine_select(out=ident[:], in_=ident[:], compare_op=ALU.not_equal, fill=1.0,
                               base=0, pattern=[[-1, P]], channel_multiplier=1).then_inc(ident_ready, 1)

            def split(dsts, srcs, u, before, done):
                pool.wait_ge(raw_loaded[u % 2], 16 * ((before + u) // 2) + 16)
                for (hi, _), s in zip(dsts, srcs):
                    last = pool.tensor_scalar(hi, s, 1.0, 0.0, ALU.mult, ALU.add)
                last.then_inc(w_hi, 1)
                pool.wait_ge(w_hi, before + u + 1)
                for (hi, lo), s in zip(dsts, srcs):
                    last = pool.tensor_tensor(lo, s, hi.bitcast(F32), ALU.subtract)
                last.then_inc(w_lo, 1)

            def units(srcs, before, put):
                for u, s in enumerate(srcs):
                    if u == 0:
                        pool.wait_ge(w_lo, before)
                        pool.dma_start(raw[:, 0, :], s).then_inc(raw_loaded[0], 16)
                    if u + 1 < len(srcs):
                        if before + u:
                            pool.wait_ge(w_lo, before + u)
                        pool.dma_start(raw[:, (u + 1) % 2, :], srcs[u + 1]).then_inc(raw_loaded[(u + 1) % 2], 16)
                    put(u)

            def rows(m, k, c0=0):
                return m[k * P:(k + 1) * P, c0:c0 + D]

            NU = 4 * KT + 2 * KT * NGRP

            def attention_weights(L):
                before = NU * L.index
                if L.index == 0:
                    for s, name in enumerate(("q_w", "k_w", "v_w", "cproj_w")):
                        def put(u, s=s):
                            split([(W[:, s, 0, u, :], W[:, s, 1, u, :])], [raw[:, u % 2, :]], u,
                                  before + s * KT, u == KT - 1)
                        units([rows(w[name], k) for k in range(KT)], before + s * KT, put)
                    return
                its = NGRP * B * TT
                pool.wait_ge(a_full, its - B * TT)
                def put_q(u):
                    split([(W[:, 0, 0, u, :], W[:, 0, 1, u, :])], [raw[:, u % 2, :]], u, before, False)
                units([rows(w["q_w1"], k) for k in range(KT)], before, put_q)
                pool.wait_ge(a_full, its)
                def put_kv(u):
                    k, half = u // 2, u % 2
                    pair = raw[:, u % 2, :].rearrange("p (n two) -> p two n", two=2)
                    c0 = half * (D // 2)
                    split([(W[:, 1 + i, 0, k, c0:c0 + D // 2], W[:, 1 + i, 1, k, c0:c0 + D // 2]) for i in (0, 1)],
                          [pair[:, i, :] for i in (0, 1)], u, before + KT, False)
                units([rows(w["kv_w"], u // 2, (u % 2) * D) for u in range(2 * KT)], before + KT, put_kv)
                def put_o(u):
                    split([(W[:, 3, 0, u, :], W[:, 3, 1, u, :])], [raw[:, u % 2, :]], u, before + 3 * KT, False)
                units([rows(w["out_w"], k) for k in range(KT)], before + 3 * KT, put_o)

            def mlp_weights(L):
                before = NU * L.index + 4 * KT
                ub = base(L, LAYERS[0].n_use)
                w1 = w["fc_w" if L.index == 0 else "mlp_w1"]
                w2 = w["proj_w" if L.index == 0 else "mlp_w2"]
                for g in range(NGRP):
                    slot = 2 * (g % 2)
                    if g == 0:
                        pool.wait_ge(pb_full, at(ub, B - 1, L.n_use, L.use["KC3"] + 1))
                    elif g == 1:
                        pool.wait_ge(pb_full, at(ub, B, L.n_use, 0))
                    else:
                        pool.wait_ge(a_full, base(L, NGRP * TT) + (g - 1) * B * TT)
                    def put(u, slot=slot, g=g):
                        s, k = slot + u // KT, u % KT
                        split([(W[:, s, 0, k, :], W[:, s, 1, k, :])], [raw[:, u % 2, :]], u,
                              before + g * 2 * KT, False)
                    units([rows(w1, k, g * D) for k in range(KT)]
                          + [rows(w2, g * KT + k) for k in range(KT)], before + g * 2 * KT, put)

            def attention(L):
                pb = base(L, LAYERS[0].n_step)
                with pool.Fori(0, B) as b:
                    for i in range(L.n_step):
                        n = C if L.tiles[i % len(L.tiles)] == CT else P
                        wait_apart(pool, (p_exp, at(pb, b, L.n_step, i + 1)), (pv_step, at(pb, b, L.n_step, i - PRING + 1)))
                        pool.tensor_scalar(ph[0:n, i % PRING, :], pf[0:n, i % PRING, :], 1.0, 0.0,
                                           ALU.mult, ALU.add).then_inc(p_hi, 1)
                    pool.wait_ge(x_again, at(base(L, 16), b, 16, 16))
                    pool.wait_ge(brow_loaded, 16 * (2 * L.index + 1))
                    for t in range(TT):
                        pool.tensor_tensor(tok[:, t, :], tok[:, t, :], brow[:, :], ALU.add).then_inc(xb_ready, 1)

            for L in LAYERS:
                attention_weights(L)
                attention(L)
                mlp_weights(L)

        @block.scalar
        def _(act):
            def attention(L):
                ub, sb_, ab, hb = (base(L, n) for n in (LAYERS[0].n_use, LAYERS[0].n_step, LAYERS[0].n_act, H))
                nS = len(L.steps)
                qb, kb = ("q_b", "k_b") if L.index == 0 else ("q_b1", "k_b1")
                with act.Fori(0, B) as b:
                    def full(u):
                        act.wait_ge(pb_full, at(ub, b, L.n_use, L.use[u] + 1))
                        return bank[L.use[u] % 2]

                    if L.index == 0:
                        act.wait_ge(var_ready, at(0, b, 1, 1))
                        act.activation(sdev[:, :], mv[:, :, 1], ACT.Sqrt, bias=cols[:, NPAR:NPAR + 1])\
                            .then_inc(sd_ready, 1)
                    for k in range(KT):
                        src = full(f"T{k}")
                        if L.index == 0:
                            act.activation(src[:, :], src[:, :], ACT.Identity, bias=par("ln1_b", k),
                                           scale=par("ln1_w", k)).then_inc(act_own, 1)
                            act.wait_ge(act_own, at(0, b, KT, k + 1))
                        act.activation(xT[:, 0, k, :], src[:, :], ACT.Copy).then_inc(act_out, 1)
                    src = full("C")
                    act.activation(cT[:, 0, :, :], src[:, 0:KT * C].rearrange("p (k n) -> p k n", k=KT),
                                   ACT.Copy).then_inc(act_out, 1)
                    for t in L.tiles:
                        src = full(f"V{t}")
                        n = C if t == CT else P
                        act.activation(VP[0:n, t, :, 0:HD], src[0:n, :].rearrange("p (h d) -> p h d", h=H),
                                       ACT.Copy).then_inc(act_out, 1)

                    def q_hi(c):
                        src = full(f"Q{c}")
                        if c:
                            act.wait_ge(stacked[(c - 1) % 2], at(base(L, 2 * STK), b, 2 * STK, STK * ((c - 1) // 2 + 1)))
                        act.activation(qt[:, 0, :], src[:, :], ACT.Identity, bias=par(qb, c)).then_inc(act_out, 1)

                    def k_hi(c):
                        for u in ([f"K{c}"] if L.main else []) + [f"KC{c}"]:
                            src = full(u)
                            o, n = (0, S) if u[:2] != "KC" else (S, C)
                            act.activation(kt[:, 0, o:o + n], src[:, 0:n], ACT.Identity, bias=par(kb, c))\
                                .then_inc(act_out, 1)

                    def exp(c, i):
                        n = c * nS + i
                        rows = C if L.steps[i][1] == CT else P
                        wait_apart(act, (s_full, at(sb_, b, L.n_step, n + 1)), (p_lo, at(sb_, b, L.n_step, n - PRING + 1)))
                        act.activation(pf[0:rows, n % PRING, :], bank[4 + n % 2][0:rows, :], ACT.Exp,
                                       scale=L.scale if L.index else anyk[0:rows, ds(b, 1)]).then_inc(p_exp, 1)

                    def o_out(h):
                        act.wait_ge(pv_step, at(sb_, b, L.n_step, (h + 1) * len(L.tiles)))
                        act.wait_ge(o_moved[h % 2], at(base(L, 256), b, 256, 32 * (h // 2)))
                        act.activation(sg[0:2 * HD + 1, h % 2, :], bank[6 + h % 2][0:2 * HD + 1, :], ACT.Copy)\
                            .then_inc(sg_ready, 1)

                    q_hi(0)
                    k_hi(0)
                    q_hi(1)
                    k_hi(1)
                    per = len(L.tiles)
                    for c in range(G):
                        done = 0
                        for i in range(nS):
                            exp(c, i)
                            if done < HG - 1 and i == (done + 1) * per - 1 + LAG + 1:
                                o_out(HG * c + done)
                                done += 1
                        if per == 1:
                            for j in range(done, HG - 1):
                                o_out(HG * c + j)
                        elif done < HG - 1:
                            raise AssertionError
                        if c + 2 < G:
                            q_hi(c + 2)
                            k_hi(c + 2)
                        o_out(HG * c + HG - 1)

            def mlp(L):
                nb = base(L, KT)
                gb = base(L, NGRP * NCH)
                with act.Fori(0, B) as b:
                    act.wait_ge(var_ready, at(B + B * L.index, b, 1, 1))
                    act.activation(sdev[:, :], mv[:, :, 1], ACT.Sqrt,
                                   bias=cols[:, NPAR + L.index:NPAR + L.index + 1]).then_inc(sd_ready, 1)
                    for k in range(KT):
                        act.wait_ge(t_full, at(nb, b, KT, k + 1))
                        src = bank[k]
                        if L.index == 0:
                            act.activation(src[:, :], src[:, :], ACT.Identity, bias=par("ln2_b", k),
                                           scale=par("ln2_w", k)).then_inc(act_own, 1)
                            wait_apart(act, (act_own, at(KT * B, b, KT, k + 1)))
                        else:
                            act.activation(src[:, :], src[:, :], ACT.Copy, scale=par("post_w", k))\
                                .then_inc(act_own, 1)
                            wait_apart(act, (act_own, at(2 * KT * B, b, KT, k + 1)))
                        act.activation(yT[:, 0, k, ds(b * S, S)], src[:, :], ACT.Copy).then_inc(y_hi, 1)
                b1 = col["fc_b" if L.index == 0 else "mlp_b1"]
                with act.Fori(0, NGRP // 2) as gg:
                    for s in range(2):
                        with act.Fori(0, B) as b:
                            it = gg * (2 * B * NCH) + b * NCH
                            for i in range(NCH):
                                n = gb + s * B * NCH + i
                                wait_apart(act, (f_full, it + (n + 1)), (g_lo, it + (n - min(i, 1))))
                                act.activation(gf[:, i % 2, :], bank[i][:, :], ACT.Gelu_apprx_tanh,
                                               bias=cols[:, ds(gg * (2 * NCH) + (b1 + s * NCH + i), 1)])\
                                    .then_inc(g_act, 1)

            act.wait_ge(consts, 3)
            for L in LAYERS:
                attention(L)
                mlp(L)

        @block.vector
        def _(dve):
            own = [0]

            def link(ins):
                own[0] += 1
                ins.then_inc(dve_own, 1)
                dve.wait_ge(dve_own, own[0])

            dve.memset(cols[:, NPAR:NPAR + 1], 1e-5).then_inc(consts, 1)
            dve.memset(cols[:, NPAR + 1:NPAR + 2], 1e-6).then_inc(consts, 1)
            dve.wait_ge(par_turned, 1)
            link(dve.tensor_copy(cols[:, 0:NPAR], bank[0][:, 0:NPAR]))
            link(dve.tensor_copy(maskf, maskr))
            link(dve.tensor_reduce(anyk[:, :], maskf.rearrange("p (b c) -> p b c", b=B), AX_X, ALU.max))
            link(dve.tensor_scalar(maskf[0:1, :], maskf[0:1, :], 1.0, BIG, ALU.subtract, ALU.mult))
            for b in range(B):
                dve.tensor_scalar(kbias[0:1, 0, b * C:(b + 1) * C], maskf[0:1, b * C:(b + 1) * C],
                                  anyk[0:1, b:b + 1], None, ALU.mult)
            link(dve.tensor_copy(mask2f, mask2))
            link(dve.tensor_scalar(kbias[0:1, 1, :], mask2f, 0.0, -BIG, ALU.is_equal, ALU.mult))
            link(dve.tensor_scalar(anyk[:, :], anyk[:, :], float(LAYERS[0].scale), None, ALU.mult))
            dve.memset(zero[:, :], 0.0).then_inc(consts, 1)

            def norm_stats(L, src, n, phase):
                for t in range(TT):
                    last = dve.bn_stats(stats[:, t, :], src(t))
                last.then_inc(normed, 1)
                wait_apart(dve, (normed, n(1)))
                for t in range(TT):
                    last = dve.bn_aggr(mv[:, t, :], stats[:, t, :])
                if phase != 2:
                    last.then_inc(var_ready, 1)
                else:
                    last.then_inc(normed, 1)
                    dve.wait_ge(normed, n(2))
                    dve.tensor_tensor(sdev[:, :], mv[:, :, 0], mv[:, :, 0], ALU.mult).then_inc(normed, 1)
                    dve.wait_ge(normed, n(3))
                    dve.tensor_tensor(mv[:, :, 1], mv[:, :, 1], sdev[:, :], ALU.add).then_inc(var_ready, 1)

            def split_lo(dst, src, hi, sem_):
                dve.tensor_tensor(dst, src, hi.bitcast(F32), ALU.subtract).then_inc(sem_, 1)

            def attention(L):
                ub, sb_, ab, hb = (base(L, n) for n in (LAYERS[0].n_use, LAYERS[0].n_step, LAYERS[0].n_act, H))
                nS, per = len(L.steps), len(L.tiles)
                qb, kb, vb = ("q_b", "k_b", "v_b") if L.index == 0 else ("q_b1", "k_b1", "v_b1")
                for s in range(2):
                    dve.memset(QS[ROWMASK:P, s, :, :].bitcast(F32), 1.0)
                    dve.memset(KS[ROWMASK:P, s, :, :].bitcast(F32), 1.0)
                last = dve.memset(VP[:, :, :, 2 * HD:VW].bitcast(F32), 1.0)
                link(last)
                for s in range(2):
                    last = dve.memset(KS[ROWMASK:ROWMASK + 1, s, :, 0:S].bitcast(F32), 0.0)
                last.then_inc(consts, 1)
                N = 3 if L.index == 0 else 1
                with dve.Fori(0, B) as b:
                    if L.index == 0:
                        def n(k):
                            return at(0, b, 3, k)
                        dve.wait_ge(x_loaded, at(0, b, 16, 16))
                        norm_stats(L, lambda t: tok[:, t, :], n, 0)
                        dve.wait_ge(sd_ready, at(0, b, 1, 1))
                        dve.reciprocal(rstd[:, :], sdev[:, :]).then_inc(normed, 1)
                        dve.wait_ge(normed, n(2))
                        for t in range(TT):
                            last = dve.tensor_scalar(tok[:, t, :], tok[:, t, :], mv[:, t, 0:1], rstd[:, t:t + 1],
                                                     ALU.subtract, ALU.mult)
                        last.then_inc(normed, 1)

                    def evac(u):
                        dve.wait_ge(act_out, at(ab, b, L.n_act, L.act[u] + 1))
                        return bank[L.use[u] % 2]

                    for k in range(KT):
                        src = evac(f"T{k}")
                        split_lo(xT[:, 1, k, :], src[:, :], xT[:, 0, k, :], pb_free)
                    src = evac("C")
                    split_lo(cT[:, 1, :, :], src[:, 0:KT * C].rearrange("p (k n) -> p k n", k=KT),
                             cT[:, 0, :, :], pb_free)
                    for t in L.tiles:
                        src = evac(f"V{t}")
                        m = C if t == CT else P
                        split_lo(VP[0:m, t, :, HD:2 * HD], src[0:m, :].rearrange("p (h d) -> p h d", h=H),
                                 VP[0:m, t, :, 0:HD], pb_free)

                    def q_lo(c):
                        src = evac(f"Q{c}")
                        dve.scalar_tensor_tensor(out=qt[:, 1, :], in0=src[:, :], scalar=par(qb, c),
                                                 in1=qt[:, 0, :].bitcast(F32), op0=ALU.add,
                                                 op1=ALU.subtract).then_inc(pb_free, 1)

                    def k_lo(c):
                        for u in ([f"K{c}"] if L.main else []) + [f"KC{c}"]:
                            src = evac(u)
                            o, m = (0, S) if u[:2] != "KC" else (S, C)
                            dve.scalar_tensor_tensor(out=kt[:, 1, o:o + m], in0=src[:, 0:m], scalar=par(kb, c),
                                                     in1=kt[:, 0, o:o + m].bitcast(F32), op0=ALU.add,
                                                     op1=ALU.subtract).then_inc(pb_free, 1)

                    mb, cb = (B * 64 * 0, base(L, H))

                    def max_main(c, m):
                        dve.wait_ge(mm_full, at(0, b, 16 * G, 16 * c + m + 1))
                        dve.tensor_reduce(nm_main[:, m:m + 1], bank[2][:, :], AX_X, ALU.max, negate=True)\
                            .then_inc(mm_free, 1)

                    def max_ctx(c, j):
                        dve.wait_ge(mc_full, at(cb, b, H, HG * c + j + 1))
                        dst = nm_ctx if L.main else nm
                        if not L.main and j == 0:
                            dve.wait_ge(pb_free, at(ub, b, L.n_use, L.use[f"R{c - 1}"] + 1 if c else 0))
                        dve.tensor_reduce(dst[:, 4 * j:4 * j + 4],
                                          bank[3][:, 0:TT * C].rearrange("p (q n) -> p q n", q=TT),
                                          AX_X, ALU.max, negate=True).then_inc(mc_free, 1)

                    def max_join(c):
                        if L.main:
                            dve.wait_ge(mm_free, at(0, b, 16 * G, 16 * (c + 1)))
                            dve.wait_ge(mc_free, at(cb, b, H, HG * (c + 1)))
                            dve.tensor_tensor(nm, nm_main, nm_ctx, ALU.min).then_inc(nm_ready, 1)

                    def max_turned(c):
                        dve.wait_ge(pb_full, at(ub, b, L.n_use, L.use[f"R{c}"] + 1))
                        dve.wait_ge(maxed[c % 2], at(base(L, 32), b, 32, 16 * (c // 2)))
                        dve.tensor_copy(nT[0:16, c % 2, :], bank[L.use[f"R{c}"] % 2][0:16, 0:P]).then_inc(pb_free, 1)

                    def lo_p(c, i):
                        m = c * nS + i
                        rows = C if L.steps[i][1] == CT else P
                        dve.wait_ge(p_hi, at(sb_, b, L.n_step, m + 1))
                        split_lo(pl[0:rows, m % PRING, :], pf[0:rows, m % PRING, :], ph[0:rows, m % PRING, :], p_lo)

                    def o_sum(h):
                        dve.wait_ge(sg_ready, at(hb, b, H, h + 1))
                        dve.tensor_tensor(sg[0:HD, h % 2, :], bank[6 + h % 2][HD:2 * HD, :], sg[0:HD, h % 2, :],
                                          ALU.add).then_inc(o_free, 1)

                    q_lo(0)
                    k_lo(0)
                    q_lo(1)
                    k_lo(1)
                    for j in range(HG):
                        if L.main:
                            for q in range(TT):
                                max_main(0, 4 * j + q)
                        max_ctx(0, j)
                    max_join(0)
                    max_turned(0)
                    for c in range(G):
                        done = 0
                        for i in range(nS):
                            j, t = L.steps[i]
                            if c + 1 < G:
                                if L.main and t < TT:
                                    max_main(c + 1, 4 * j + t)
                                if t == CT:
                                    max_ctx(c + 1, j)
                            lo_p(c, i)
                            if done < HG - 1 and i == (done + 1) * per - 1 + LAG + 1:
                                o_sum(HG * c + done)
                                done += 1
                        if c + 1 < G:
                            max_join(c + 1)
                        for j in range(done, HG - 1):
                            o_sum(HG * c + j)
                        if c + 2 < G:
                            q_lo(c + 2)
                        if c + 1 < G:
                            max_turned(c + 1)
                        if c + 2 < G:
                            k_lo(c + 2)
                        o_sum(HG * c + HG - 1)

                    for s in range(2):
                        dve.wait_ge(o_moved[s], at(base(L, 256), b, 256, 256))
                    dve.reciprocal(r16[0:H, :], s16[0:H, :]).then_inc(r_ready, 1)
                    dve.wait_ge(r_spread, at(base(L, 256), b, 256, 256))
                    for k in range(KT):
                        dve.tensor_tensor(oa[:, k, :], oa[:, k, :], rb[:, k, :], ALU.mult).then_inc(scaled, 1)
                    for k in range(KT):
                        dve.wait_ge(scaled, at(base(L, KT), b, KT, k + 1))
                        dve.tensor_scalar(xT[:, 0, k, :], oa[:, k, :], par(vb, k), None, ALU.add)\
                            .then_inc(att_ready, 1)
                    for k in range(KT):
                        dve.wait_ge(att_ready, at(base(L, 2 * KT), b, 2 * KT, k + 1))
                        dve.scalar_tensor_tensor(out=xT[:, 1, k, :], in0=oa[:, k, :], scalar=par(vb, k),
                                                 in1=xT[:, 0, k, :].bitcast(F32), op0=ALU.add,
                                                 op1=ALU.subtract).then_inc(att_ready, 1)
                    for t in range(TT):
                        dve.wait_ge(pb_full, at(ub, b, L.n_use, L.use[f"O{t}"] + 1))
                        dve.wait_ge(xb_ready, at(base(L, TT), b, TT, t + 1))
                        dve.tensor_tensor(tok[:, t, :], bank[L.use[f"O{t}"] % 2][:, :], tok[:, t, :],
                                          ALU.add).then_inc(pb_free, 1)

            def mlp(L):
                nb = base(L, KT)
                n0 = 3 * B + (3 * B if L.index else 0)
                npb = 3 if L.index == 0 else 5
                with dve.Fori(0, B) as b:
                    def n(k):
                        return at(n0, b, npb, k)
                    dve.wait_ge(nt_loaded, at(base(L, 16), b, 16, 16))
                    norm_stats(L, lambda t: nt[:, t, :], n, 1 + L.index)
                    k0 = 1 if L.index == 0 else 3
                    dve.wait_ge(sd_ready, at(B + B * L.index, b, 1, 1))
                    dve.reciprocal(rstd[:, :], sdev[:, :]).then_inc(normed, 1)
                    dve.wait_ge(normed, n(k0 + 1))
                    for t in range(TT):
                        if L.index == 0:
                            last = dve.tensor_scalar(nt[:, t, :], nt[:, t, :], mv[:, t, 0:1], rstd[:, t:t + 1],
                                                     ALU.subtract, ALU.mult)
                        else:
                            last = dve.tensor_scalar(nt[:, t, :], nt[:, t, :], rstd[:, t:t + 1], None, ALU.mult)
                    last.then_inc(normed, 1)
                    for k in range(KT):
                        dve.wait_ge(y_hi, at(nb, b, KT, k + 1))
                        split_lo(yT[:, 1, k, ds(b * S, S)], bank[k][:, :], yT[:, 0, k, ds(b * S, S)], y_ready)
                    dve.wait_ge(acc_loaded, at(base(L, 16), b, 16, 16))
                    dve.wait_ge(brow_loaded, 16 * (2 * L.index + 2))
                    for t in range(TT):
                        a = acc_[:, ds(b * (TT * D) + t * D, D)]
                        last = dve.tensor_tensor(a, a, brow[:, :], ALU.add)
                    last.then_inc(biased, 1)
                gb = base(L, NGRP * NCH)
                with dve.Fori(0, NGRP // 2) as gg:
                    for s in range(2):
                        with dve.Fori(0, B) as b:
                            it = gg * (2 * B * NCH) + b * NCH
                            for i in range(NCH):
                                m = gb + s * B * NCH + i
                                dve.wait_ge(g_act, it + (m + 1))
                                dve.tensor_copy(gs[:, 0, i, :], gf[:, i % 2, :]).then_inc(g_hi, 1)
                                dve.wait_ge(g_hi, it + (m + 1))
                                split_lo(gs[:, 1, i, :], gf[:, i % 2, :], gs[:, 0, i, :], g_lo)
                            dve.wait_ge(biased, B * (L.index + 1))
                            for t in range(TT):
                                dve.wait_ge(a_full, it + (gb + s * B * NCH + t + 1))
                                a = acc_[:, ds(b * (TT * D) + t * D, D)]
                                dve.tensor_tensor(a, bank[4 + t][:, :], a, ALU.add).then_inc(acc_added, 1)

            for L in LAYERS:
                attention(L)
                mlp(L)

        @block.tensor
        def _(pe):
            HL = ((0, 0), (0, 1), (1, 0))
            LH = ((0, 0), (1, 0), (0, 1))

            pe.wait_ge(par_loaded, 16 * (len(order) + 2))
            pe.wait_ge(ident_ready, 2)
            pe.transpose(bank[0][:, 0:NPAR], par_rows, ident[0:NPAR, 0:NPAR]).then_inc(par_turned, 1)

            def attention(L):
                ub, sb_, hb = (base(L, n) for n in (LAYERS[0].n_use, LAYERS[0].n_step, H))
                nS, per = len(L.steps), len(L.tiles)
                wb = (4 + 2 * NGRP) * L.index
                NU = 4 * KT + 2 * KT * NGRP

                def weights(slot):
                    done = {0: KT, 1: 2 * KT, 2: 3 * KT, 3: 4 * KT}[slot]
                    if L.index and slot == 1:
                        done = 3 * KT
                    pe.wait_ge(w_lo, NU * L.index + done)
                pe.wait_ge(consts, 4 + L.index)
                with pe.Fori(0, B) as b:
                    def free(u):
                        m = L.use[u]
                        pe.wait_ge(pb_free, at(ub, b, L.n_use, m - 1))
                        return bank[m % 2]

                    if L.index == 0:
                        pe.wait_ge(normed, at(0, b, 3, 3))
                    else:
                        pe.wait_ge(x_loaded, at(16 * B, b, 16, 16))
                    for k in range(KT):
                        dst = free(f"T{k}")
                        for t in range(TT):
                            last = pe.transpose(dst[:, t * P:(t + 1) * P], tok[:, t, k * P:(k + 1) * P], ident[:, :])
                        last.then_inc(pb_full, 1)
                    dst = bank[L.use["C"] % 2]
                    wait_apart(pe, (c_loaded, at(base(L, 16), b, 16, 16)),
                               (pb_free, at(ub, b, L.n_use, L.use["C"] - 1)))
                    for k in range(KT):
                        last = pe.transpose(dst[:, k * C:(k + 1) * C], ctok[0:C, k * P:(k + 1) * P], ident[0:C, 0:C])
                    last.then_inc(pb_full, 1)

                    def inputs(u):
                        pe.wait_ge(pb_free, at(ub, b, L.n_use, L.use[u] + 1))

                    weights(2)
                    for t in L.tiles:
                        dst = free(f"V{t}")
                        inputs("C")
                        m = C if t == CT else P
                        last = None
                        for k in range(KT):
                            for a, c in HL:
                                src = cT[:, a, k, :] if t == CT else xT[:, a, k, t * P:(t + 1) * P]
                                last = pe.matmul(dst[0:m, :], src, W[:, 2, c, k, :],
                                                 start=(k == 0 and a == 0 and c == 0),
                                                 stop=(k == KT - 1 and a == 1))
                        last.then_inc(pb_full, 1)

                    def project(u, slot, c, src, m):
                        dst = free(u)
                        for k in range(KT):
                            for a, d in HL:
                                last = pe.matmul(dst[:, 0:m], W[:, slot, a, k, c * P:(c + 1) * P], src[:, d, k, :],
                                                 start=(k == 0 and a == 0 and d == 0),
                                                 stop=(k == KT - 1 and a == 1))
                        last.then_inc(pb_full, 1)

                    def q_proj(c):
                        project(f"Q{c}", 0, c, xT, S)

                    def k_proj(c):
                        if L.main:
                            project(f"K{c}", 1, c, xT, S)
                        project(f"KC{c}", 1, c, cT, C)

                    def stacks(c):
                        pe.wait_ge(stacked[c % 2], at(base(L, 2 * STK), b, 2 * STK, STK * (c // 2 + 1)))

                    def max_main(c, m):
                        j, q = divmod(m, TT)
                        n = 16 * c + m
                        pe.wait_ge(mm_free, at(0, b, 16 * G, n))
                        pe.matmul(bank[2][:, :], QS[0:ROWMAX, c % 2, j, q * P:(q + 1) * P],
                                  KS[0:ROWMAX, c % 2, j, 0:S], start=True, stop=True).then_inc(mm_full, 1)

                    def max_ctx(c, j):
                        pe.wait_ge(mc_free, at(hb, b, H, HG * c + j))
                        for q in range(TT):
                            last = pe.matmul(bank[3][:, q * C:(q + 1) * C], QS[0:ROWMAX, c % 2, j, q * P:(q + 1) * P],
                                             KS[0:ROWMAX, c % 2, j, S:NK], start=True, stop=True)
                        last.then_inc(mc_full, 1)

                    def max_turn(c):
                        if L.main:
                            pe.wait_ge(nm_ready, at(0, b, G, c + 1))
                        else:
                            pe.wait_ge(mc_free, at(hb, b, H, HG * (c + 1)))
                        dst = free(f"R{c}")
                        pe.transpose(dst[0:16, 0:P], nm, ident[:, :]).then_inc(pb_full, 1)

                    def scores(c, i):
                        j, t = L.steps[i]
                        n = c * nS + i
                        if i == 0:
                            pe.wait_ge(maxed[c % 2], at(base(L, 32), b, 32, 16 * (c // 2 + 1)))
                        pe.wait_ge(p_exp, at(sb_, b, L.n_step, n - 1))
                        m = C if t == CT else P
                        pe.matmul(bank[4 + n % 2][0:m, :], KS[0:ROWMAX + 1, c % 2, j, t * P:t * P + m],
                                  QS[0:ROWMAX + 1, c % 2, j, :], start=True, stop=True).then_inc(s_full, 1)

                    def values(c, i):
                        j, t = L.steps[i]
                        n = c * nS + i
                        h = HG * c + j
                        m = C if t == CT else P
                        if t == L.tiles[0]:
                            pe.wait_ge(o_free, at(hb, b, H, h - 1))
                        pe.wait_ge(p_lo, at(sb_, b, L.n_step, n + 1))
                        v = VP[0:m, t, h, 0:2 * HD + 1]
                        o = bank[6 + h % 2][0:2 * HD + 1, :]
                        pe.matmul(o, v, ph[0:m, n % PRING, :], start=(t == L.tiles[0]), stop=False)
                        pe.matmul(o, v, pl[0:m, n % PRING, :], start=False, stop=(t == CT)).then_inc(pv_step, 1)

                    weights(0)
                    q_proj(0)
                    weights(1)
                    k_proj(0)
                    q_proj(1)
                    k_proj(1)
                    stacks(0)
                    for j in range(HG):
                        if L.main:
                            for q in range(TT):
                                max_main(0, TT * j + q)
                        max_ctx(0, j)
                    max_turn(0)
                    for c in range(G):
                        if c + 1 < G:
                            stacks(c + 1)
                        for i in range(nS):
                            j, t = L.steps[i]
                            scores(c, i)
                            if c + 1 < G:
                                if L.main and t < TT:
                                    max_main(c + 1, TT * j + t)
                                if t == CT:
                                    max_ctx(c + 1, j)
                            if i >= LAG:
                                values(c, i - LAG)
                        last_head = max(nS - LAG, nS - per)
                        for i in range(nS - LAG, last_head):
                            values(c, i)
                        if c + 2 < G:
                            q_proj(c + 2)
                        if c + 1 < G:
                            max_turn(c + 1)
                        if c + 2 < G:
                            k_proj(c + 2)
                        for i in range(last_head, nS):
                            values(c, i)
                    weights(3)
                    pe.wait_ge(att_ready, at(base(L, 2 * KT), b, 2 * KT, 2 * KT))
                    for t in range(TT):
                        dst = free(f"O{t}")
                        for k in range(KT):
                            for a, d in HL:
                                last = pe.matmul(dst[:, :], xT[:, a, k, t * P:(t + 1) * P], W[:, 3, d, k, :],
                                                 start=(k == 0 and a == 0 and d == 0),
                                                 stop=(k == KT - 1 and a == 1))
                        last.then_inc(pb_full, 1)

            def mlp(L):
                nb = base(L, KT)
                NU = 4 * KT + 2 * KT * NGRP
                ub = base(L, LAYERS[0].n_use)
                n0 = 3 * B + (3 * B if L.index else 0)
                npb = 3 if L.index == 0 else 5
                with pe.Fori(0, B) as b:
                    pe.wait_ge(normed, at(n0, b, npb, npb))
                    for k in range(KT):
                        pe.wait_ge(y_ready, at(nb, b, KT, 0))
                        for t in range(TT):
                            last = pe.transpose(bank[k][:, t * P:(t + 1) * P], nt[:, t, k * P:(k + 1) * P], ident[:, :])
                        last.then_inc(t_full, 1)
                pe.wait_ge(y_ready, KT * B * (L.index + 1))
                gb = base(L, NGRP * NCH)
                with pe.Fori(0, NGRP // 2) as gg:
                    for s in range(2):
                        wait_apart(pe, (w_lo, gg * (4 * KT) + (NU * L.index + 4 * KT + (s + 1) * 2 * KT)))
                        with pe.Fori(0, B) as b:
                            it = gg * (2 * B * NCH) + b * NCH
                            g0 = gb + s * B * NCH

                            def fc1(i):
                                if i == 0:
                                    wait_apart(pe, (g_act, it + g0))
                                for k in range(KT):
                                    for a, d in HL:
                                        last = pe.matmul(bank[i][:, :], W[:, 2 * s, a, k, i * P:(i + 1) * P],
                                                         yT[:, d, k, ds(b * S, S)],
                                                         start=(k == 0 and a == 0 and d == 0),
                                                         stop=(k == KT - 1 and a == 1))
                                last.then_inc(f_full, 1)

                            def fc2(i):
                                if i == 0:
                                    pe.wait_ge(acc_added, it + g0)
                                pe.wait_ge(g_lo, it + (g0 + i + 1))
                                for t in range(TT):
                                    for a, d in HL:
                                        last = pe.matmul(bank[4 + t][:, :], gs[:, a, i, t * P:(t + 1) * P],
                                                         W[:, 2 * s + 1, d, i, :],
                                                         start=(i == 0 and a == 0 and d == 0),
                                                         stop=(i == NCH - 1 and a == 1))
                                    if i == NCH - 1:
                                        last.then_inc(a_full, 1)

                            fc1(0)
                            fc1(1)
                            fc2(0)
                            fc1(2)
                            fc2(1)
                            fc1(3)
                            fc2(2)
                            fc2(3)

            for L in LAYERS:
                attention(L)
                mlp(L)


_WEIGHTS = {
    "ln1_w": "L0_xattn_ln1_w", "ln1_b": "L0_xattn_ln1_b", "q_w": "L0_xattn_q_w", "q_b": "L0_xattn_q_b",
    "k_w": "L0_xattn_k_w", "k_b": "L0_xattn_k_b", "v_w": "L0_xattn_v_w", "v_b": "L0_xattn_v_b",
    "cproj_w": "L0_xattn_cproj_w", "cproj_b": "L0_xattn_cproj_b", "ln2_w": "L0_xattn_ln2_w",
    "ln2_b": "L0_xattn_ln2_b", "fc_w": "L0_xattn_fc_w", "fc_b": "L0_xattn_fc_b",
    "proj_w": "L0_xattn_proj_w", "proj_b": "L0_xattn_proj_b", "q_w1": "L1_xattn_q_w",
    "q_b1": "L1_xattn_q_b", "kv_w": "L1_xattn_kv_w", "kv_b": "L1_xattn_kv_b", "out_w": "L1_xattn_out_w",
    "out_b": "L1_xattn_out_b", "post_w": "L1_xattn_postnorm_w", "mlp_w1": "L1_xattn_mlp_w1",
    "mlp_b1": "L1_xattn_mlp_b1", "mlp_w2": "L1_xattn_mlp_w2", "mlp_b2": "L1_xattn_mlp_b2",
}


def kernel(**inputs):
    import numpy as np
    import concourse.bacc as bacc
    from concourse.bass_utils import run_bass_kernel_spmd

    nc = bacc.Bacc("TRN2", target_bir_lowering=False, num_devices=1)
    arrays = {}

    def dram_in(name):
        a = np.ascontiguousarray(inputs[name])
        if a.dtype == np.bool_:
            a = a.view(np.uint8)
        arrays[f"in_{name}_dram"] = a
        return nc.dram_tensor(f"in_{name}_dram", a.shape, mybir.dt.from_np(a.dtype), kind="ExternalInput").ap()

    main = [dram_in(n) for n in ("x", "ctx_2048", "mask_BxS2_bf1", "mask_BxS2_ik0")]
    weights = {k: dram_in(v) for k, v in _WEIGHTS.items()}
    between = [nc.dram_tensor(n, (B, S, D), F32, kind="Internal").ap() for n in ("after_att0", "after_layer0", "after_att1")]
    out = nc.dram_tensor("out_0_dram", (B, S, D), F32, kind="ExternalOutput").ap()
    program(nc, *main, weights, *between, out)
    r = run_bass_kernel_spmd(nc, [arrays], core_ids=[0])
    return r.results[0]["out_0_dram"]
```

```python
from contextlib import ExitStack

import concourse.bass as bass
from concourse import mybir

F32 = mybir.dt.float32
F32R = mybir.dt.float32r
U8 = mybir.dt.uint8
I32 = mybir.dt.int32
ACT = mybir.ActivationFunctionType
ALU = mybir.AluOpType
AX_X = mybir.AxisListType.X
ds = bass.ds

P = 128
B, S, D = 4, 512, 512
C = 64
H, HD = 16, 32
INNER = 4 * D
KT = D // P
TT = S // P
HG = P // HD
G = H // HG
NK = S + C
CT = TT
ROWMASK, ROWMAX = 3 * HD, 3 * HD + 1
VW = 2 * HD + 2
BIG = 2.0 ** 126
PRING = 3
LAG = 2
STK = 16 * (6 * HG + 1)
NGRP = INNER // D
NCH = D // P
PAIRS = HG // 2
ONE = 1


class Layer:

    def __init__(self, index):
        self.index = index
        self.tiles = [CT] if index == 0 else list(range(TT + 1))
        self.main = index == 1
        self.scale = HD ** -0.5 if index == 0 else 1.0 / HD
        self.eps = 1e-5 if index == 0 else 1e-6
        v = [f"V{t}" for t in self.tiles]

        def key(c):
            return ([f"K{c}"] if self.main else []) + [f"KC{c}"]
        uses = [f"T{k}" for k in range(KT)] + ["C"] + v
        uses += ["Q0"] + key(0) + ["Q1"] + key(1) + ["R0"]
        for c in range(G):
            uses += [f"Q{c + 2}"] if c + 2 < G else []
            uses += [f"R{c + 1}"] if c + 1 < G else []
            uses += key(c + 2) if c + 2 < G else []
        uses += [f"O{t}" for t in range(TT)]
        self.uses = uses
        by_act = [u for u in uses if u[0] not in "RO"]
        self.use = {u: n for n, u in enumerate(uses)}
        self.act = {u: n for n, u in enumerate(by_act)}
        self.n_use, self.n_act = len(uses), len(by_act)
        self.n_step = H * len(self.tiles)
        self.steps = [(j, t) for j in range(HG) for t in self.tiles]


LAYERS = [Layer(0), Layer(1)]


def at(base, b, per, n):
    return b * per + (base + max(n, 0) + ONE)


def program(nc, x, ctx, mask_bool, mask_int, w, x1, xm, x2, out):
    es = ExitStack()
    with es:
        def sb(name, shape, dt):
            return es.enter_context(nc.sbuf_tensor(name, shape, dt))

        started = []

        def sem(name):
            started.append(es.enter_context(nc.semaphore(name)))
            return started[-1]

        bank = [es.enter_context(nc.psum_tensor(f"bank{i}", [P, 512], F32)) for i in range(8)]

        W = sb("W", [P, 4, 2, KT, D], F32R)
        raw = sb("raw", [P, 2, D], F32)
        ident = sb("ident", [P, P], F32)
        cols = sb("cols", [P, 80], F32)
        brow = sb("brow", [P, D], F32)
        stats = sb("stats", [P, TT, 6], F32)
        mv = sb("mv", [P, TT, 2], F32)
        sdev = sb("sdev", [P, TT], F32)
        rstd = sb("rstd", [P, TT], F32)
        anyk = sb("anyk", [P, B], F32)
        kbias = sb("kbias", [1, 2, B * C], F32R)
        zero = sb("zero", [1, 8], F32)

        NR_ATT = (2 * KT * S + 2 * KT * C + 2 * HG * S + 2 * HG * NK + 5 * H * VW
                  + 2 * PRING * S + 2 * S + 2 * NK + 2 * P)
        NR_MLP = 2 * KT * B * S + 2 * 4 * S
        RA = sb("RA", [P, max(NR_ATT, NR_MLP)], F32R)
        NF_ATT = PRING * S + 2 * S + KT * S + KT * S + D + 2 * S + 4 * 16
        NF_MLP = B * TT * D + TT * D
        FA = sb("FA", [P, max(NF_ATT, NF_MLP)], F32)

        def cut(arena, sizes):
            o, parts = 0, []
            for n in sizes:
                parts.append(arena[:, o:o + n])
                o += n
            return parts

        xT_, cT_, QS_, KS_, VP_, ph_, pl_, qt_, kt_, nT_ = cut(RA, [
            2 * KT * S, 2 * KT * C, 2 * HG * S, 2 * HG * NK, 5 * H * VW,
            PRING * S, PRING * S, 2 * S, 2 * NK, 2 * P])
        xT = xT_.rearrange("p (h k n) -> p h k n", h=2, k=KT)
        cT = cT_.rearrange("p (h k n) -> p h k n", h=2, k=KT)
        QS = QS_.rearrange("p (s j n) -> p s j n", s=2, j=HG)
        KS = KS_.rearrange("p (s j n) -> p s j n", s=2, j=HG)
        VP = VP_.rearrange("p (t h n) -> p t h n", t=5, h=H)
        ph = ph_.rearrange("p (r n) -> p r n", r=PRING)
        pl = pl_.rearrange("p (r n) -> p r n", r=PRING)
        qt = qt_.rearrange("p (h n) -> p h n", h=2)
        kt = kt_.rearrange("p (h n) -> p h n", h=2)
        nT = nT_.rearrange("p (s n) -> p s n", s=2)
        pf_, sg_, oa_, tok_, ct_, sr_, nm_ = cut(FA, [
            PRING * S, 2 * S, KT * S, KT * S, D, 2 * S, 4 * 16])
        pf = pf_.rearrange("p (r n) -> p r n", r=PRING)
        sg = sg_.rearrange("p (r n) -> p r n", r=2)
        oa = oa_.rearrange("p (k n) -> p k n", k=KT)
        tok = tok_.rearrange("p (t n) -> p t n", t=TT)
        rb = tok
        ctok = ct_
        s16, r16 = sr_[:, 0:S], sr_[:, S:2 * S]
        nm_main, nm_ctx, nm = nm_[:, 0:16], nm_[:, 16:32], nm_[:, 32:48]
        xT0_, cT0_, qg_, KB_, VB_, kk_, KM_, first_, PT_, aT_ = cut(RA, [
            2 * KT * S, 2 * KT * P, 2 * 2 * S, 2 * G * HG * C, 2 * G * PAIRS * P, 2 * G * C,
            B * HG * C, P, 2 * PAIRS * 2 * S, 2 * KT * S])
        xT0 = xT0_.rearrange("p (h k n) -> p h k n", h=2, k=KT)
        cT0 = cT0_.rearrange("p (h k n) -> p h k n", h=2, k=KT)
        qg = qg_.rearrange("p (r h n) -> p r h n", r=2, h=2)
        KB = KB_.rearrange("p (h c n) -> p h c n", h=2, c=G)
        VB = VB_.rearrange("p (h c a n) -> p h c a n", h=2, c=G, a=PAIRS)
        kk = kk_.rearrange("p (h n) -> p h n", h=2)
        PT = PT_.rearrange("p (r a h n) -> p r a h n", r=2, a=PAIRS, h=2)
        aT = aT_.rearrange("p (h k n) -> p h k n", h=2, k=KT)
        tok0_, res0_, ex_, pn_, ctok0, kf, HM, mx_, sm_, rc_ = cut(FA, [
            TT * D, TT * D, 2 * S, 4 * S, D, G * C, HG, 16, 16, 16])
        tok0 = tok0_.rearrange("p (t n) -> p t n", t=TT)
        res0 = res0_.rearrange("p (t n) -> p t n", t=TT)
        ex = ex_.rearrange("p (r n) -> p r n", r=2)
        pn = pn_.rearrange("p (r n) -> p r n", r=4)
        mx = mx_.rearrange("p (r n) -> p r n", r=2)
        sm = sm_.rearrange("p (r n) -> p r n", r=2)
        rc = rc_.rearrange("p (r n) -> p r n", r=2)
        yT_, g_ = cut(RA, [2 * KT * B * S, 2 * 4 * S])
        yT = yT_.rearrange("p (h k n) -> p h k n", h=2, k=KT)
        gs = g_.rearrange("p (h r n) -> p h r n", h=2, r=4)
        acc_, nt_ = cut(FA, [B * TT * D, TT * D])
        nt = nt_.rearrange("p (t n) -> p t n", t=TT)
        gf = nt[:, 0:2, :]

        ident_ready = sem("ident_ready")
        par_loaded = sem("par_loaded")
        par_turned = sem("par_turned")
        consts = sem("consts")
        dve_own = sem("dve_own")
        brow_loaded = sem("brow_loaded")
        x_loaded = sem("x_loaded")
        c_loaded = sem("c_loaded")
        var_ready = sem("var_ready")
        sd_ready = sem("sd_ready")
        normed = sem("normed")
        pb_full = sem("pb_full")
        pb_free = sem("pb_free")
        act_out = sem("act_out")
        act_own = sem("act_own")
        stacked = [sem("stacked0"), sem("stacked1")]
        maxed = [sem("maxed0"), sem("maxed1")]
        mm_full = sem("mm_full")
        mm_free = sem("mm_free")
        mc_full = sem("mc_full")
        mc_free = sem("mc_free")
        nm_ready = sem("nm_ready")
        s_full = sem("s_full")
        p_exp = sem("p_exp")
        p_hi = sem("p_hi")
        p_lo = sem("p_lo")
        pv_step = sem("pv_step")
        sg_ready = sem("sg_ready")
        o_free = sem("o_free")
        o_moved = [sem("o_moved0"), sem("o_moved1")]
        r_ready = sem("r_ready")
        r_spread = sem("r_spread")
        scaled = sem("scaled")
        att_ready = sem("att_ready")
        x_again = sem("x_again")
        xb_ready = sem("xb_ready")
        stored = sem("stored")
        raw_loaded = [es.enter_context(nc.semaphore(f"raw_loaded{i}")) for i in range(2)]
        w_hi = sem("w_hi")
        w_lo = sem("w_lo")
        w_ready = sem("w_ready")
        acc_loaded = sem("acc_loaded")
        nt_loaded = sem("nt_loaded")
        t_full = sem("t_full")
        y_hi = sem("y_hi")
        y_ready = sem("y_ready")
        f_full = sem("f_full")
        g_act = sem("g_act")
        g_hi = sem("g_hi")
        g_lo = sem("g_lo")
        a_full = sem("a_full")
        acc_added = sem("acc_added")
        biased = sem("biased")

        order = ["ln1_w", "ln1_b", "q_b", "v_b", "k_b", "ln2_w", "ln2_b", "fc_b",
                 "q_b1", "k_b1", "v_b1", "post_w", "mlp_b1"]
        col, at_row = {}, 0
        for name in order:
            col[name] = at_row
            at_row += (4 * D if name in ("fc_b", "mlp_b1") else D) // P
        NPAR = at_row

        def par(name, k):
            return cols[:, col[name] + k:col[name] + k + 1]

        par_rows = tok0_[0:NPAR, 0:P]
        maskf = pn_[:, 0:B * C]
        maskr = pn_[:, S:S + B * C // 4].bitcast(U8)
        mask2 = pn_[0:1, 2 * S:2 * S + B * C].bitcast(I32)
        mask2f = pn_[0:1, 3 * S:3 * S + B * C]

        def tokens(t):
            return t.rearrange("b (t p) d -> p b t d", p=P)

        src_of = [x, xm]
        mid_of = [x1, x2]
        dst_of = [xm, out]

        tok_loaded = sem("tok_loaded")
        ctx_loaded = sem("ctx_loaded")
        res_loaded = sem("res_loaded")
        res_biased = sem("res_biased")
        tok_normed = sem("tok_normed")
        var0_ready = sem("var0_ready")
        sd0_ready = sem("sd0_ready")
        pb0_full = sem("pb0_full")
        pb0_free = sem("pb0_free")
        y0_affine = sem("y0_affine")
        in_hi = sem("in_hi")
        v_hi = sem("v_hi")
        q_hi_ready = sem("q_hi_ready")
        kh_ready = sem("kh_ready")
        kl_ready = sem("kl_ready")
        k_spread = sem("k_spread")
        s0_full = sem("s0_full")
        s0_max = sem("s0_max")
        s0_less = sem("s0_less")
        s0_exp = sem("s0_exp")
        s0_sum = sem("s0_sum")
        s0_inv = sem("s0_inv")
        prob_ready = sem("prob_ready")
        pt_full = sem("pt_full")
        pt_hi = sem("pt_hi")
        pt_lo = sem("pt_lo")
        o0_full = sem("o0_full")
        o0_hi = sem("o0_hi")
        o0_lo = sem("o0_lo")

        def use0(u, last=False, first=False):
            n = {"Q": 8, "T": 12, "C": 16, "K": 17, "V": 19, "O": 12 if last else 20}[u[0]] + int(u[1:] or 0)
            return n - 12 if first else n

        def base(L, per0):
            return B * per0 if L.index else 0

        passed = sem("passed")

        def wait_apart(eng, *waits):
            for sem_, v in waits:
                eng.wait_ge(sem_, v)
            eng.sem_inc(passed, 1)

        block = es.enter_context(nc.Block())

        @block.sync
        def _(sp):
            for sem_ in started:
                sp.sem_inc(sem_, ONE)
            n = 0
            for name in order:
                rows = (4 * D if name in ("fc_b", "mlp_b1") else D) // P
                if name in ("k_b1", "v_b1"):
                    two = w["kv_b"].rearrange("(c n two) -> two c n", n=P, two=2)
                    with nc.allow_non_contiguous_dma(reason="kv_b interleaves k and v"):
                        sp.dma_start(par_rows[col[name]:col[name] + rows, :],
                                     two[int(name == "v_b1")]).then_inc(par_loaded, 16)
                else:
                    sp.dma_start(par_rows[col[name]:col[name] + rows, :],
                                 w[name].rearrange("(c n) -> c n", n=P)).then_inc(par_loaded, 16)
                n += 1
            sp.dma_start(maskr, mask_bool.rearrange("b c -> (b c)").partition_broadcast(P))\
                .then_inc(par_loaded, 16)
            sp.dma_start(mask2, mask_int.rearrange("(o b) c -> o (b c)", o=1)).then_inc(par_loaded, 16)
            sp.wait_ge(consts, 3 + ONE)

            def attention0():
                src, dst = tokens(x), tokens(x1)

                def inputs(nb):
                    sp.dma_start(tok0, src[:, ds(nb, 1), :, :]).then_inc(tok_loaded, 16)
                    for i in range(2):
                        sp.dma_start(ctok0[i * C:(i + 1) * C, :], ctx[ds(nb, 1), :, :].rearrange("o c d -> (o c) d"))\
                            .then_inc(ctx_loaded, 16)

                def batch(b, last):
                    wait_apart(sp, (stored, at(0, b, 64, 0)))
                    sp.dma_start(res0, src[:, ds(b, 1), :, :]).then_inc(res_loaded, 16)
                    if not last:
                        wait_apart(sp, (pb0_full, at(0, b, 16, use0("C", first=True) + 1)))
                        inputs(b + 1)
                    for t in range(TT):
                        sp.wait_ge(pb0_free, at(0, b, 16, use0(f"O{t}", last) + 1))
                        sp.dma_start(dst[:, ds(b, 1), t:t + 1, :], res0[:, t:t + 1, :]).then_inc(stored, 16)

                sp.dma_start(brow[:, :], w["cproj_b"].partition_broadcast(P)).then_inc(brow_loaded, 16)
                inputs(0)
                with sp.Fori(0, B - 1) as b:
                    batch(b, False)
                batch(B - 1, True)

            def attention(L):
                src, dst = tokens(src_of[L.index]), tokens(mid_of[L.index])
                if L.index:
                    sp.wait_ge(stored, 16 * 4 * B * 2 + ONE)
                sp.dma_start(brow[:, :], w["cproj_b" if L.index == 0 else "out_b"].partition_broadcast(P))\
                    .then_inc(brow_loaded, 16)
                U = L.n_use
                ub = 0
                sb_ = 0
                nS = len(L.steps)
                k0 = 0 if L.main else S
                with sp.Fori(0, B) as b:
                    wait_apart(sp, (stored, at(16 * 4 * B * 2 * L.index, b, 64, 0)))
                    sp.dma_start(tok, src[:, ds(b, 1), :, :]).then_inc(x_loaded, 16)
                    sp.dma_start(ctok[0:C, :], ctx[ds(b, 1), :, :].rearrange("o c d -> (o c) d"))\
                        .then_inc(c_loaded, 16)

                    def q_stack(c):
                        wait_apart(sp, (pb_free, at(ub, b, U, L.use[f"Q{c}"] + 1)))
                        if c >= 2:
                            wait_apart(sp, (s_full, at(sb_, b, L.n_step, (c - 1) * nS)))
                        for r, half in ((0, 0), (HD, 0), (2 * HD, 1)):
                            for j in range(HG):
                                sp.dma_start(QS[r:r + HD, c % 2, j, :].bitcast(F32), qt[HD * j:HD * j + HD, half, :].bitcast(F32))\
                                    .then_inc(stacked[c % 2], 16)

                    def k_stack(c):
                        sp.wait_ge(pb_free, at(ub, b, U, L.use[f"KC{c}"] + 1))
                        for r, half in ((0, 0), (HD, 1), (2 * HD, 0)):
                            for j in range(HG):
                                sp.dma_start(KS[r:r + HD, c % 2, j, k0:].bitcast(F32), kt[HD * j:HD * j + HD, half, k0:].bitcast(F32))\
                                    .then_inc(stacked[c % 2], 16)
                        sp.dma_start(KS[ROWMASK:ROWMASK + 1, c % 2, :, S:NK].bitcast(F32),
                                     kbias[0:1, L.index, ds(b * C, C)].bitcast(F32).unsqueeze(1).to_broadcast([1, HG, C]))\
                            .then_inc(stacked[c % 2], 16)

                    def max_row(c):
                        sp.wait_ge(pb_free, at(ub, b, U, L.use[f"R{c}"] + 1))
                        sp.dma_start(QS[ROWMAX:ROWMAX + 1, c % 2, :, :].rearrange("o j (q n) -> o (j q) n", n=P).bitcast(F32),
                                     nT[0:16, c % 2, :].bitcast(F32)).then_inc(maxed[c % 2], 16)

                    def o_move(c, j):
                        h = HG * c + j
                        hb = 0
                        sp.wait_ge(o_free, at(hb, b, H, h + 1))
                        sp.dma_start(oa[HD * j:HD * j + HD, c, :], sg[0:HD, h % 2, :])\
                            .then_inc(o_moved[h % 2], 16)
                        sp.dma_start(s16[4 * j + c:4 * j + c + 1, :], sg[2 * HD:2 * HD + 1, h % 2, :])\
                            .then_inc(o_moved[h % 2], 16)

                    q_stack(0)
                    k_stack(0)
                    q_stack(1)
                    k_stack(1)
                    max_row(0)
                    for c in range(G):
                        for j in range(HG - 1):
                            o_move(c, j)
                        if c + 2 < G:
                            q_stack(c + 2)
                        if c + 1 < G:
                            max_row(c + 1)
                        if c + 2 < G:
                            k_stack(c + 2)
                        o_move(c, HG - 1)
                    sp.wait_ge(r_ready, at(0, b, 1, 1))
                    for j in range(HG):
                        for c in range(G):
                            row = r16[4 * j + c:4 * j + c + 1, :]
                            sp.dma_start(rb[HD * j:HD * j + HD, c, :],
                                         row.unsqueeze(1).to_broadcast([1, HD, S])).then_inc(r_spread, 16)
                    wait_apart(sp, (scaled, at(0, b, KT, KT)))
                    sp.dma_start(tok, src[:, ds(b, 1), :, :]).then_inc(x_again, 16)
                    for t in range(TT):
                        sp.wait_ge(pb_free, at(ub, b, U, L.use[f"O{t}"] + 1))
                        sp.dma_start(dst[:, ds(b, 1), t:t + 1, :], tok[:, t:t + 1, :]).then_inc(stored, 16)

            def mlp(L):
                st = 16 * 4 * B * (2 * L.index + 1)
                sp.wait_ge(stored, st + ONE)
                sp.dma_start(brow[:, :], w["proj_b" if L.index == 0 else "mlp_b2"].partition_broadcast(P))\
                    .then_inc(brow_loaded, 16)
                res = tokens(x1 if L.index == 0 else xm)
                mid, dst = tokens(mid_of[L.index]), tokens(dst_of[L.index])
                with sp.Fori(0, B) as b:
                    sp.dma_start(acc_[:, ds(b * TT * D, TT * D)].rearrange("p (t d) -> p t d", d=D),
                                 res[:, ds(b, 1), :, :]).then_inc(acc_loaded, 16)
                    wait_apart(sp, (t_full, at(base(L, KT), b, KT, 0)))
                    sp.dma_start(nt, mid[:, ds(b, 1), :, :]).then_inc(nt_loaded, 16)
                with sp.Fori(0, B) as b:
                    sp.wait_ge(acc_added, at(base(L, NGRP * TT) + (NGRP - 1) * B * TT, b, TT, TT))
                    sp.dma_start(dst[:, ds(b, 1), :, :],
                                 acc_[:, ds(b * TT * D, TT * D)].rearrange("p (t d) -> p t d", d=D))\
                        .then_inc(stored, 64)

            attention0()
            mlp(LAYERS[0])
            attention(LAYERS[1])
            mlp(LAYERS[1])
            sp.wait_ge(stored, 16 * 4 * B * 4 + ONE)

        @block.gpsimd
        def _(pool):
            pool.memset(ident[:], 0.0).then_inc(ident_ready, 1)
            pool.wait_ge(ident_ready, 1 + ONE)
            pool.affine_select(out=ident[:], in_=ident[:], compare_op=ALU.not_equal, fill=1.0,
                               base=0, pattern=[[-1, P]], channel_multiplier=1).then_inc(ident_ready, 1)

            def split(dsts, srcs, u, before, done):
                pool.wait_ge(raw_loaded[u % 2], 16 * ((before + u) // 2) + 16)
                for (hi, _), s in zip(dsts, srcs):
                    last = pool.tensor_scalar(hi, s, 1.0, 0.0, ALU.mult, ALU.add)
                last.then_inc(w_hi, 1)
                pool.wait_ge(w_hi, before + u + 1 + ONE)
                for (hi, lo), s in zip(dsts, srcs):
                    last = pool.tensor_tensor(lo, s, hi.bitcast(F32), ALU.subtract)
                last.then_inc(w_lo, 1)

            def units(srcs, before, put):
                for u, s in enumerate(srcs):
                    if u == 0:
                        pool.wait_ge(w_lo, before + ONE)
                        pool.dma_start(raw[:, 0, :], s).then_inc(raw_loaded[0], 16)
                    if u + 1 < len(srcs):
                        if before + u:
                            pool.wait_ge(w_lo, before + u + ONE)
                        pool.dma_start(raw[:, (u + 1) % 2, :], srcs[u + 1]).then_inc(raw_loaded[(u + 1) % 2], 16)
                    put(u)

            def rows(m, k, c0=0):
                return m[k * P:(k + 1) * P, c0:c0 + D]

            NU = 4 * KT + 2 * KT * NGRP

            def attention_weights(L):
                before = NU * L.index
                if L.index == 0:
                    for s, name in enumerate(("q_w", "k_w", "v_w", "cproj_w")):
                        def put(u, s=s):
                            split([(W[:, s, 0, u, :], W[:, s, 1, u, :])], [raw[:, u % 2, :]], u,
                                  before + s * KT, u == KT - 1)
                        units([rows(w[name], k) for k in range(KT)], before + s * KT, put)
                    return
                its = NGRP * B * TT
                pool.wait_ge(a_full, its - B * TT + ONE)
                def put_q(u):
                    split([(W[:, 0, 0, u, :], W[:, 0, 1, u, :])], [raw[:, u % 2, :]], u, before, False)
                units([rows(w["q_w1"], k) for k in range(KT)], before, put_q)
                pool.wait_ge(a_full, its + ONE)
                def put_kv(u):
                    k, half = u // 2, u % 2
                    pair = raw[:, u % 2, :].rearrange("p (n two) -> p two n", two=2)
                    c0 = half * (D // 2)
                    split([(W[:, 1 + i, 0, k, c0:c0 + D // 2], W[:, 1 + i, 1, k, c0:c0 + D // 2]) for i in (0, 1)],
                          [pair[:, i, :] for i in (0, 1)], u, before + KT, False)
                units([rows(w["kv_w"], u // 2, (u % 2) * D) for u in range(2 * KT)], before + KT, put_kv)
                def put_o(u):
                    split([(W[:, 3, 0, u, :], W[:, 3, 1, u, :])], [raw[:, u % 2, :]], u, before + 3 * KT, False)
                units([rows(w["out_w"], k) for k in range(KT)], before + 3 * KT, put_o)

            def mlp_weights(L):
                before = NU * L.index + 4 * KT
                w1 = w["fc_w" if L.index == 0 else "mlp_w1"]
                w2 = w["proj_w" if L.index == 0 else "mlp_w2"]
                for g in range(NGRP):
                    slot = 2 * (g % 2)
                    if g == 0 and L.index == 0:
                        pool.wait_ge(pb0_full, at(0, B - 1, 16, use0("Q3") + 1))
                    elif g == 0:
                        pool.wait_ge(pb_full, at(0, B - 1, L.n_use, L.use["KC3"] + 1))
                    elif g == 1 and L.index == 0:
                        pool.wait_ge(pb0_full, at(0, B - 1, 16, use0("O3", last=True) + 1))
                    elif g == 1:
                        pool.wait_ge(pb_full, at(0, B, L.n_use, 0))
                    else:
                        pool.wait_ge(a_full, base(L, NGRP * TT) + (g - 1) * B * TT + ONE)
                    def put(u, slot=slot, g=g):
                        s, k = slot + u // KT, u % KT
                        split([(W[:, s, 0, k, :], W[:, s, 1, k, :])], [raw[:, u % 2, :]], u,
                              before + g * 2 * KT, False)
                    units([rows(w1, k, g * D) for k in range(KT)]
                          + [rows(w2, g * KT + k) for k in range(KT)], before + g * 2 * KT, put)

            def attention0():
                def spread(nb, b):
                    pool.wait_ge(kl_ready, at(0, nb, 1, 1))
                    if b is not None:
                        pool.wait_ge(s0_full, at(0, b, 2 * G, 2 * G))
                    for h in range(2):
                        for c in range(G):
                            last = pool.tensor_tensor(
                                KB[:, h, c, :].rearrange("p (j n) -> p j n", j=HG),
                                kk[:, h, c * C:(c + 1) * C].bitcast(F32).unsqueeze(1).to_broadcast([P, HG, C]),
                                HM.unsqueeze(2).to_broadcast([P, HG, C]), ALU.mult)
                        last.then_inc(k_spread, 1)

                def batch(b, last):
                    def probs(c):
                        for u in (2 * c, 2 * c + 1):
                            pool.wait_ge(s0_inv, at(0, b, 2 * G, u + 1))
                            wait_apart(pool, (pt_full, at(0, b, 2 * G, 2 * c - 2)))
                            pool.tensor_tensor(pn[:, u % 4, :].rearrange("p (m n) -> p m n", m=8),
                                               ex[:, u % 2, :].rearrange("p (m n) -> p m n", m=8),
                                               rc[:, u % 2, :].unsqueeze(2).to_broadcast([P, 8, C]),
                                               ALU.mult).then_inc(prob_ready, 1)
                    probs(0)
                    probs(1)
                    probs(2)
                    pool.wait_ge(res_loaded, at(0, b, 16, 16))
                    for t in range(TT):
                        pool.tensor_tensor(res0[:, t, :], res0[:, t, :], brow[:, :], ALU.add).then_inc(res_biased, 1)
                    probs(3)
                    if not last:
                        spread(b + 1, b)

                pool.wait_ge(brow_loaded, 16 + ONE)
                pool.wait_ge(consts, 4 + ONE)
                spread(0, None)
                with pool.Fori(0, B - 1) as b:
                    batch(b, False)
                batch(B - 1, True)

            def attention(L):
                pb = 0
                with pool.Fori(0, B) as b:
                    for i in range(L.n_step):
                        n = C if L.tiles[i % len(L.tiles)] == CT else P
                        wait_apart(pool, (p_exp, at(pb, b, L.n_step, i + 1)), (pv_step, at(pb, b, L.n_step, i - PRING + 1)))
                        pool.tensor_scalar(ph[0:n, i % PRING, :], pf[0:n, i % PRING, :], 1.0, 0.0,
                                           ALU.mult, ALU.add).then_inc(p_hi, 1)
                    pool.wait_ge(x_again, at(0, b, 16, 16))
                    pool.wait_ge(brow_loaded, 16 * (2 * L.index + 1) + ONE)
                    for t in range(TT):
                        pool.tensor_tensor(tok[:, t, :], tok[:, t, :], brow[:, :], ALU.add).then_inc(xb_ready, 1)

            attention_weights(LAYERS[0])
            attention0()
            mlp_weights(LAYERS[0])
            attention_weights(LAYERS[1])
            attention(LAYERS[1])
            mlp_weights(LAYERS[1])

        @block.scalar
        def _(act):
            def attention0():
                def sqrt(nb):
                    act.wait_ge(var0_ready, at(0, nb, 1, 1))
                    act.activation(sdev[:, :], mv[:, :, 1], ACT.Sqrt, bias=cols[:, NPAR:NPAR + 1])\
                        .then_inc(sd0_ready, 1)

                def full(b, u, first=False, last=False):
                    n = use0(u, first=first, last=last)
                    act.wait_ge(pb0_full, at(0, b, 16, n + 1))
                    return bank[n % 2]

                def front(nb, b, first):
                    for k in range(KT):
                        src = full(b, f"T{k}", first)
                        act.activation(src[:, :], src[:, :], ACT.Identity, bias=par("ln1_b", k),
                                       scale=par("ln1_w", k)).then_inc(y0_affine, 1)
                        act.wait_ge(y0_affine, at(0, nb, KT, k + 1))
                        act.activation(xT0[:, 0, k, :], src[:, :], ACT.Copy).then_inc(in_hi, 1)
                    src = full(b, "C", first)
                    act.activation(cT0[:, 0, :, :], src[:, :].rearrange("p (k n) -> p k n", k=KT),
                                   ACT.Copy).then_inc(in_hi, 1)
                    act.wait_ge(pb0_free, at(0, b, 16, use0("K1", first=first) + 1))
                    act.wait_ge(k_spread, at(0, nb, 2, 0))
                    act.activation(kk[:, 0, :], kf, ACT.Copy).then_inc(kh_ready, 1)

                def values(b, first):
                    src = full(b, "V", first)
                    if not first:
                        act.wait_ge(o0_full, at(0, b, G, G))
                    for i in range(2):
                        for a in range(PAIRS):
                            rows, o = slice(i * C, (i + 1) * C), (2 * a + i) * HD
                            last = act.activation(
                                VB[rows, 0, :, a, o:o + HD],
                                src[rows, :].rearrange("p (c n) -> p c n", c=G)[:, :, o:o + HD], ACT.Copy)
                    last.then_inc(v_hi, 1)

                def batch(b, last):
                    def q_hi(c):
                        src = full(b, f"Q{c}")
                        act.wait_ge(s0_full, at(0, b, 2 * G, 2 * c - 2))
                        act.activation(qg[:, c % 2, 0, :], src[:, :], ACT.Identity, bias=par("q_b", c))\
                            .then_inc(q_hi_ready, 1)

                    def exp(c):
                        for u in (2 * c, 2 * c + 1):
                            wait_apart(act, (s0_less, at(0, b, 2 * G, u + 1)))
                            act.activation(ex[:, u % 2, :], ex[:, u % 2, :], ACT.Exp, scale=anyk[:, ds(b, 1)])\
                                .then_inc(s0_exp, 1)

                    def p_hi_(c):
                        act.wait_ge(o0_full, at(0, b, G, c - 1))
                        for a in range(PAIRS):
                            act.wait_ge(pt_full, at(0, b, 2 * G, 2 * c + a + 1))
                            act.activation(PT[:, c % 2, a, 0, :], bank[4 + a][:, :], ACT.Copy).then_inc(pt_hi, 1)

                    def o_hi_(c):
                        act.wait_ge(o0_full, at(0, b, G, c + 1))
                        act.wait_ge(pb0_full, at(0, b, 16, 8))
                        act.activation(aT[:, 0, c, :], bank[6 + c % 2][:, :], ACT.Identity, bias=par("v_b", c))\
                            .then_inc(o0_hi, 1)

                    q_hi(0)
                    q_hi(1)
                    exp(0)
                    for c in range(G):
                        if c + 2 < G:
                            q_hi(c + 2)
                        if c + 1 < G:
                            exp(c + 1)
                        if c == G - 2 and not last:
                            sqrt(b + 1)
                        if c == G - 1 and not last:
                            front(b + 1, b, False)
                        p_hi_(c)
                        if c:
                            o_hi_(c - 1)
                    o_hi_(G - 1)
                    if not last:
                        values(b, False)

                sqrt(0)
                front(0, 0, True)
                act.wait_ge(consts, 4 + ONE)
                values(0, True)
                with act.Fori(0, B - 1) as b:
                    batch(b, False)
                batch(B - 1, True)

            def attention(L):
                ub, sb_, ab, hb = (0 for n in (LAYERS[0].n_use, LAYERS[0].n_step, LAYERS[0].n_act, H))
                nS = len(L.steps)
                qb, kb = ("q_b", "k_b") if L.index == 0 else ("q_b1", "k_b1")
                with act.Fori(0, B) as b:
                    def full(u):
                        act.wait_ge(pb_full, at(ub, b, L.n_use, L.use[u] + 1))
                        return bank[L.use[u] % 2]

                    if L.index == 0:
                        act.wait_ge(var_ready, at(0, b, 1, 1))
                        act.activation(sdev[:, :], mv[:, :, 1], ACT.Sqrt, bias=cols[:, NPAR:NPAR + 1])\
                            .then_inc(sd_ready, 1)
                    for k in range(KT):
                        src = full(f"T{k}")
                        if L.index == 0:
                            act.activation(src[:, :], src[:, :], ACT.Identity, bias=par("ln1_b", k),
                                           scale=par("ln1_w", k)).then_inc(act_own, 1)
                            act.wait_ge(act_own, at(0, b, KT, k + 1))
                        act.activation(xT[:, 0, k, :], src[:, :], ACT.Copy).then_inc(act_out, 1)
                    src = full("C")
                    act.activation(cT[:, 0, :, :], src[:, 0:KT * C].rearrange("p (k n) -> p k n", k=KT),
                                   ACT.Copy).then_inc(act_out, 1)
                    for t in L.tiles:
                        src = full(f"V{t}")
                        n = C if t == CT else P
                        act.activation(VP[0:n, t, :, 0:HD], src[0:n, :].rearrange("p (h d) -> p h d", h=H),
                                       ACT.Copy).then_inc(act_out, 1)

                    def q_hi(c):
                        src = full(f"Q{c}")
                        if c:
                            act.wait_ge(stacked[(c - 1) % 2], at(0, b, 2 * STK, STK * ((c - 1) // 2 + 1)))
                        act.activation(qt[:, 0, :], src[:, :], ACT.Identity, bias=par(qb, c)).then_inc(act_out, 1)

                    def k_hi(c):
                        for u in ([f"K{c}"] if L.main else []) + [f"KC{c}"]:
                            src = full(u)
                            o, n = (0, S) if u[:2] != "KC" else (S, C)
                            act.activation(kt[:, 0, o:o + n], src[:, 0:n], ACT.Identity, bias=par(kb, c))\
                                .then_inc(act_out, 1)

                    def exp(c, i):
                        n = c * nS + i
                        rows = C if L.steps[i][1] == CT else P
                        wait_apart(act, (s_full, at(sb_, b, L.n_step, n + 1)), (p_lo, at(sb_, b, L.n_step, n - PRING + 1)))
                        act.activation(pf[0:rows, n % PRING, :], bank[4 + n % 2][0:rows, :], ACT.Exp,
                                       scale=L.scale if L.index else anyk[0:rows, ds(b, 1)]).then_inc(p_exp, 1)

                    def o_out(h):
                        act.wait_ge(pv_step, at(sb_, b, L.n_step, (h + 1) * len(L.tiles)))
                        act.wait_ge(o_moved[h % 2], at(0, b, 256, 32 * (h // 2)))
                        act.activation(sg[0:2 * HD + 1, h % 2, :], bank[6 + h % 2][0:2 * HD + 1, :], ACT.Copy)\
                            .then_inc(sg_ready, 1)

                    q_hi(0)
                    k_hi(0)
                    q_hi(1)
                    k_hi(1)
                    per = len(L.tiles)
                    for c in range(G):
                        done = 0
                        for i in range(nS):
                            exp(c, i)
                            if done < HG - 1 and i == (done + 1) * per - 1 + LAG + 1:
                                o_out(HG * c + done)
                                done += 1
                        if per == 1:
                            for j in range(done, HG - 1):
                                o_out(HG * c + j)
                        elif done < HG - 1:
                            raise AssertionError
                        if c + 2 < G:
                            q_hi(c + 2)
                            k_hi(c + 2)
                        o_out(HG * c + HG - 1)

            def mlp(L):
                nb = base(L, KT)
                gb = base(L, NGRP * NCH)
                with act.Fori(0, B) as b:
                    act.wait_ge(var_ready, at(B * L.index, b, 1, 1))
                    act.activation(sdev[:, :], mv[:, :, 1], ACT.Sqrt,
                                   bias=cols[:, NPAR + L.index:NPAR + L.index + 1]).then_inc(sd_ready, 1)
                    for k in range(KT):
                        act.wait_ge(t_full, at(nb, b, KT, k + 1))
                        src = bank[k]
                        if L.index == 0:
                            act.activation(src[:, :], src[:, :], ACT.Identity, bias=par("ln2_b", k),
                                           scale=par("ln2_w", k)).then_inc(act_own, 1)
                            wait_apart(act, (act_own, at(0, b, KT, k + 1)))
                        else:
                            act.activation(src[:, :], src[:, :], ACT.Copy, scale=par("post_w", k))\
                                .then_inc(act_own, 1)
                            wait_apart(act, (act_own, at(KT * B, b, KT, k + 1)))
                        act.activation(yT[:, 0, k, ds(b * S, S)], src[:, :], ACT.Copy).then_inc(y_hi, 1)
                b1 = col["fc_b" if L.index == 0 else "mlp_b1"]
                with act.Fori(0, NGRP // 2) as gg:
                    for s in range(2):
                        with act.Fori(0, B) as b:
                            it = gg * (2 * B * NCH) + b * NCH
                            for i in range(NCH):
                                n = gb + s * B * NCH + i
                                wait_apart(act, (f_full, it + (n + 1 + ONE)), (g_lo, it + (n - min(i, 1) + ONE)))
                                act.activation(gf[:, i % 2, :], bank[i][:, :], ACT.Gelu_apprx_tanh,
                                               bias=cols[:, ds(gg * (2 * NCH) + (b1 + s * NCH + i), 1)])\
                                    .then_inc(g_act, 1)

            act.wait_ge(consts, 3 + ONE)
            attention0()
            mlp(LAYERS[0])
            attention(LAYERS[1])
            mlp(LAYERS[1])

        @block.vector
        def _(dve):
            own = [0]

            def link(ins):
                own[0] += 1
                ins.then_inc(dve_own, 1)
                dve.wait_ge(dve_own, own[0] + ONE)

            dve.memset(cols[:, NPAR:NPAR + 1], 1e-5).then_inc(consts, 1)
            dve.memset(cols[:, NPAR + 1:NPAR + 2], 1e-6).then_inc(consts, 1)
            dve.wait_ge(par_turned, 1 + ONE)
            link(dve.tensor_copy(cols[:, 0:NPAR], bank[0][:, 0:NPAR]))
            link(dve.tensor_copy(maskf, maskr))
            link(dve.tensor_reduce(anyk[:, :], maskf.rearrange("p (b c) -> p b c", b=B), AX_X, ALU.max))
            link(dve.tensor_scalar(maskf[0:1, :], maskf[0:1, :], 1.0, BIG, ALU.subtract, ALU.mult))
            for b in range(B):
                dve.tensor_scalar(kbias[0:1, 0, b * C:(b + 1) * C], maskf[0:1, b * C:(b + 1) * C],
                                  anyk[0:1, b:b + 1], None, ALU.mult)
            link(dve.tensor_copy(mask2f, mask2))
            link(dve.tensor_scalar(kbias[0:1, 1, :], mask2f, 0.0, -BIG, ALU.is_equal, ALU.mult))
            link(dve.tensor_scalar(anyk[:, :], anyk[:, :], float(LAYERS[0].scale), None, ALU.mult))
            dve.memset(zero[:, :], 0.0).then_inc(consts, 1)

            def attention0():
                link(dve.memset(VB_[:, :].bitcast(F32), 0.0))
                dve.memset(KM_[:, :].bitcast(F32), 0.0)
                dve.memset(first_[:, :].bitcast(F32), 0.0)
                link(dve.memset(HM, 0.0))
                for j in range(HG):
                    dve.memset(HM[j * HD:(j + 1) * HD, j:j + 1], 1.0)
                dve.memset(first_[0:1, :].bitcast(F32), 1.0)
                dve.tensor_copy(KM_[0:1, :].rearrange("p (b j n) -> p b j n", b=B, j=HG),
                                kbias[0:1, 0, :].bitcast(F32).rearrange("p (b n) -> p b n", b=B)
                                .unsqueeze(2).to_broadcast([1, B, HG, C])).then_inc(consts, 1)

                def norm(nb):
                    dve.wait_ge(tok_loaded, at(0, nb, 16, 16))
                    for t in range(TT):
                        last = dve.bn_stats(stats[:, t, :], tok0[:, t, :])
                    last.then_inc(tok_normed, 1)
                    wait_apart(dve, (tok_normed, at(0, nb, 3, 1)))
                    for t in range(TT):
                        last = dve.bn_aggr(mv[:, t, :], stats[:, t, :])
                    last.then_inc(var0_ready, 1)
                    dve.wait_ge(sd0_ready, at(0, nb, 1, 1))
                    dve.reciprocal(rstd[:, :], sdev[:, :]).then_inc(tok_normed, 1)
                    dve.wait_ge(tok_normed, at(0, nb, 3, 2))
                    for t in range(TT):
                        last = dve.tensor_scalar(tok0[:, t, :], tok0[:, t, :], mv[:, t, 0:1], rstd[:, t:t + 1],
                                                 ALU.subtract, ALU.mult)
                    last.then_inc(tok_normed, 1)

                def front(nb, b, first):
                    for k in range(KT):
                        dve.wait_ge(in_hi, at(0, nb, KT + 1, k + 1))
                        split_lo(xT0[:, 1, k, :], bank[k % 2][:, :], xT0[:, 0, k, :], pb0_free)
                    dve.wait_ge(in_hi, at(0, nb, KT + 1, KT + 1))
                    split_lo(cT0[:, 1, :, :], bank[use0("C") % 2][:, :].rearrange("p (k n) -> p k n", k=KT),
                             cT0[:, 0, :, :], pb0_free)
                    for i in range(2):
                        n = use0(f"K{i}", first=first)
                        dve.wait_ge(pb0_full, at(0, b, 16, n + 1))
                        dve.wait_ge(kl_ready, at(0, nb, 1, 0))
                        half = kf[:, i * 2 * C:(i + 1) * 2 * C].rearrange("p (c n) -> p c n", c=2)
                        kb = cols[:, col["k_b"] + 2 * i:col["k_b"] + 2 * i + 2]
                        dve.tensor_tensor(half, bank[n % 2][:, 0:2 * C].rearrange("p (c n) -> p c n", c=2),
                                          kb.unsqueeze(2).to_broadcast([P, 2, C]), ALU.add).then_inc(pb0_free, 1)

                def keys_lo(nb):
                    dve.wait_ge(kh_ready, at(0, nb, 1, 1))
                    split_lo(kk[:, 1, :], kf, kk[:, 0, :], kl_ready)

                def values(nb, b, first):
                    src = bank[use0("V") % 2]
                    dve.wait_ge(v_hi, at(0, nb, 1, 1))
                    for i in range(2):
                        for a in range(PAIRS):
                            rows, o = slice(i * C, (i + 1) * C), (2 * a + i) * HD
                            last = dve.tensor_tensor(
                                VB[rows, 1, :, a, o:o + HD],
                                src[rows, :].rearrange("p (c n) -> p c n", c=G)[:, :, o:o + HD],
                                VB[rows, 0, :, a, o:o + HD].bitcast(F32), ALU.subtract)
                    last.then_inc(pb0_free, 1)

                def batch(b, last):
                    def q_lo(c):
                        dve.wait_ge(q_hi_ready, at(0, b, G, c + 1))
                        dve.scalar_tensor_tensor(out=qg[:, c % 2, 1, :], in0=bank[c % 2][:, :],
                                                 scalar=par("q_b", c), in1=qg[:, c % 2, 0, :].bitcast(F32),
                                                 op0=ALU.add, op1=ALU.subtract).then_inc(pb0_free, 1)

                    def less_max(c):
                        for u in (2 * c, 2 * c + 1):
                            s_ = bank[2 + u % 2][:, :].rearrange("p (m n) -> p m n", m=8)
                            dve.wait_ge(s0_full, at(0, b, 2 * G, u + 1))
                            dve.tensor_reduce(mx[:, u % 2, :], s_, AX_X, ALU.max).then_inc(s0_max, 1)
                            dve.wait_ge(s0_max, at(0, b, 2 * G, u + 1))
                            dve.wait_ge(prob_ready, at(0, b, 2 * G, u - 1))
                            dve.tensor_tensor(ex[:, u % 2, :].rearrange("p (m n) -> p m n", m=8), s_,
                                              mx[:, u % 2, :].unsqueeze(2).to_broadcast([P, 8, C]),
                                              ALU.subtract).then_inc(s0_less, 1)

                    def inv_sum(c):
                        for u in (2 * c, 2 * c + 1):
                            dve.wait_ge(s0_exp, at(0, b, 2 * G, u + 1))
                            dve.tensor_reduce(sm[:, u % 2, :], ex[:, u % 2, :].rearrange("p (m n) -> p m n", m=8),
                                              AX_X, ALU.add).then_inc(s0_sum, 1)
                            dve.wait_ge(s0_sum, at(0, b, 2 * G, u + 1))
                            dve.reciprocal(rc[:, u % 2, :], sm[:, u % 2, :]).then_inc(s0_inv, 1)

                    def p_lo_(c):
                        for a in range(PAIRS):
                            dve.wait_ge(pt_hi, at(0, b, 2 * G, 2 * c + a + 1))
                            split_lo(PT[:, c % 2, a, 1, :], bank[4 + a][:, :], PT[:, c % 2, a, 0, :], pt_lo)

                    def o_lo_(c):
                        dve.wait_ge(o0_hi, at(0, b, G, c + 1))
                        dve.scalar_tensor_tensor(out=aT[:, 1, c, :], in0=bank[6 + c % 2][:, :],
                                                 scalar=par("v_b", c), in1=aT[:, 0, c, :].bitcast(F32),
                                                 op0=ALU.add, op1=ALU.subtract).then_inc(o0_lo, 1)

                    q_lo(0)
                    q_lo(1)
                    less_max(0)
                    inv_sum(0)
                    for c in range(G):
                        if c + 2 < G:
                            q_lo(c + 2)
                        if c + 1 < G:
                            less_max(c + 1)
                        if c == G - 2 and not last:
                            norm(b + 1)
                        if c + 1 < G:
                            inv_sum(c + 1)
                        if c == G - 1 and not last:
                            front(b + 1, b, False)
                        p_lo_(c)
                        if c == G - 1 and not last:
                            keys_lo(b + 1)
                        if c:
                            o_lo_(c - 1)
                    o_lo_(G - 1)
                    if not last:
                        values(b + 1, b, False)
                    for t in range(TT):
                        n = use0(f"O{t}", last)
                        dve.wait_ge(pb0_full, at(0, b, 16, n + 1))
                        dve.wait_ge(res_biased, at(0, b, TT, t + 1))
                        dve.tensor_tensor(res0[:, t, :], bank[n % 2][:, :], res0[:, t, :], ALU.add)\
                            .then_inc(pb0_free, 1)

                norm(0)
                front(0, 0, True)
                keys_lo(0)
                values(0, 0, True)
                with dve.Fori(0, B - 1) as b:
                    batch(b, False)
                batch(B - 1, True)

            def norm_stats(L, src, n, phase):
                for t in range(TT):
                    last = dve.bn_stats(stats[:, t, :], src(t))
                last.then_inc(normed, 1)
                wait_apart(dve, (normed, n(1)))
                for t in range(TT):
                    last = dve.bn_aggr(mv[:, t, :], stats[:, t, :])
                if phase != 2:
                    last.then_inc(var_ready, 1)
                else:
                    last.then_inc(normed, 1)
                    dve.wait_ge(normed, n(2))
                    dve.tensor_tensor(sdev[:, :], mv[:, :, 0], mv[:, :, 0], ALU.mult).then_inc(normed, 1)
                    dve.wait_ge(normed, n(3))
                    dve.tensor_tensor(mv[:, :, 1], mv[:, :, 1], sdev[:, :], ALU.add).then_inc(var_ready, 1)

            def split_lo(dst, src, hi, sem_):
                dve.tensor_tensor(dst, src, hi.bitcast(F32), ALU.subtract).then_inc(sem_, 1)

            def attention(L):
                ub, sb_, ab, hb = (0 for n in (LAYERS[0].n_use, LAYERS[0].n_step, LAYERS[0].n_act, H))
                nS, per = len(L.steps), len(L.tiles)
                qb, kb, vb = ("q_b", "k_b", "v_b") if L.index == 0 else ("q_b1", "k_b1", "v_b1")
                for s in range(2):
                    dve.memset(QS[ROWMASK:P, s, :, :].bitcast(F32), 1.0)
                    dve.memset(KS[ROWMASK:P, s, :, :].bitcast(F32), 1.0)
                last = dve.memset(VP[:, :, :, 2 * HD:VW].bitcast(F32), 1.0)
                link(last)
                for s in range(2):
                    last = dve.memset(KS[ROWMASK:ROWMASK + 1, s, :, 0:S].bitcast(F32), 0.0)
                last.then_inc(consts, 1)
                N = 3 if L.index == 0 else 1
                with dve.Fori(0, B) as b:
                    if L.index == 0:
                        def n(k):
                            return at(0, b, 3, k)
                        dve.wait_ge(x_loaded, at(0, b, 16, 16))
                        norm_stats(L, lambda t: tok[:, t, :], n, 0)
                        dve.wait_ge(sd_ready, at(0, b, 1, 1))
                        dve.reciprocal(rstd[:, :], sdev[:, :]).then_inc(normed, 1)
                        dve.wait_ge(normed, n(2))
                        for t in range(TT):
                            last = dve.tensor_scalar(tok[:, t, :], tok[:, t, :], mv[:, t, 0:1], rstd[:, t:t + 1],
                                                     ALU.subtract, ALU.mult)
                        last.then_inc(normed, 1)

                    def evac(u):
                        dve.wait_ge(act_out, at(ab, b, L.n_act, L.act[u] + 1))
                        return bank[L.use[u] % 2]

                    for k in range(KT):
                        src = evac(f"T{k}")
                        split_lo(xT[:, 1, k, :], src[:, :], xT[:, 0, k, :], pb_free)
                    src = evac("C")
                    split_lo(cT[:, 1, :, :], src[:, 0:KT * C].rearrange("p (k n) -> p k n", k=KT),
                             cT[:, 0, :, :], pb_free)
                    for t in L.tiles:
                        src = evac(f"V{t}")
                        m = C if t == CT else P
                        split_lo(VP[0:m, t, :, HD:2 * HD], src[0:m, :].rearrange("p (h d) -> p h d", h=H),
                                 VP[0:m, t, :, 0:HD], pb_free)

                    def q_lo(c):
                        src = evac(f"Q{c}")
                        dve.scalar_tensor_tensor(out=qt[:, 1, :], in0=src[:, :], scalar=par(qb, c),
                                                 in1=qt[:, 0, :].bitcast(F32), op0=ALU.add,
                                                 op1=ALU.subtract).then_inc(pb_free, 1)

                    def k_lo(c):
                        for u in ([f"K{c}"] if L.main else []) + [f"KC{c}"]:
                            src = evac(u)
                            o, m = (0, S) if u[:2] != "KC" else (S, C)
                            dve.scalar_tensor_tensor(out=kt[:, 1, o:o + m], in0=src[:, 0:m], scalar=par(kb, c),
                                                     in1=kt[:, 0, o:o + m].bitcast(F32), op0=ALU.add,
                                                     op1=ALU.subtract).then_inc(pb_free, 1)

                    mb, cb = (B * 64 * 0, 0)

                    def max_main(c, m):
                        dve.wait_ge(mm_full, at(0, b, 16 * G, 16 * c + m + 1))
                        dve.tensor_reduce(nm_main[:, m:m + 1], bank[2][:, :], AX_X, ALU.max, negate=True)\
                            .then_inc(mm_free, 1)

                    def max_ctx(c, j):
                        dve.wait_ge(mc_full, at(cb, b, H, HG * c + j + 1))
                        dst = nm_ctx if L.main else nm
                        if not L.main and j == 0:
                            dve.wait_ge(pb_free, at(ub, b, L.n_use, L.use[f"R{c - 1}"] + 1 if c else 0))
                        dve.tensor_reduce(dst[:, 4 * j:4 * j + 4],
                                          bank[3][:, 0:TT * C].rearrange("p (q n) -> p q n", q=TT),
                                          AX_X, ALU.max, negate=True).then_inc(mc_free, 1)

                    def max_join(c):
                        if L.main:
                            dve.wait_ge(mm_free, at(0, b, 16 * G, 16 * (c + 1)))
                            dve.wait_ge(mc_free, at(cb, b, H, HG * (c + 1)))
                            dve.tensor_tensor(nm, nm_main, nm_ctx, ALU.min).then_inc(nm_ready, 1)

                    def max_turned(c):
                        dve.wait_ge(pb_full, at(ub, b, L.n_use, L.use[f"R{c}"] + 1))
                        dve.wait_ge(maxed[c % 2], at(0, b, 32, 16 * (c // 2)))
                        dve.tensor_copy(nT[0:16, c % 2, :], bank[L.use[f"R{c}"] % 2][0:16, 0:P]).then_inc(pb_free, 1)

                    def lo_p(c, i):
                        m = c * nS + i
                        rows = C if L.steps[i][1] == CT else P
                        dve.wait_ge(p_hi, at(sb_, b, L.n_step, m + 1))
                        split_lo(pl[0:rows, m % PRING, :], pf[0:rows, m % PRING, :], ph[0:rows, m % PRING, :], p_lo)

                    def o_sum(h):
                        dve.wait_ge(sg_ready, at(hb, b, H, h + 1))
                        dve.tensor_tensor(sg[0:HD, h % 2, :], bank[6 + h % 2][HD:2 * HD, :], sg[0:HD, h % 2, :],
                                          ALU.add).then_inc(o_free, 1)

                    q_lo(0)
                    k_lo(0)
                    q_lo(1)
                    k_lo(1)
                    for j in range(HG):
                        if L.main:
                            for q in range(TT):
                                max_main(0, 4 * j + q)
                        max_ctx(0, j)
                    max_join(0)
                    max_turned(0)
                    for c in range(G):
                        done = 0
                        for i in range(nS):
                            j, t = L.steps[i]
                            if c + 1 < G:
                                if L.main and t < TT:
                                    max_main(c + 1, 4 * j + t)
                                if t == CT:
                                    max_ctx(c + 1, j)
                            lo_p(c, i)
                            if done < HG - 1 and i == (done + 1) * per - 1 + LAG + 1:
                                o_sum(HG * c + done)
                                done += 1
                        if c + 1 < G:
                            max_join(c + 1)
                        for j in range(done, HG - 1):
                            o_sum(HG * c + j)
                        if c + 2 < G:
                            q_lo(c + 2)
                        if c + 1 < G:
                            max_turned(c + 1)
                        if c + 2 < G:
                            k_lo(c + 2)
                        o_sum(HG * c + HG - 1)

                    for s in range(2):
                        dve.wait_ge(o_moved[s], at(0, b, 256, 256))
                    dve.reciprocal(r16[0:H, :], s16[0:H, :]).then_inc(r_ready, 1)
                    dve.wait_ge(r_spread, at(0, b, 256, 256))
                    for k in range(KT):
                        dve.tensor_tensor(oa[:, k, :], oa[:, k, :], rb[:, k, :], ALU.mult).then_inc(scaled, 1)
                    for k in range(KT):
                        dve.wait_ge(scaled, at(0, b, KT, k + 1))
                        dve.tensor_scalar(xT[:, 0, k, :], oa[:, k, :], par(vb, k), None, ALU.add)\
                            .then_inc(att_ready, 1)
                    for k in range(KT):
                        dve.wait_ge(att_ready, at(0, b, 2 * KT, k + 1))
                        dve.scalar_tensor_tensor(out=xT[:, 1, k, :], in0=oa[:, k, :], scalar=par(vb, k),
                                                 in1=xT[:, 0, k, :].bitcast(F32), op0=ALU.add,
                                                 op1=ALU.subtract).then_inc(att_ready, 1)
                    for t in range(TT):
                        dve.wait_ge(pb_full, at(ub, b, L.n_use, L.use[f"O{t}"] + 1))
                        dve.wait_ge(xb_ready, at(0, b, TT, t + 1))
                        dve.tensor_tensor(tok[:, t, :], bank[L.use[f"O{t}"] % 2][:, :], tok[:, t, :],
                                          ALU.add).then_inc(pb_free, 1)

            def mlp(L):
                nb = base(L, KT)
                n0 = 3 * B if L.index else 0
                npb = 3 if L.index == 0 else 5
                with dve.Fori(0, B) as b:
                    def n(k):
                        return at(n0, b, npb, k)
                    dve.wait_ge(nt_loaded, at(base(L, 16), b, 16, 16))
                    norm_stats(L, lambda t: nt[:, t, :], n, 1 + L.index)
                    k0 = 1 if L.index == 0 else 3
                    dve.wait_ge(sd_ready, at(B * L.index, b, 1, 1))
                    dve.reciprocal(rstd[:, :], sdev[:, :]).then_inc(normed, 1)
                    dve.wait_ge(normed, n(k0 + 1))
                    for t in range(TT):
                        if L.index == 0:
                            last = dve.tensor_scalar(nt[:, t, :], nt[:, t, :], mv[:, t, 0:1], rstd[:, t:t + 1],
                                                     ALU.subtract, ALU.mult)
                        else:
                            last = dve.tensor_scalar(nt[:, t, :], nt[:, t, :], rstd[:, t:t + 1], None, ALU.mult)
                    last.then_inc(normed, 1)
                    for k in range(KT):
                        dve.wait_ge(y_hi, at(nb, b, KT, k + 1))
                        split_lo(yT[:, 1, k, ds(b * S, S)], bank[k][:, :], yT[:, 0, k, ds(b * S, S)], y_ready)
                    dve.wait_ge(acc_loaded, at(base(L, 16), b, 16, 16))
                    dve.wait_ge(brow_loaded, 16 * (2 * L.index + 2) + ONE)
                    for t in range(TT):
                        a = acc_[:, ds(b * (TT * D) + t * D, D)]
                        last = dve.tensor_tensor(a, a, brow[:, :], ALU.add)
                    last.then_inc(biased, 1)
                gb = base(L, NGRP * NCH)
                with dve.Fori(0, NGRP // 2) as gg:
                    for s in range(2):
                        with dve.Fori(0, B) as b:
                            it = gg * (2 * B * NCH) + b * NCH
                            for i in range(NCH):
                                m = gb + s * B * NCH + i
                                dve.wait_ge(g_act, it + (m + 1 + ONE))
                                dve.tensor_copy(gs[:, 0, i, :], gf[:, i % 2, :]).then_inc(g_hi, 1)
                                dve.wait_ge(g_hi, it + (m + 1 + ONE))
                                split_lo(gs[:, 1, i, :], gf[:, i % 2, :], gs[:, 0, i, :], g_lo)
                            dve.wait_ge(biased, B * (L.index + 1) + ONE)
                            for t in range(TT):
                                dve.wait_ge(a_full, it + (gb + s * B * NCH + t + 1 + ONE))
                                a = acc_[:, ds(b * (TT * D) + t * D, D)]
                                dve.tensor_tensor(a, bank[4 + t][:, :], a, ALU.add).then_inc(acc_added, 1)

            attention0()
            mlp(LAYERS[0])
            attention(LAYERS[1])
            mlp(LAYERS[1])

        @block.tensor
        def _(pe):
            HL = ((0, 0), (0, 1), (1, 0))
            LH = ((0, 0), (1, 0), (0, 1))

            pe.wait_ge(par_loaded, 16 * (len(order) + 2) + ONE)
            pe.wait_ge(ident_ready, 2 + ONE)
            pe.transpose(bank[0][:, 0:NPAR], par_rows, ident[0:NPAR, 0:NPAR]).then_inc(par_turned, 1)

            def attention0():
                def free(b, u, first=False, last=False):
                    n = use0(u, first=first, last=last)
                    pe.wait_ge(pb0_free, at(0, b, 16, n - 1))
                    return bank[n % 2]

                def front(nb, b, first):
                    pe.wait_ge(tok_normed, at(0, nb, 3, 3))
                    for k in range(KT):
                        dst = free(b, f"T{k}", first)
                        for t in range(TT):
                            last = pe.transpose(dst[:, t * P:(t + 1) * P], tok0[:, t, k * P:(k + 1) * P], ident[:, :])
                        last.then_inc(pb0_full, 1)
                    dst = free(b, "C", first)
                    pe.wait_ge(ctx_loaded, at(0, nb, 32, 32))
                    for k in range(KT):
                        last = pe.transpose(dst[:, k * P:(k + 1) * P], ctok0[:, k * P:(k + 1) * P], ident[:, :])
                    last.then_inc(pb0_full, 1)
                    for i in range(2):
                        dst = free(b, f"K{i}", first)
                        pe.wait_ge(pb0_free, at(0, b, 16, use0("C", first=first) + 1))
                        for c in (2 * i, 2 * i + 1):
                            for k in range(KT):
                                for a, d in HL:
                                    last = pe.matmul(dst[:, (c % 2) * C:(c % 2) * C + C],
                                                     W[:, 1, a, k, c * P:(c + 1) * P], cT0[:, d, k, 0:C],
                                                     start=(k == 0 and a == 0 and d == 0),
                                                     stop=(k == KT - 1 and a == 1))
                        last.then_inc(pb0_full, 1)

                def values(b, first):
                    dst = free(b, "V", first)
                    for k in range(KT):
                        for a, d in HL:
                            last = pe.matmul(dst[:, :], cT0[:, a, k, :], W[:, 2, d, k, :],
                                             start=(k == 0 and a == 0 and d == 0),
                                             stop=(k == KT - 1 and a == 1))
                    last.then_inc(pb0_full, 1)

                def batch(b, last_batch):
                    def q_proj(c):
                        dst = free(b, f"Q{c}")
                        for k in range(KT):
                            for a, d in HL:
                                last = pe.matmul(dst[:, :], W[:, 0, a, k, c * P:(c + 1) * P], xT0[:, d, k, :],
                                                 start=(k == 0 and a == 0 and d == 0),
                                                 stop=(k == KT - 1 and a == 1))
                        last.then_inc(pb0_full, 1)

                    def scores(c):
                        pe.wait_ge(pb0_free, at(0, b, 16, use0(f"Q{c}") + 1))
                        if c == 0:
                            pe.wait_ge(k_spread, at(0, b, 2, 2))
                        for u in (2 * c, 2 * c + 1):
                            pe.wait_ge(s0_less, at(0, b, 2 * G, u - 1))
                            for i in range(2):
                                dst = bank[2 + u % 2][:, i * HG * C:(i + 1) * HG * C]
                                q = (2 * (u % 2) + i) * P
                                for a, d in HL:
                                    pe.matmul(dst, qg[:, c % 2, a, q:q + P], KB[:, d, c, :],
                                              start=(a == 0 and d == 0), stop=False)
                                last = pe.matmul(dst, first_[:, :], KM_[:, ds(b * (HG * C), HG * C)],
                                                 start=False, stop=True)
                            last.then_inc(s0_full, 1)

                    def turn(c):
                        pe.wait_ge(prob_ready, at(0, b, 2 * G, 2 * c + 2))
                        for a in range(PAIRS):
                            pe.wait_ge(pt_lo, at(0, b, 2 * G, 2 * c - 1 + a))
                            for q in range(TT):
                                o = (q % 2) * HG * C + a * P
                                last = pe.transpose(bank[4 + a][:, q * P:(q + 1) * P],
                                                    pn[:, (2 * c + q // 2) % 4, o:o + P], ident[:, :])
                            last.then_inc(pt_full, 1)

                    def out_(c):
                        pe.wait_ge(pt_lo, at(0, b, 2 * G, 2 * c + 2))
                        pe.wait_ge(o0_lo, at(0, b, G, c - 1))
                        for a in range(PAIRS):
                            for v, p in HL:
                                last = pe.matmul(bank[6 + c % 2][:, :], VB[:, v, c, a, :], PT[:, c % 2, a, p, :],
                                                 start=(a == 0 and v == 0 and p == 0),
                                                 stop=(a == PAIRS - 1 and v == 1))
                        last.then_inc(o0_full, 1)

                    q_proj(0)
                    q_proj(1)
                    scores(0)
                    for c in range(G):
                        if c + 2 < G:
                            q_proj(c + 2)
                        if c + 1 < G:
                            scores(c + 1)
                        if c == G - 1 and not last_batch:
                            front(b + 1, b, False)
                        turn(c)
                        if c:
                            out_(c - 1)
                    out_(G - 1)
                    if not last_batch:
                        values(b, False)
                    pe.wait_ge(o0_lo, at(0, b, G, G))
                    for t in range(TT):
                        dst = free(b, f"O{t}", last=last_batch)
                        for k in range(KT):
                            for a, d in HL:
                                last = pe.matmul(dst[:, :], aT[:, a, k, t * P:(t + 1) * P], W[:, 3, d, k, :],
                                                 start=(k == 0 and a == 0 and d == 0),
                                                 stop=(k == KT - 1 and a == 1))
                        last.then_inc(pb0_full, 1)

                pe.wait_ge(consts, 4 + ONE)
                pe.wait_ge(w_lo, 4 * KT + ONE)
                front(0, 0, True)
                values(0, True)
                with pe.Fori(0, B - 1) as b:
                    batch(b, False)
                batch(B - 1, True)

            def attention(L):
                ub, sb_, hb = (0 for n in (LAYERS[0].n_use, LAYERS[0].n_step, H))
                nS, per = len(L.steps), len(L.tiles)
                wb = (4 + 2 * NGRP) * L.index
                NU = 4 * KT + 2 * KT * NGRP

                def weights(slot):
                    done = {0: KT, 1: 2 * KT, 2: 3 * KT, 3: 4 * KT}[slot]
                    if L.index and slot == 1:
                        done = 3 * KT
                    pe.wait_ge(w_lo, NU * L.index + done + ONE)
                pe.wait_ge(consts, 5 + ONE)
                with pe.Fori(0, B) as b:
                    def free(u):
                        m = L.use[u]
                        pe.wait_ge(pb_free, at(ub, b, L.n_use, m - 1))
                        return bank[m % 2]

                    if L.index == 0:
                        pe.wait_ge(normed, at(0, b, 3, 3))
                    else:
                        pe.wait_ge(x_loaded, at(0, b, 16, 16))
                    for k in range(KT):
                        dst = free(f"T{k}")
                        for t in range(TT):
                            last = pe.transpose(dst[:, t * P:(t + 1) * P], tok[:, t, k * P:(k + 1) * P], ident[:, :])
                        last.then_inc(pb_full, 1)
                    dst = bank[L.use["C"] % 2]
                    wait_apart(pe, (c_loaded, at(0, b, 16, 16)),
                               (pb_free, at(ub, b, L.n_use, L.use["C"] - 1)))
                    for k in range(KT):
                        last = pe.transpose(dst[:, k * C:(k + 1) * C], ctok[0:C, k * P:(k + 1) * P], ident[0:C, 0:C])
                    last.then_inc(pb_full, 1)

                    def inputs(u):
                        pe.wait_ge(pb_free, at(ub, b, L.n_use, L.use[u] + 1))

                    weights(2)
                    for t in L.tiles:
                        dst = free(f"V{t}")
                        inputs("C")
                        m = C if t == CT else P
                        last = None
                        for k in range(KT):
                            for a, c in HL:
                                src = cT[:, a, k, :] if t == CT else xT[:, a, k, t * P:(t + 1) * P]
                                last = pe.matmul(dst[0:m, :], src, W[:, 2, c, k, :],
                                                 start=(k == 0 and a == 0 and c == 0),
                                                 stop=(k == KT - 1 and a == 1))
                        last.then_inc(pb_full, 1)

                    def project(u, slot, c, src, m):
                        dst = free(u)
                        for k in range(KT):
                            for a, d in HL:
                                last = pe.matmul(dst[:, 0:m], W[:, slot, a, k, c * P:(c + 1) * P], src[:, d, k, :],
                                                 start=(k == 0 and a == 0 and d == 0),
                                                 stop=(k == KT - 1 and a == 1))
                        last.then_inc(pb_full, 1)

                    def q_proj(c):
                        project(f"Q{c}", 0, c, xT, S)

                    def k_proj(c):
                        if L.main:
                            project(f"K{c}", 1, c, xT, S)
                        project(f"KC{c}", 1, c, cT, C)

                    def stacks(c):
                        pe.wait_ge(stacked[c % 2], at(0, b, 2 * STK, STK * (c // 2 + 1)))

                    def max_main(c, m):
                        j, q = divmod(m, TT)
                        n = 16 * c + m
                        pe.wait_ge(mm_free, at(0, b, 16 * G, n))
                        pe.matmul(bank[2][:, :], QS[0:ROWMAX, c % 2, j, q * P:(q + 1) * P],
                                  KS[0:ROWMAX, c % 2, j, 0:S], start=True, stop=True).then_inc(mm_full, 1)

                    def max_ctx(c, j):
                        pe.wait_ge(mc_free, at(hb, b, H, HG * c + j))
                        for q in range(TT):
                            last = pe.matmul(bank[3][:, q * C:(q + 1) * C], QS[0:ROWMAX, c % 2, j, q * P:(q + 1) * P],
                                             KS[0:ROWMAX, c % 2, j, S:NK], start=True, stop=True)
                        last.then_inc(mc_full, 1)

                    def max_turn(c):
                        if L.main:
                            pe.wait_ge(nm_ready, at(0, b, G, c + 1))
                        else:
                            pe.wait_ge(mc_free, at(hb, b, H, HG * (c + 1)))
                        dst = free(f"R{c}")
                        pe.transpose(dst[0:16, 0:P], nm, ident[:, :]).then_inc(pb_full, 1)

                    def scores(c, i):
                        j, t = L.steps[i]
                        n = c * nS + i
                        if i == 0:
                            pe.wait_ge(maxed[c % 2], at(0, b, 32, 16 * (c // 2 + 1)))
                        pe.wait_ge(p_exp, at(sb_, b, L.n_step, n - 1))
                        m = C if t == CT else P
                        pe.matmul(bank[4 + n % 2][0:m, :], KS[0:ROWMAX + 1, c % 2, j, t * P:t * P + m],
                                  QS[0:ROWMAX + 1, c % 2, j, :], start=True, stop=True).then_inc(s_full, 1)

                    def values(c, i):
                        j, t = L.steps[i]
                        n = c * nS + i
                        h = HG * c + j
                        m = C if t == CT else P
                        if t == L.tiles[0]:
                            pe.wait_ge(o_free, at(hb, b, H, h - 1))
                        pe.wait_ge(p_lo, at(sb_, b, L.n_step, n + 1))
                        v = VP[0:m, t, h, 0:2 * HD + 1]
                        o = bank[6 + h % 2][0:2 * HD + 1, :]
                        pe.matmul(o, v, ph[0:m, n % PRING, :], start=(t == L.tiles[0]), stop=False)
                        pe.matmul(o, v, pl[0:m, n % PRING, :], start=False, stop=(t == CT)).then_inc(pv_step, 1)

                    weights(0)
                    q_proj(0)
                    weights(1)
                    k_proj(0)
                    q_proj(1)
                    k_proj(1)
                    stacks(0)
                    for j in range(HG):
                        if L.main:
                            for q in range(TT):
                                max_main(0, TT * j + q)
                        max_ctx(0, j)
                    max_turn(0)
                    for c in range(G):
                        if c + 1 < G:
                            stacks(c + 1)
                        for i in range(nS):
                            j, t = L.steps[i]
                            scores(c, i)
                            if c + 1 < G:
                                if L.main and t < TT:
                                    max_main(c + 1, TT * j + t)
                                if t == CT:
                                    max_ctx(c + 1, j)
                            if i >= LAG:
                                values(c, i - LAG)
                        last_head = max(nS - LAG, nS - per)
                        for i in range(nS - LAG, last_head):
                            values(c, i)
                        if c + 2 < G:
                            q_proj(c + 2)
                        if c + 1 < G:
                            max_turn(c + 1)
                        if c + 2 < G:
                            k_proj(c + 2)
                        for i in range(last_head, nS):
                            values(c, i)
                    weights(3)
                    pe.wait_ge(att_ready, at(0, b, 2 * KT, 2 * KT))
                    for t in range(TT):
                        dst = free(f"O{t}")
                        for k in range(KT):
                            for a, d in HL:
                                last = pe.matmul(dst[:, :], xT[:, a, k, t * P:(t + 1) * P], W[:, 3, d, k, :],
                                                 start=(k == 0 and a == 0 and d == 0),
                                                 stop=(k == KT - 1 and a == 1))
                        last.then_inc(pb_full, 1)

            def mlp(L):
                nb = base(L, KT)
                NU = 4 * KT + 2 * KT * NGRP
                ub = base(L, LAYERS[0].n_use)
                n0 = 3 * B if L.index else 0
                npb = 3 if L.index == 0 else 5
                with pe.Fori(0, B) as b:
                    pe.wait_ge(normed, at(n0, b, npb, npb))
                    for k in range(KT):
                        pe.wait_ge(y_ready, at(nb, b, KT, 0))
                        for t in range(TT):
                            last = pe.transpose(bank[k][:, t * P:(t + 1) * P], nt[:, t, k * P:(k + 1) * P], ident[:, :])
                        last.then_inc(t_full, 1)
                pe.wait_ge(y_ready, KT * B * (L.index + 1) + ONE)
                gb = base(L, NGRP * NCH)
                with pe.Fori(0, NGRP // 2) as gg:
                    for s in range(2):
                        wait_apart(pe, (w_lo, gg * (4 * KT) + (NU * L.index + 4 * KT + (s + 1) * 2 * KT + ONE)))
                        with pe.Fori(0, B) as b:
                            it = gg * (2 * B * NCH) + b * NCH
                            g0 = gb + s * B * NCH

                            def fc1(i):
                                if i == 0:
                                    wait_apart(pe, (g_act, it + (g0 + ONE)))
                                for k in range(KT):
                                    for a, d in HL:
                                        last = pe.matmul(bank[i][:, :], W[:, 2 * s, a, k, i * P:(i + 1) * P],
                                                         yT[:, d, k, ds(b * S, S)],
                                                         start=(k == 0 and a == 0 and d == 0),
                                                         stop=(k == KT - 1 and a == 1))
                                last.then_inc(f_full, 1)

                            def fc2(i):
                                if i == 0:
                                    pe.wait_ge(acc_added, it + (g0 + ONE))
                                pe.wait_ge(g_lo, it + (g0 + i + 1 + ONE))
                                for t in range(TT):
                                    for a, d in HL:
                                        last = pe.matmul(bank[4 + t][:, :], gs[:, a, i, t * P:(t + 1) * P],
                                                         W[:, 2 * s + 1, d, i, :],
                                                         start=(i == 0 and a == 0 and d == 0),
                                                         stop=(i == NCH - 1 and a == 1))
                                    if i == NCH - 1:
                                        last.then_inc(a_full, 1)

                            fc1(0)
                            fc1(1)
                            fc2(0)
                            fc1(2)
                            fc2(1)
                            fc1(3)
                            fc2(2)
                            fc2(3)

            attention0()
            mlp(LAYERS[0])
            attention(LAYERS[1])
            mlp(LAYERS[1])


_WEIGHTS = {
    "ln1_w": "L0_xattn_ln1_w", "ln1_b": "L0_xattn_ln1_b", "q_w": "L0_xattn_q_w", "q_b": "L0_xattn_q_b",
    "k_w": "L0_xattn_k_w", "k_b": "L0_xattn_k_b", "v_w": "L0_xattn_v_w", "v_b": "L0_xattn_v_b",
    "cproj_w": "L0_xattn_cproj_w", "cproj_b": "L0_xattn_cproj_b", "ln2_w": "L0_xattn_ln2_w",
    "ln2_b": "L0_xattn_ln2_b", "fc_w": "L0_xattn_fc_w", "fc_b": "L0_xattn_fc_b",
    "proj_w": "L0_xattn_proj_w", "proj_b": "L0_xattn_proj_b", "q_w1": "L1_xattn_q_w",
    "q_b1": "L1_xattn_q_b", "kv_w": "L1_xattn_kv_w", "kv_b": "L1_xattn_kv_b", "out_w": "L1_xattn_out_w",
    "out_b": "L1_xattn_out_b", "post_w": "L1_xattn_postnorm_w", "mlp_w1": "L1_xattn_mlp_w1",
    "mlp_b1": "L1_xattn_mlp_b1", "mlp_w2": "L1_xattn_mlp_w2", "mlp_b2": "L1_xattn_mlp_b2",
}


def kernel(**inputs):
    import numpy as np
    import concourse.bacc as bacc
    from concourse.bass_utils import run_bass_kernel_spmd

    nc = bacc.Bacc("TRN2", target_bir_lowering=False, num_devices=1)
    arrays = {}

    def dram_in(name):
        a = np.ascontiguousarray(inputs[name])
        if a.dtype == np.bool_:
            a = a.view(np.uint8)
        arrays[f"in_{name}_dram"] = a
        return nc.dram_tensor(f"in_{name}_dram", a.shape, mybir.dt.from_np(a.dtype), kind="ExternalInput").ap()

    main = [dram_in(n) for n in ("x", "ctx_2048", "mask_BxS2_bf1", "mask_BxS2_ik0")]
    weights = {k: dram_in(v) for k, v in _WEIGHTS.items()}
    between = [nc.dram_tensor(n, (B, S, D), F32, kind="Internal").ap() for n in ("after_att0", "after_layer0", "after_att1")]
    out = nc.dram_tensor("out_0_dram", (B, S, D), F32, kind="ExternalOutput").ap()
    program(nc, *main, weights, *between, out)
    r = run_bass_kernel_spmd(nc, [arrays], core_ids=[0])
    return r.results[0]["out_0_dram"]
```

```python
from contextlib import ExitStack

import concourse.bass as bass
from concourse import mybir

F32 = mybir.dt.float32
F32R = mybir.dt.float32r
U8 = mybir.dt.uint8
I32 = mybir.dt.int32
ACT = mybir.ActivationFunctionType
ALU = mybir.AluOpType
AX_X = mybir.AxisListType.X
ds = bass.ds

P = 128
B, S, D = 4, 512, 512
C = 64
H, HD = 16, 32
INNER = 4 * D
KT = D // P
TT = S // P
HG = P // HD
G = H // HG
NK = S + C
ROWMASK, ROWMAX = 3 * HD, 3 * HD + 1
VW = 2 * HD + 2
BIG = 2.0 ** 126
PRING = 3
NGRP = INNER // D
NCH = D // P
FC1_BANK = (0, 1, 2, 0)
HALF = TT // 2
PAIRS = HG // 2
ONE = 1


class Layer:

    def __init__(self, index, mlp_units, att_units):
        self.index = index
        self.units = att_units
        self.before = mlp_units


NU_MLP = 2 * KT * NGRP
LAYERS = [Layer(0, 0, 0), Layer(1, NU_MLP, 6 * KT)]

STEPS = [(j, t) for j in range(HG) for t in range(TT + 1)]
NSTEP = len(STEPS)
BSTEP = G * NSTEP
SCALE0, SCALE1 = HD ** -0.5, 1.0 / HD
TURN = 18
LAG = 3


def max_items(i):
    return range(min(i * 8 // 7, NSTEP), min((i + 1) * 8 // 7, NSTEP))


def fillers(c, last):
    if c < 2:
        names = (f"Q{c + 2}", f"K{c + 2}", f"KC{c + 2}")
    else:
        names = () if last else (f"nQ{c - 2}", f"nK{c - 2}", f"nKC{c - 2}")
    plan = [(s0, n, u) for (s0, n), u in zip(((2, 4), (6, 4), (10, 1)), names)]
    if c == 1 and not last:
        plan += [(11 + k, 1, f"nT{k}") for k in range(KT)] + [(15, 1, "nC")]
    return plan


def results(last):
    out = []
    for c in range(G):
        out += [u for _, _, u in fillers(c, last)]
        out += [f"R{c + 1}"] if c + 1 < G else [] if last else ["nR0"]
    out += [] if last else [f"nV{t}" for t in range(TT + 1)]
    return out + [f"B{k}" for k in range(KT)] + [f"O{t}" for t in range(TT)]


FIRST = ([f"nT{k}" for k in range(KT)] + ["nC", "nQ0", "nK0", "nKC0", "nQ1", "nK1", "nKC1"]
         + [f"nV{t}" for t in range(TT + 1)] + ["nR0"])
BODY = {False: results(False), True: results(True)}


def split_by_act(names):
    return [u for u in names if u.lstrip("n")[0] not in "RBO"]


USES, SPLITS = len(BODY[False]), len(split_by_act(BODY[False]))


def use1(u, last=False, first=False):
    return FIRST.index(u) if first else len(FIRST) + BODY[last].index(u)


def split1(u, last=False, first=False):
    return split_by_act(FIRST).index(u) if first else \
        len(split_by_act(FIRST)) + split_by_act(BODY[last]).index(u)


def by_act(i):
    return STEPS[i % NSTEP][1] in (1, 3)


def kind_count(i):
    return sum(by_act(m) == by_act(i) for m in range(i + 1))


ACT_STEPS = sum(by_act(m) for m in range(BSTEP))
STACK = 16 * 13


def stack_count(c):
    return 16 * 7 if c < 2 else STACK


def at(base, b, per, n):
    return b * per + (base + max(n, 0) + ONE)


def program(nc, x, ctx, mask_bool, mask_int, w, x1, xm, x2, q_parts, k_parts, out):
    es = ExitStack()
    with es:
        def sb(name, shape, dt):
            return es.enter_context(nc.sbuf_tensor(name, shape, dt))

        started = []

        def sem(name):
            started.append(es.enter_context(nc.semaphore(name)))
            return started[-1]

        bank = [es.enter_context(nc.psum_tensor(f"bank{i}", [P, 512], F32)) for i in range(8)]

        W = sb("W", [P, 4, 2, KT, D], F32R)
        raw = sb("raw", [P, 2, D], F32)
        ident = sb("ident", [P, P], F32)
        cols = sb("cols", [P, 80], F32)
        brow = sb("brow", [P, D], F32)
        stats = sb("stats", [P, TT, 6], F32)
        mv = sb("mv", [P, TT, 2], F32)
        sdev = sb("sdev", [P, TT], F32)
        rstd = sb("rstd", [P, TT], F32)
        anyk = sb("anyk", [P, B], F32)

        rows_ = sb("rows_", [P, 2 * B * C], F32R)

        NR_ATT = (2 * KT * S + 2 * KT * C + 2 * HG * S + 2 * HG * NK + 5 * H * VW
                  + 2 * PRING * S + 2 * 2 * KT * P)
        NR_MLP = 2 * KT * B * S + 2 * 4 * S
        RA = sb("RA", [P, max(NR_ATT, NR_MLP)], F32R)
        NF_ATT = PRING * S + 2 * S + KT * S + TT * D + D + 2 * D + 4 * 16 + 2 * S + 2 * NK
        NF_MLP = B * TT * D + TT * D
        FA = sb("FA", [P, max(NF_ATT, NF_MLP)], F32)

        def cut(arena, sizes):
            o, parts = 0, []
            for n in sizes:
                parts.append(arena[:, o:o + n])
                o += n
            return parts

        kbias = rows_[32:33, :].rearrange("p (l n) -> p l n", l=2)
        nT = rows_[0:H, 0:2 * P].rearrange("p (s n) -> p s n", s=2)
        pick = rows_[C:C + H, :].bitcast(F32)
        xT_, cT_, QS_, KS_, VP_, ph_, pl_, AS_ = cut(RA, [
            2 * KT * S, 2 * KT * C, 2 * HG * S, 2 * HG * NK, 5 * H * VW,
            PRING * S, PRING * S, 2 * 2 * KT * P])
        xT = xT_.rearrange("p (h k n) -> p h k n", h=2, k=KT)
        cT = cT_.rearrange("p (h k n) -> p h k n", h=2, k=KT)
        QS = QS_.rearrange("p (s j n) -> p s j n", s=2, j=HG)
        KS = KS_.rearrange("p (s j n) -> p s j n", s=2, j=HG)
        VP = VP_.rearrange("p (t h n) -> p t h n", t=5, h=H)
        ph = ph_.rearrange("p (r n) -> p r n", r=PRING)
        pl = pl_.rearrange("p (r n) -> p r n", r=PRING)
        AS = AS_.rearrange("p (r h k n) -> p r h k n", r=2, h=2, k=KT)
        tok_, ct_, pf_, sg_, oa_, res_, nm_, qt_, kt_ = cut(FA, [
            TT * D, D, PRING * S, 2 * S, KT * S, 2 * D, 4 * 16, 2 * S, 2 * NK])
        qt = qt_.bitcast(F32R).rearrange("p (h n) -> p h n", h=2)
        kt = kt_.bitcast(F32R).rearrange("p (h n) -> p h n", h=2)
        res = res_.rearrange("p (r n) -> p r n", r=2)
        pf = pf_.rearrange("p (r n) -> p r n", r=PRING)
        sg = sg_.rearrange("p (r n) -> p r n", r=2)
        oa = oa_.rearrange("p (k n) -> p k n", k=KT)
        tok = tok_.rearrange("p (t n) -> p t n", t=TT)
        ctok = ct_[0:C, :]
        s16 = ct_[C:C + H, :]
        nm_main, nm_ctx, nm = nm_[:, 0:16], nm_[:, 16:32], nm_[:, 32:48]
        xT0_, cT0_, qg_, KB_, VB_, kk_, KM_, first_, PT_, aT_ = cut(RA, [
            2 * KT * S, 2 * KT * P, 2 * 2 * S, 2 * G * HG * C, 2 * G * PAIRS * P, 2 * G * C,
            B * HG * C, P, 2 * PAIRS * 2 * S, 2 * KT * S])
        xT0 = xT0_.rearrange("p (h k n) -> p h k n", h=2, k=KT)
        cT0 = cT0_.rearrange("p (h k n) -> p h k n", h=2, k=KT)
        qg = qg_.rearrange("p (r h n) -> p r h n", r=2, h=2)
        KB = KB_.rearrange("p (h c n) -> p h c n", h=2, c=G)
        VB = VB_.rearrange("p (h c a n) -> p h c a n", h=2, c=G, a=PAIRS)
        kk = kk_.rearrange("p (h n) -> p h n", h=2)
        PT = PT_.rearrange("p (r a h n) -> p r a h n", r=2, a=PAIRS, h=2)
        aT = aT_.rearrange("p (h k n) -> p h k n", h=2, k=KT)
        tok0_, res0_, ex_, pn_, ctok0, kf, HM, mx_, sm_, rc_, wk_ = cut(FA, [
            TT * D, TT * D, 2 * S, 4 * S, D, G * C, HG, 16, 16, 16, KT * D])
        tok0 = tok0_.rearrange("p (t n) -> p t n", t=TT)
        res0 = res0_.rearrange("p (t n) -> p t n", t=TT)
        ex = ex_.rearrange("p (r n) -> p r n", r=2)
        pn = pn_.rearrange("p (r n) -> p r n", r=4)
        mx = mx_.rearrange("p (r n) -> p r n", r=2)
        sm = sm_.rearrange("p (r n) -> p r n", r=2)
        rc = rc_.rearrange("p (r n) -> p r n", r=2)
        first_w = [t.rearrange("p (k n) -> p k n", k=KT) for t in (wk_, pn_, res0_, wk_)]
        yT_, g_ = cut(RA, [2 * KT * B * S, 2 * 4 * S])
        yT = yT_.rearrange("p (h k n) -> p h k n", h=2, k=KT)
        gs = g_.rearrange("p (h r n) -> p h r n", h=2, r=4)
        acc_, nt_ = cut(FA, [B * TT * D, TT * D])
        nt_ = nt_.rearrange("p (r t n) -> p r t n", r=2, t=HALF)
        nt, gf = nt_[:, 0, :, :], nt_[:, 1, :, :]

        ident_ready = sem("ident_ready")
        par_loaded = sem("par_loaded")
        par_turned = sem("par_turned")
        consts = sem("consts")
        dve_own = sem("dve_own")
        brow_loaded = sem("brow_loaded")
        x_loaded = sem("x_loaded")
        c_loaded = sem("c_loaded")
        var_ready = sem("var_ready")
        sd_ready = sem("sd_ready")
        normed = sem("normed")
        pb_full = sem("pb_full")
        pb_free = sem("pb_free")
        act_out = sem("act_out")
        act_own = sem("act_own")
        parted = [[sem(f"{x}_parted{i}") for i in range(2)] for x in "qk"]
        stacked = [[sem(f"stacked{i}_{j}") for j in range(2)] for i in range(2)]
        maxed = [sem("maxed0"), sem("maxed1")]
        mm_full = sem("mm_full")
        mm_free = sem("mm_free")
        nm_ready = sem("nm_ready")
        s_full = sem("s_full")
        p_exp = sem("p_exp")
        p_hi = sem("p_hi")
        p_lo = sem("p_lo")
        p_lo_pool = sem("p_lo_pool")
        pv_step = sem("pv_step")
        sg_ready = sem("sg_ready")
        o_free = sem("o_free")
        o_moved = [sem("o_moved0"), sem("o_moved1")]
        r_ready = sem("r_ready")
        v_biased = sem("v_biased")
        as_hi = sem("as_hi")
        as_lo = sem("as_lo")
        xres_loaded = [sem("xres_loaded0"), sem("xres_loaded1")]
        xres_biased = sem("xres_biased")
        stored1 = [sem("stored1_0"), sem("stored1_1")]
        stored = sem("stored")
        layer_stored = [sem(f"layer_stored{b}") for b in range(B)]
        raw_loaded = [es.enter_context(nc.semaphore(f"raw_loaded{i}")) for i in range(2)]
        w0_loaded = [sem(f"w0_loaded{i}") for i in range(4)]
        w0_hi = sem("w0_hi")
        w0_kv = sem("w0_kv")
        w0_qo = sem("w0_qo")
        w_hi = sem("w_hi")
        w_lo = sem("w_lo")
        w_ready = sem("w_ready")
        acc_loaded = sem("acc_loaded")
        nt_loaded = [sem("nt_loaded0"), sem("nt_loaded1")]
        t_full = sem("t_full")
        y_hi = sem("y_hi")
        y_ready = sem("y_ready")
        f_full = sem("f_full")
        g_act = sem("g_act")
        g_hi = sem("g_hi")
        g_lo = sem("g_lo")
        a_full = sem("a_full")
        acc_added = sem("acc_added")
        biased = sem("biased")

        order = ["ln1_w", "ln1_b", "q_b", "v_b", "k_b", "ln2_w", "ln2_b", "fc_b",
                 "q_b1", "k_b1", "v_b1", "post_w", "mlp_b1"]
        col, at_row = {}, 0
        for name in order:
            col[name] = at_row
            at_row += (4 * D if name in ("fc_b", "mlp_b1") else D) // P
        NPAR = at_row

        def par(name, k):
            return cols[:, col[name] + k:col[name] + k + 1]

        par_rows = ex_[0:NPAR, 832:832 + P]
        maskf = ex_[:, 0:B * C]
        maskr = ex_[:, 256:256 + B * C // 4].bitcast(U8)
        mask2 = ex_[0:1, 320:320 + B * C].bitcast(I32)
        mask2f = ex_[0:1, 576:576 + B * C]

        def tokens(t):
            return t.rearrange("b (t p) d -> p b t d", p=P)

        tok_loaded = sem("tok_loaded")
        ctx_loaded = sem("ctx_loaded")
        res_loaded = sem("res_loaded")
        res_biased = sem("res_biased")
        tok_normed = sem("tok_normed")
        var0_ready = sem("var0_ready")
        sd0_ready = sem("sd0_ready")
        pb0_full = sem("pb0_full")
        pb0_free = sem("pb0_free")
        y0_affine = sem("y0_affine")
        in_hi = sem("in_hi")
        v_hi = sem("v_hi")
        q_hi_ready = sem("q_hi_ready")
        kh_ready = sem("kh_ready")
        kl_ready = sem("kl_ready")
        k_spread = sem("k_spread")
        s0_full = sem("s0_full")
        s0_max = sem("s0_max")
        s0_less = sem("s0_less")
        s0_exp = sem("s0_exp")
        s0_sum = sem("s0_sum")
        s0_inv = sem("s0_inv")
        prob_ready = sem("prob_ready")
        pt_full = sem("pt_full")
        pt_hi = sem("pt_hi")
        pt_lo = sem("pt_lo")
        o0_full = sem("o0_full")
        o0_hi = sem("o0_hi")
        o0_lo = sem("o0_lo")

        def use0(u, last=False, first=False):
            i = int(u[1:] or 0)
            if first:
                return {"T": 0, "C": 4, "K": 5, "V": 7}[u[0]] + i
            if u[0] == "O":
                return 12 + (i if last else 2 * i)
            return {"Q": 8, "T": 13 + i, "C": 20, "K": 21, "V": 23}[u[0]] + i

        def base(L, per0):
            return B * per0 if L.index else 0

        passed = sem("passed")

        def wait_apart(eng, *waits):
            for sem_, v in waits:
                eng.wait_ge(sem_, v)
            eng.sem_inc(passed, 1)

        block = es.enter_context(nc.Block())

        @block.sync
        def _(sp):
            def inputs0(nb):
                sp.dma_start(tok0, tokens(x)[:, ds(nb, 1), :, :]).then_inc(tok_loaded, 16)
                for i in range(2):
                    sp.dma_start(ctok0[i * C:(i + 1) * C, :], ctx[ds(nb, 1), :, :].rearrange("o c d -> (o c) d"))\
                        .then_inc(ctx_loaded, 16)

            def weights0(i):
                sp.dma_start(first_w[i],
                             w[("k_w", "v_w", "q_w", "cproj_w")[i]].rearrange("(k p) n -> p k n", p=P))\
                    .then_inc(w0_loaded[i], 16)

            inputs0(0)
            for sem_ in started:
                sp.sem_inc(sem_, ONE)
            n = 0
            for name in order:
                rows = (4 * D if name in ("fc_b", "mlp_b1") else D) // P
                if name in ("k_b1", "v_b1"):
                    two = w["kv_b"].rearrange("(c n two) -> two c n", n=P, two=2)
                    with nc.allow_non_contiguous_dma(reason="kv_b interleaves k and v"):
                        sp.dma_start(par_rows[col[name]:col[name] + rows, :],
                                     two[int(name == "v_b1")]).then_inc(par_loaded, 16)
                else:
                    sp.dma_start(par_rows[col[name]:col[name] + rows, :],
                                 w[name].rearrange("(c n) -> c n", n=P)).then_inc(par_loaded, 16)
                n += 1
            sp.dma_start(maskr, mask_bool.rearrange("b c -> (b c)").partition_broadcast(P))\
                .then_inc(par_loaded, 16)
            sp.dma_start(mask2, mask_int.rearrange("(o b) c -> o (b c)", o=1)).then_inc(par_loaded, 16)
            for i in range(3):
                weights0(i)
            sp.wait_ge(w0_kv, KT + ONE)
            weights0(3)
            sp.wait_ge(consts, 3 + ONE)

            def attention0():
                src, dst = tokens(x), tokens(x1)

                def batch(b, last):
                    wait_apart(sp, (stored, at(0, b, 64, 0)))
                    sp.dma_start(res0, src[:, ds(b, 1), :, :]).then_inc(res_loaded, 16)
                    if not last:
                        wait_apart(sp, (pb0_full, at(0, b, 16, use0("C", first=True) + 1)))
                        inputs0(b + 1)
                    for t in range(TT):
                        sp.wait_ge(pb0_free, at(0, b, 16, use0(f"O{t}", last) + 1))
                        sp.dma_start(dst[:, ds(b, 1), t:t + 1, :], res0[:, t:t + 1, :]).then_inc(stored, 16)

                sp.dma_start(brow[:, :], w["cproj_b"].partition_broadcast(P)).then_inc(brow_loaded, 16)
                sp.wait_ge(w0_qo, KT + ONE)
                with sp.Fori(0, B - 1) as b:
                    batch(b, False)
                batch(B - 1, True)

            def inputs1(nb):
                sp.dma_start(tok, tokens(xm)[:, ds(nb, 1), :, :]).then_inc(x_loaded, 16)
                sp.dma_start(ctok, ctx[ds(nb, 1), :, :].rearrange("o c d -> (o c) d")).then_inc(c_loaded, 16)

            def attention1():
                src, dst = tokens(xm), tokens(x2)

                def parts(x, nb, c):
                    for half in range(2):
                        wait_apart(sp, (stacked[c % 2][half], at(0, nb, STACK, stack_count(c - 2) if c >= 2 else 0)))
                    sp.dma_start((q_parts, k_parts)[x][c % 2], (qt, kt)[x].bitcast(F32)).then_inc(parted[x][c % 2], 16)

                def stack(nb, c, half):
                    to = stacked[c % 2][half]
                    heads = slice(2 * half, 2 * half + 2)
                    for x, dst_, src_, order_ in ((0, QS, q_parts, (0, 0, 1)), (1, KS, k_parts, (0, 1, 0))):
                        wait_apart(sp, (parted[x][c % 2], at(0, nb, 32, 16 * (c // 2 + 1))))
                        rows_of = src_[c % 2].rearrange("(j p) h n -> p j h n", p=HD)
                        for r, part in enumerate(order_):
                            sp.dma_start(dst_[r * HD:(r + 1) * HD, c % 2, heads, :].bitcast(F32),
                                         rows_of[:, heads, part, :]).then_inc(to, 16)
                    if c < 2:
                        sp.dma_start(KS[ROWMASK:ROWMASK + 1, c % 2, heads, S:NK].bitcast(F32),
                                     kbias[0:1, 1, ds(nb * C, C)].bitcast(F32).unsqueeze(1).to_broadcast([1, 2, C]))\
                            .then_inc(to, 16)

                def max_row(nb, c):
                    sp.dma_start(QS[ROWMAX:ROWMAX + 1, c % 2, :, :].rearrange("o j (q n) -> o (j q) n", n=P).bitcast(F32),
                                 nT[:, c % 2, :].bitcast(F32)).then_inc(maxed[c % 2], 16)

                def residual(b, t):
                    sp.dma_start(res[:, t % 2, :].unsqueeze(1), src[:, ds(b, 1), t, :]).then_inc(xres_loaded[t % 2], 16)

                def batch(b, last):
                    for r in range(2):
                        wait_apart(sp, (stored1[r], at(0, b, 32, 0)))
                    for t in range(2):
                        residual(b, t)
                    if not last:
                        inputs1(b + 1)
                    for c in range(G):
                        def sums(j):
                            h = HG * c + j
                            sp.wait_ge(sg_ready, at(0, b, H, h + 1))
                            sp.dma_start(s16[h:h + 1, :], sg[2 * HD:2 * HD + 1, h % 2, :])\
                                .then_inc(o_moved[h % 2], 16)
                        nc_ = (c + 2) % G
                        nb = b if c < 2 else b + 1
                        ahead = c < 2 or not last
                        pre = "" if c < 2 else "n"

                        def pair(half):
                            wait_apart(sp, (s_full, at(0, b, BSTEP, NSTEP * c + 2 * (TT + 1) * (half + 1))))
                            stack(nb, nc_, half)
                        if ahead:
                            wait_apart(sp, (pb_free, at(0, b, USES, use1(f"{pre}Q{nc_}", last) + 1)))
                            parts(0, nb, nc_)
                        sums(0)
                        if ahead:
                            wait_apart(sp, (pb_free, at(0, b, USES, use1(f"{pre}KC{nc_}", last) + 1)))
                            parts(1, nb, nc_)
                            pair(0)
                        sums(1)
                        sums(2)
                        if not (last and c == G - 1):
                            u = f"R{c + 1}" if c + 1 < G else "nR0"
                            wait_apart(sp, (pb_free, at(0, b, USES, use1(u, last) + 1)))
                            max_row(b if c + 1 < G else b + 1, (c + 1) % G)
                        if ahead:
                            pair(1)
                        sums(3)
                    for t in range(TT):
                        wait_apart(sp, (pb_free, at(0, b, USES, use1(f"O{t}", last) + 1)))
                        sp.dma_start(dst[:, ds(b, 1), t, :], res[:, t % 2, :].unsqueeze(1)).then_inc(stored1[t % 2], 16)
                        if t + 2 < TT:
                            wait_apart(sp, (stored1[t % 2], at(0, b, 32, 16 * (t // 2 + 1))))
                            residual(b, t + 2)

                for b in range(B):
                    sp.wait_ge(layer_stored[b], 16 + ONE)
                sp.dma_start(brow[:, :], w["out_b"].partition_broadcast(P)).then_inc(brow_loaded, 16)
                for c in range(2):
                    sp.wait_ge(pb_free, use1(f"nKC{c}", first=True) + 1 + ONE)
                    parts(0, 0, c)
                    parts(1, 0, c)
                    sp.wait_ge(consts, 5 + ONE)
                    for half in range(2):
                        stack(0, c, half)
                sp.wait_ge(pb_free, use1("nR0", first=True) + 1 + ONE)
                max_row(0, 0)
                with sp.Fori(0, B - 1) as b:
                    batch(b, False)
                batch(B - 1, True)

            def first_inputs1():
                for b in range(2):
                    sp.wait_ge(layer_stored[b], 16 + ONE)
                inputs1(0)

            def mlp(L):
                if L.index == 0:
                    sp.wait_ge(stored, 16 * 4 * B + ONE)
                else:
                    for r in range(2):
                        sp.wait_ge(stored1[r], 32 * B + ONE)
                sp.dma_start(brow[:, :], w["proj_b" if L.index == 0 else "mlp_b2"].partition_broadcast(P))\
                    .then_inc(brow_loaded, 16)
                left = tokens(x1 if L.index == 0 else xm)
                mid, dst = tokens((x1, x2)[L.index]), tokens((xm, out)[L.index])
                for q in range(2 * B):
                    if q > 1:
                        sp.wait_ge(t_full, 4 * B * L.index + 2 * q + ONE)
                    sp.dma_start(gf if q == 1 else nt,
                                 mid[:, q // 2, (q % 2) * HALF:(q % 2 + 1) * HALF, :]).then_inc(nt_loaded[q % 2], 16)
                    for b in {2: (0, 1), 3: (2, 3)}.get(q, ()):
                        sp.dma_start(acc_[:, b * TT * D:(b + 1) * TT * D].rearrange("p (t d) -> p t d", d=D),
                                     left[:, b, :, :]).then_inc(acc_loaded, 16)
                for b in range(B):
                    if b == 2 and L.index == 0:
                        first_inputs1()
                    sp.wait_ge(acc_added, NGRP * TT * B * (L.index + 1) - (B - 1 - b) * TT + ONE)
                    sp.dma_start(dst[:, b, :, :],
                                 acc_[:, b * TT * D:(b + 1) * TT * D].rearrange("p (t d) -> p t d", d=D))\
                        .then_inc(layer_stored[b], 16)

            attention0()
            mlp(LAYERS[0])
            attention1()
            mlp(LAYERS[1])
            for b in range(B):
                sp.wait_ge(layer_stored[b], 32 + ONE)

        @block.gpsimd
        def _(pool):
            pool.memset(ident[:], 0.0).then_inc(ident_ready, 1)
            pool.wait_ge(ident_ready, 1 + ONE)
            pool.affine_select(out=ident[:], in_=ident[:], compare_op=ALU.not_equal, fill=1.0,
                               base=0, pattern=[[-1, P]], channel_multiplier=1).then_inc(ident_ready, 1)

            def split(dsts, srcs, u, before):
                pool.wait_ge(raw_loaded[u % 2], 16 * ((before + u) // 2) + 16)
                for (hi, _), s in zip(dsts, srcs):
                    last = pool.tensor_scalar(hi, s, 1.0, 0.0, ALU.mult, ALU.add)
                last.then_inc(w_hi, 1)
                pool.wait_ge(w_hi, before + u + 1 + ONE)
                for (hi, lo), s in zip(dsts, srcs):
                    last = pool.tensor_tensor(lo, s, hi.bitcast(F32), ALU.subtract)
                last.then_inc(w_lo, 1)

            def load(srcs, u, before):
                if u == 0:
                    pool.wait_ge(w_lo, before + ONE)
                    pool.dma_start(raw[:, 0, :], srcs[0]).then_inc(raw_loaded[0], 16)
                if u + 1 < len(srcs):
                    if before + u:
                        pool.wait_ge(w_lo, before + u + ONE)
                    pool.dma_start(raw[:, (u + 1) % 2, :], srcs[u + 1]).then_inc(raw_loaded[(u + 1) % 2], 16)

            def units(srcs, before, put):
                for u in range(len(srcs)):
                    load(srcs, u, before)
                    put(u)

            def rows(m, k, c0=0):
                return m[k * P:(k + 1) * P, c0:c0 + D]

            def attention_weights(L):
                before = L.before
                its = NGRP * B * TT
                pool.wait_ge(a_full, its - B * TT + ONE)

                def put_q(u):
                    split([(W[:, 0, 0, u, :], W[:, 0, 1, u, :])], [raw[:, u % 2, :]], u, before)
                units([rows(w["q_w1"], k) for k in range(KT)], before, put_q)
                for i in range(2):
                    if i:
                        pool.wait_ge(a_full, its + ONE)
                    first = before + KT + i * 2 * KT

                    def put_kv(u):
                        k, c0 = u // 2, (u % 2) * (D // 2)
                        pair = raw[:, u % 2, :].rearrange("p (n two) -> p two n", two=2)
                        split([(W[:, 1 + i, 0, k, c0:c0 + D // 2], W[:, 1 + i, 1, k, c0:c0 + D // 2])],
                              [pair[:, i, :]], u, first)
                    units([rows(w["kv_w"], u // 2, (u % 2) * D) for u in range(2 * KT)], first, put_kv)
                first = before + 5 * KT

                def put_o(u):
                    split([(W[:, 3, 0, u, :], W[:, 3, 1, u, :])], [raw[:, u % 2, :]], u, first)
                units([rows(w["out_w"], k) for k in range(KT)], first, put_o)

            def mlp_group_weights(L, g):
                w1 = w["fc_w" if L.index == 0 else "mlp_w1"]
                w2 = w["proj_w" if L.index == 0 else "mlp_w2"]
                before = L.before + L.units + g * 2 * KT
                slot = 2 * (g % 2)
                if g == 0 and L.index == 0:
                    pool.wait_ge(pb0_full, at(0, B - 1, 16, use0("Q3") + 1))
                elif g == 0:
                    pool.wait_ge(pb_full, at(0, B - 1, USES, use1("KC3", True) + 1))
                elif g == 1 and L.index == 0:
                    pool.wait_ge(pb0_full, at(0, B - 1, 16, use0("O3", last=True) + 1))
                elif g == 1:
                    pool.wait_ge(pb_full, at(0, B - 1, USES, use1("O3", True) + 1))
                else:
                    pool.wait_ge(a_full, base(L, NGRP * TT) + (g - 1) * B * TT + ONE)
                srcs = [rows(w1, k, g * D) for k in range(KT)] + [rows(w2, g * KT + k) for k in range(KT)]
                for u in range(2 * KT):
                    load(srcs, u, before)
                    s, k = slot + u // KT, u % KT
                    split([(W[:, s, 0, k, :], W[:, s, 1, k, :])], [raw[:, u % 2, :]], u, before)
                    yield

            def mlp_weights(L, start):
                for g in range(start, NGRP):
                    for _ in mlp_group_weights(L, g):
                        pass

            def attention0():
                def spread(nb, b):
                    pool.wait_ge(kl_ready, at(0, nb, 1, 1))
                    if b is not None:
                        pool.wait_ge(s0_full, at(0, b, 2 * G, 2 * G))
                    for h in range(2):
                        for c in range(G):
                            last = pool.tensor_tensor(
                                KB[:, h, c, :].rearrange("p (j n) -> p j n", j=HG),
                                kk[:, h, c * C:(c + 1) * C].bitcast(F32).unsqueeze(1).to_broadcast([P, HG, C]),
                                HM.unsqueeze(2).to_broadcast([P, HG, C]), ALU.mult)
                        last.then_inc(k_spread, 1)

                def batch(b, last):
                    def probs(c):
                        for u in (2 * c, 2 * c + 1):
                            pool.wait_ge(s0_inv, at(0, b, 2 * G, u + 1))
                            wait_apart(pool, (pt_full, at(0, b, 2 * G, 2 * c - 2)))
                            pool.tensor_tensor(pn[:, u % 4, :].rearrange("p (m n) -> p m n", m=8),
                                               ex[:, u % 2, :].rearrange("p (m n) -> p m n", m=8),
                                               rc[:, u % 2, :].unsqueeze(2).to_broadcast([P, 8, C]),
                                               ALU.mult).then_inc(prob_ready, 1)
                    probs(0)
                    probs(1)
                    probs(2)
                    pool.wait_ge(res_loaded, at(0, b, 16, 16))
                    for t in range(TT):
                        pool.tensor_tensor(res0[:, t, :], res0[:, t, :], brow[:, :], ALU.add).then_inc(res_biased, 1)
                    probs(3)
                    if not last:
                        spread(b + 1, b)

                pool.wait_ge(brow_loaded, 16 + ONE)
                pool.wait_ge(consts, 4 + ONE)
                spread(0, None)
                with pool.Fori(0, B - 1) as b:
                    batch(b, False)
                batch(B - 1, True)

            def attention1():
                def batch(b, last):
                    more = mlp_group_weights(LAYERS[1], 0) if last else None
                    for n in range(BSTEP):
                        m, r = C if STEPS[n % NSTEP][1] == TT else P, n % PRING
                        if by_act(n):
                            wait_apart(pool, (p_exp, at(0, b, BSTEP, n + 1)))
                            pool.tensor_tensor(pl[0:m, r, :], pf[0:m, r, :], ph[0:m, r, :].bitcast(F32),
                                               ALU.subtract).then_inc(p_lo_pool, 1)
                        else:
                            wait_apart(pool, (p_exp, at(0, b, BSTEP, n + 1)), (pv_step, at(0, b, BSTEP, n - PRING + 1)))
                            pool.tensor_scalar(ph[0:m, r, :], pf[0:m, r, :], 1.0, 0.0,
                                               ALU.mult, ALU.add).then_inc(p_hi, 1)
                        if last and n >= 2 * NSTEP and n % 5 == 0:
                            next(more, None)
                    if last:
                        for _ in more:
                            pass
                    for t in range(TT):
                        wait_apart(pool, (xres_loaded[t % 2], at(0, b, 32, 16 * (t // 2 + 1))))
                        pool.tensor_tensor(res[:, t % 2, :], res[:, t % 2, :], brow[:, :], ALU.add)\
                            .then_inc(xres_biased, 1)

                pool.wait_ge(brow_loaded, 16 * 3 + ONE)
                with pool.Fori(0, B - 1) as b:
                    batch(b, False)
                batch(B - 1, True)

            for u in range(2 * KT, 4 * KT):
                s_, k = (0, 3)[u // KT - 2], u % KT
                pool.wait_ge(w0_hi, u + 1 + ONE)
                pool.tensor_tensor(W[:, s_, 1, k, :], first_w[u // KT][:, u % KT, :], W[:, s_, 0, k, :].bitcast(F32),
                                   ALU.subtract).then_inc(w0_qo, 1)
            attention0()
            mlp_weights(LAYERS[0], 0)
            attention_weights(LAYERS[1])
            attention1()
            mlp_weights(LAYERS[1], 1)

        @block.scalar
        def _(act):
            def attention0():
                def sqrt(nb):
                    act.wait_ge(var0_ready, at(0, nb, 1, 1))
                    act.activation(sdev[:, :], mv[:, :, 1], ACT.Sqrt, bias=cols[:, NPAR:NPAR + 1])\
                        .then_inc(sd0_ready, 1)

                def full(b, u, first=False, last=False):
                    n = use0(u, first=first, last=last)
                    act.wait_ge(pb0_full, at(0, b, 16, n + 1))
                    return bank[n % 2]

                def turned_tokens(nb, b, first, ks):
                    for k in ks:
                        src = full(b, f"T{k}", first)
                        act.activation(src[:, :], src[:, :], ACT.Identity, bias=par("ln1_b", k),
                                       scale=par("ln1_w", k)).then_inc(y0_affine, 1)
                        act.wait_ge(y0_affine, at(0, nb, KT, k + 1))
                        act.activation(xT0[:, 0, k, :], src[:, :], ACT.Copy).then_inc(in_hi, 1)

                def front(nb, b, first):
                    src = full(b, "C", first)
                    act.activation(cT0[:, 0, :, :], src[:, :].rearrange("p (k n) -> p k n", k=KT),
                                   ACT.Copy).then_inc(in_hi, 1)
                    act.wait_ge(pb0_free, at(0, b, 16, use0("K1", first=first) + 1))
                    act.wait_ge(k_spread, at(0, nb, 2, 0))
                    act.activation(kk[:, 0, :], kf, ACT.Copy).then_inc(kh_ready, 1)

                def values(b, first):
                    src = full(b, "V", first)
                    if not first:
                        act.wait_ge(o0_full, at(0, b, G, G))
                    for i in range(2):
                        for a in range(PAIRS):
                            rows, o = slice(i * C, (i + 1) * C), (2 * a + i) * HD
                            last = act.activation(
                                VB[rows, 0, :, a, o:o + HD],
                                src[rows, :].rearrange("p (c n) -> p c n", c=G)[:, :, o:o + HD], ACT.Copy)
                    last.then_inc(v_hi, 1)

                def batch(b, last):
                    def q_hi(c):
                        src = full(b, f"Q{c}")
                        act.wait_ge(s0_full, at(0, b, 2 * G, 2 * c - 2))
                        act.activation(qg[:, c % 2, 0, :], src[:, :], ACT.Identity, bias=par("q_b", c))\
                            .then_inc(q_hi_ready, 1)

                    def exp(c):
                        for u in (2 * c, 2 * c + 1):
                            wait_apart(act, (s0_less, at(0, b, 2 * G, u + 1)))
                            act.activation(ex[:, u % 2, :], ex[:, u % 2, :], ACT.Exp, scale=anyk[:, ds(b, 1)])\
                                .then_inc(s0_exp, 1)

                    def p_hi_(c):
                        act.wait_ge(o0_full, at(0, b, G, c - 1))
                        for a in range(PAIRS):
                            act.wait_ge(pt_full, at(0, b, 2 * G, 2 * c + a + 1))
                            act.activation(PT[:, c % 2, a, 0, :], bank[4 + a][:, :], ACT.Copy).then_inc(pt_hi, 1)

                    def o_hi_(c):
                        act.wait_ge(o0_full, at(0, b, G, c + 1))
                        act.wait_ge(pb0_full, at(0, b, 16, 8))
                        act.activation(aT[:, 0, c, :], bank[6 + c % 2][:, :], ACT.Identity, bias=par("v_b", c))\
                            .then_inc(o0_hi, 1)

                    q_hi(0)
                    q_hi(1)
                    exp(0)
                    for c in range(G):
                        if c + 2 < G:
                            q_hi(c + 2)
                        if c + 1 < G:
                            exp(c + 1)
                        p_hi_(c)
                        if c:
                            o_hi_(c - 1)
                        if c == G - 2 and not last:
                            sqrt(b + 1)
                    o_hi_(G - 1)
                    if not last:
                        turned_tokens(b + 1, b, False, range(KT))
                        front(b + 1, b, False)
                        values(b, False)

                def weights_hi(i):
                    act.wait_ge(w0_loaded[i], 16 + ONE)
                    for k in range(KT):
                        act.activation(W[:, (1, 2, 0, 3)[i], 0, k, :], first_w[i][:, k, :], ACT.Copy).then_inc(w0_hi, 1)

                sqrt(0)
                weights_hi(0)
                act.wait_ge(consts, 3 + ONE)
                turned_tokens(0, 0, True, range(KT))
                front(0, 0, True)
                weights_hi(1)
                weights_hi(2)
                act.wait_ge(consts, 4 + ONE)
                values(0, True)
                weights_hi(3)
                with act.Fori(0, B - 1) as b:
                    batch(b, False)
                batch(B - 1, True)

            def attention1():
                def full(b, u, last, first):
                    n = use1(u, last, first)
                    act.wait_ge(pb_full, at(0, b, USES, n + 1))
                    return bank[n % 2]

                def hi(b, u, last=False, first=False):
                    kind = u.lstrip("n")
                    if kind[0] in "QK":
                        c = int(kind[-1])
                        own = b + 1 if u[0] == "n" and not first else b
                        if not (first and c == 0):
                            wait_apart(act, (parted["QK".index(kind[0])][(c + 1) % 2],
                                             at(0, own, 32, 16 * ((c - 1) // 2 + 1) if c else 0)))
                    src = full(b, u, last, first)
                    if kind[0] == "T":
                        dst, src = xT[:, 0, int(kind[1:]), :], src[:, :]
                    elif kind == "C":
                        dst, src = cT[:, 0, :, :], src[:, 0:KT * C].rearrange("p (k n) -> p k n", k=KT)
                    elif kind[0] == "V":
                        t = int(kind[1:])
                        if not first:
                            wait_apart(act, (pv_step, at(0, b, BSTEP, BSTEP)))
                        m = C if t == TT else P
                        dst, src = VP[0:m, t, :, 0:HD], src[0:m, :].rearrange("p (h d) -> p h d", h=H)
                    elif kind[0] == "Q":
                        act.activation(qt[:, 0, :], src[:, :], ACT.Identity, bias=par("q_b1", int(kind[1:])))\
                            .then_inc(act_out, 1)
                        return
                    else:
                        o, n = (S, C) if kind[1] == "C" else (0, S)
                        act.activation(kt[:, 0, o:o + n], src[:, 0:n], ACT.Identity, bias=par("k_b1", int(kind[-1])))\
                            .then_inc(act_out, 1)
                        return
                    act.activation(dst, src, ACT.Copy).then_inc(act_out, 1)

                def batch(b, last):
                    def exp(n):
                        m, r = C if STEPS[n % NSTEP][1] == TT else P, n % PRING
                        before = n - PRING
                        waits = [(s_full, at(0, b, BSTEP, n + 1))]
                        if before < 0:
                            waits += [(p_lo, at(0, b, BSTEP - ACT_STEPS, 0)), (p_lo_pool, at(0, b, ACT_STEPS, 0))]
                        elif by_act(before):
                            waits += [(p_lo_pool, at(0, b, ACT_STEPS, kind_count(before)))]
                        else:
                            waits += [(p_lo, at(0, b, BSTEP - ACT_STEPS, kind_count(before)))]
                        if by_act(n):
                            waits += [(pv_step, at(0, b, BSTEP, n - PRING + 1))]
                        wait_apart(act, *waits)
                        src = bank[4 + n % 2][0:m, :]
                        if by_act(n):
                            act.activation(ph[0:m, r, :], src, ACT.Exp, scale=SCALE1)
                        act.activation(pf[0:m, r, :], src, ACT.Exp, scale=SCALE1).then_inc(p_exp, 1)

                    def o_out(h):
                        wait_apart(act, (pv_step, at(0, b, BSTEP, (h + 1) * (TT + 1))),
                                   (o_moved[h % 2], at(0, b, 128, 16 * (h // 2))), (o_free, at(0, b, H, h - 1)))
                        act.activation(sg[0:2 * HD + 1, h % 2, :], bank[6 + h % 2][0:2 * HD + 1, :], ACT.Copy)\
                            .then_inc(sg_ready, 1)

                    for c in range(G):
                        at_step = {s0 + n: u for s0, n, u in fillers(c, last)}
                        for i in range(NSTEP):
                            exp(NSTEP * c + i)
                            if i in at_step:
                                hi(b, at_step[i], last)
                            j, t = divmod(i - LAG - 1, TT + 1)
                            if t == TT and 0 <= j < HG - 1:
                                o_out(HG * c + j)
                        o_out(HG * c + HG - 1)
                    if not last:
                        for t in range(TT + 1):
                            hi(b, f"nV{t}")
                    for k in range(KT):
                        wait_apart(act, (pb_free, at(0, b, USES, use1(f"B{k}", last) + 1)))
                        act.activation(oa[:, k, :], oa[:, k, :], ACT.Identity, bias=par("v_b1", k)).then_inc(v_biased, 1)
                    for t in range(TT):
                        wait_apart(act, (v_biased, at(0, b, KT, KT)),
                                   (pb_full, at(0, b, USES, use1(f"O{t - 2}", last) + 1 if t >= 2 else len(FIRST))))
                        act.activation(AS[:, t % 2, 0, :, :], oa[:, :, t * P:(t + 1) * P], ACT.Copy).then_inc(as_hi, 1)

                for u in split_by_act(FIRST):
                    hi(0, u, first=True)
                with act.Fori(0, B - 1) as b:
                    batch(b, False)
                batch(B - 1, True)

            def mlp(L):
                def sqrt(nb, h):
                    act.wait_ge(var_ready, at(base(L, 2), nb, 2, h + 1))
                    act.activation(sdev[:, 0:HALF], mv[:, 0:HALF, 1], ACT.Sqrt,
                                   bias=cols[:, NPAR + L.index:NPAR + L.index + 1]).then_inc(sd_ready, 1)

                def turned(nb, u, b3=3):
                    act.wait_ge(t_full, at(base(L, 4), nb, 4, u + 1))
                    src = bank[b3][:, :].rearrange("p (k n) -> p k n", k=2)
                    for i in range(2):
                        k = 2 * (u % 2) + i
                        if L.index == 0:
                            op = act.activation(src[:, i, :], src[:, i, :], ACT.Identity, bias=par("ln2_b", k),
                                                scale=par("ln2_w", k))
                        else:
                            op = act.activation(src[:, i, :], src[:, i, :], ACT.Copy, scale=par("post_w", k))
                    op.then_inc(act_own, 1)
                    wait_apart(act, (act_own, at(base(L, 4), nb, 4, u + 1)))
                    k = 2 * (u % 2)
                    act.activation(yT[:, 0, k:k + 2, ds(nb * S + (u // 2) * HALF * P, HALF * P)], src, ACT.Copy)\
                        .then_inc(y_hi, 1)

                b1 = col["fc_b" if L.index == 0 else "mlp_b1"]

                def batch(b, g, ahead):
                    def gelu(i):
                        n = base(L, NGRP * NCH) + g * B * NCH + i
                        wait_apart(act, (f_full, b * NCH + (n + 1 + ONE)), (g_lo, b * NCH + (n - min(i, 1) + ONE)))
                        act.activation(gf[:, i % 2, :], bank[FC1_BANK[i]][:, :], ACT.Gelu_apprx_tanh,
                                       bias=cols[:, b1 + g * NCH + i:b1 + g * NCH + i + 1]).then_inc(g_act, 1)
                    gelu(0)
                    if ahead:
                        sqrt(b + 1, 0)
                    gelu(1)
                    if ahead:
                        turned(b + 1, 0)
                    gelu(2)
                    if ahead:
                        turned(b + 1, 1)
                        sqrt(b + 1, 1)
                    gelu(3)
                    if ahead:
                        turned(b + 1, 2)
                        turned(b + 1, 3)

                sqrt(0, 0)
                turned(0, 0, 0)
                sqrt(0, 1)
                for u in range(1, 4):
                    turned(0, u, u)
                with act.Fori(0, B - 1) as b:
                    batch(b, 0, True)
                batch(B - 1, 0, False)
                for g in range(1, NGRP):
                    with act.Fori(0, B) as b:
                        batch(b, g, False)

            act.wait_ge(consts, 2 + ONE)
            attention0()
            mlp(LAYERS[0])
            attention1()
            mlp(LAYERS[1])

        @block.vector
        def _(dve):
            own = [0]

            def link(ins):
                own[0] += 1
                ins.then_inc(dve_own, 1)
                dve.wait_ge(dve_own, own[0] + ONE)

            def norm0(nb):
                dve.wait_ge(tok_loaded, at(0, nb, 16, 16))
                for t in range(TT):
                    last = dve.bn_stats(stats[:, t, :], tok0[:, t, :])
                last.then_inc(tok_normed, 1)
                wait_apart(dve, (tok_normed, at(0, nb, 3, 1)))
                for t in range(TT):
                    last = dve.bn_aggr(mv[:, t, :], stats[:, t, :])
                last.then_inc(var0_ready, 1)
                dve.wait_ge(sd0_ready, at(0, nb, 1, 1))
                dve.reciprocal(rstd[:, :], sdev[:, :]).then_inc(tok_normed, 1)
                dve.wait_ge(tok_normed, at(0, nb, 3, 2))
                for t in range(TT):
                    last = dve.tensor_scalar(tok0[:, t, :], tok0[:, t, :], mv[:, t, 0:1], rstd[:, t:t + 1],
                                             ALU.subtract, ALU.mult)
                last.then_inc(tok_normed, 1)

            dve.memset(cols[:, NPAR:NPAR + 1], 1e-5).then_inc(consts, 1)
            dve.memset(cols[:, NPAR + 1:NPAR + 2], 1e-6).then_inc(consts, 1)
            norm0(0)
            dve.wait_ge(par_turned, 1 + ONE)
            link(dve.tensor_copy(cols[:, 0:NPAR], bank[7][:, 0:NPAR]))
            dve.wait_ge(ident_ready, 2 + ONE)
            link(dve.tensor_copy(pick.rearrange("p (h n) -> p h n", h=H),
                                 ident[C:C + H, C:C + H].unsqueeze(2).to_broadcast([H, H, HD])))
            dve.memset(cols[:, NPAR + 2:NPAR + 3], 0.0).then_inc(consts, 1)

            def attention0():
                def turned_tokens(nb, k, first):
                    dve.wait_ge(in_hi, at(0, nb, KT + 1, k + 1))
                    split_lo(xT0[:, 1, k, :], bank[use0(f"T{k}", first=first) % 2][:, :], xT0[:, 0, k, :], pb0_free)

                def front(nb, b, first):
                    dve.wait_ge(in_hi, at(0, nb, KT + 1, KT + 1))
                    split_lo(cT0[:, 1, :, :], bank[use0("C") % 2][:, :].rearrange("p (k n) -> p k n", k=KT),
                             cT0[:, 0, :, :], pb0_free)
                    for i in range(2):
                        n = use0(f"K{i}", first=first)
                        dve.wait_ge(pb0_full, at(0, b, 16, n + 1))
                        dve.wait_ge(kl_ready, at(0, nb, 1, 0))
                        half = kf[:, i * 2 * C:(i + 1) * 2 * C].rearrange("p (c n) -> p c n", c=2)
                        kb = cols[:, col["k_b"] + 2 * i:col["k_b"] + 2 * i + 2]
                        dve.tensor_tensor(half, bank[n % 2][:, 0:2 * C].rearrange("p (c n) -> p c n", c=2),
                                          kb.unsqueeze(2).to_broadcast([P, 2, C]), ALU.add).then_inc(pb0_free, 1)

                def keys_lo(nb):
                    dve.wait_ge(kh_ready, at(0, nb, 1, 1))
                    split_lo(kk[:, 1, :], kf, kk[:, 0, :], kl_ready)

                def values(nb, b, first):
                    src = bank[use0("V") % 2]
                    dve.wait_ge(v_hi, at(0, nb, 1, 1))
                    for i in range(2):
                        for a in range(PAIRS):
                            rows, o = slice(i * C, (i + 1) * C), (2 * a + i) * HD
                            last = dve.tensor_tensor(
                                VB[rows, 1, :, a, o:o + HD],
                                src[rows, :].rearrange("p (c n) -> p c n", c=G)[:, :, o:o + HD],
                                VB[rows, 0, :, a, o:o + HD].bitcast(F32), ALU.subtract)
                    last.then_inc(pb0_free, 1)

                def batch(b, last):
                    def q_lo(c):
                        dve.wait_ge(q_hi_ready, at(0, b, G, c + 1))
                        dve.scalar_tensor_tensor(out=qg[:, c % 2, 1, :], in0=bank[c % 2][:, :],
                                                 scalar=par("q_b", c), in1=qg[:, c % 2, 0, :].bitcast(F32),
                                                 op0=ALU.add, op1=ALU.subtract).then_inc(pb0_free, 1)

                    def less_max(c):
                        for u in (2 * c, 2 * c + 1):
                            s_ = bank[2 + u % 2][:, :].rearrange("p (m n) -> p m n", m=8)
                            dve.wait_ge(s0_full, at(0, b, 2 * G, u + 1))
                            dve.tensor_reduce(mx[:, u % 2, :], s_, AX_X, ALU.max).then_inc(s0_max, 1)
                            dve.wait_ge(s0_max, at(0, b, 2 * G, u + 1))
                            dve.wait_ge(prob_ready, at(0, b, 2 * G, u - 1))
                            dve.tensor_tensor(ex[:, u % 2, :].rearrange("p (m n) -> p m n", m=8), s_,
                                              mx[:, u % 2, :].unsqueeze(2).to_broadcast([P, 8, C]),
                                              ALU.subtract).then_inc(s0_less, 1)

                    def inv_sum(c):
                        for u in (2 * c, 2 * c + 1):
                            dve.wait_ge(s0_exp, at(0, b, 2 * G, u + 1))
                            dve.tensor_reduce(sm[:, u % 2, :], ex[:, u % 2, :].rearrange("p (m n) -> p m n", m=8),
                                              AX_X, ALU.add).then_inc(s0_sum, 1)
                            dve.wait_ge(s0_sum, at(0, b, 2 * G, u + 1))
                            dve.reciprocal(rc[:, u % 2, :], sm[:, u % 2, :]).then_inc(s0_inv, 1)

                    def p_lo_(c):
                        for a in range(PAIRS):
                            dve.wait_ge(pt_hi, at(0, b, 2 * G, 2 * c + a + 1))
                            split_lo(PT[:, c % 2, a, 1, :], bank[4 + a][:, :], PT[:, c % 2, a, 0, :], pt_lo)

                    def o_lo_(c):
                        dve.wait_ge(o0_hi, at(0, b, G, c + 1))
                        dve.scalar_tensor_tensor(out=aT[:, 1, c, :], in0=bank[6 + c % 2][:, :],
                                                 scalar=par("v_b", c), in1=aT[:, 0, c, :].bitcast(F32),
                                                 op0=ALU.add, op1=ALU.subtract).then_inc(o0_lo, 1)

                    q_lo(0)
                    q_lo(1)
                    less_max(0)
                    inv_sum(0)
                    for c in range(G):
                        if c + 2 < G:
                            q_lo(c + 2)
                        if c + 1 < G:
                            less_max(c + 1)
                        if c + 1 < G:
                            inv_sum(c + 1)
                        p_lo_(c)
                        if c:
                            o_lo_(c - 1)
                        if c == G - 2 and not last:
                            norm0(b + 1)
                    o_lo_(G - 1)
                    for t in range(TT):
                        n = use0(f"O{t}", last)
                        dve.wait_ge(pb0_full, at(0, b, 16, n + 1))
                        dve.wait_ge(res_biased, at(0, b, TT, t + 1))
                        dve.tensor_tensor(res0[:, t, :], bank[n % 2][:, :], res0[:, t, :], ALU.add)\
                            .then_inc(pb0_free, 1)
                        if not last:
                            turned_tokens(b + 1, t, False)
                    if not last:
                        front(b + 1, b, False)
                        keys_lo(b + 1)
                        values(b + 1, b, False)

                def weights_lo(i):
                    for k in range(KT):
                        dve.wait_ge(w0_hi, KT * i + k + 1 + ONE)
                        split_lo(W[:, 1 + i, 1, k, :], first_w[i][:, k, :], W[:, 1 + i, 0, k, :], w0_kv)

                weights_lo(0)
                for k in range(KT):
                    turned_tokens(0, k, True)
                front(0, 0, True)
                keys_lo(0)
                weights_lo(1)
                link(dve.tensor_copy(maskf, maskr))
                link(dve.tensor_reduce(anyk[:, :], maskf.rearrange("p (b c) -> p b c", b=B), AX_X, ALU.max))
                link(dve.tensor_scalar(maskf[0:1, :], maskf[0:1, :], 1.0, BIG, ALU.subtract, ALU.mult))
                for b in range(B):
                    dve.tensor_scalar(kbias[0:1, 0, b * C:(b + 1) * C], maskf[0:1, b * C:(b + 1) * C],
                                      anyk[0:1, b:b + 1], None, ALU.mult)
                link(dve.tensor_copy(mask2f, mask2))
                link(dve.tensor_scalar(kbias[0:1, 1, :], mask2f, 0.0, -BIG, ALU.is_equal, ALU.mult))
                link(dve.tensor_scalar(anyk[:, :], anyk[:, :], float(SCALE0), None, ALU.mult))
                link(dve.memset(VB_[:, :].bitcast(F32), 0.0))
                dve.memset(KM_[:, :].bitcast(F32), 0.0)
                dve.memset(first_[:, :].bitcast(F32), 0.0)
                link(dve.memset(HM, 0.0))
                for j in range(HG):
                    dve.memset(HM[j * HD:(j + 1) * HD, j:j + 1], 1.0)
                dve.memset(first_[0:1, :].bitcast(F32), 1.0)
                dve.tensor_copy(KM_[0:1, :].rearrange("p (b j n) -> p b j n", b=B, j=HG),
                                kbias[0:1, 0, :].bitcast(F32).rearrange("p (b n) -> p b n", b=B)
                                .unsqueeze(2).to_broadcast([1, B, HG, C])).then_inc(consts, 1)

                values(0, 0, True)
                with dve.Fori(0, B - 1) as b:
                    batch(b, False)
                batch(B - 1, True)

            def split_lo(dst, src, hi, sem_):
                dve.tensor_tensor(dst, src, hi.bitcast(F32), ALU.subtract).then_inc(sem_, 1)

            def attention1():
                def lo(b, u, last=False, first=False):
                    kind = u.lstrip("n")
                    dve.wait_ge(act_out, at(0, b, SPLITS, split1(u, last, first) + 1))
                    src = bank[use1(u, last, first) % 2]
                    if kind[0] == "T":
                        k = int(kind[1:])
                        split_lo(xT[:, 1, k, :], src[:, :], xT[:, 0, k, :], pb_free)
                    elif kind == "C":
                        split_lo(cT[:, 1, :, :], src[:, 0:KT * C].rearrange("p (k n) -> p k n", k=KT),
                                 cT[:, 0, :, :], pb_free)
                    elif kind[0] == "V":
                        t = int(kind[1:])
                        m = C if t == TT else P
                        split_lo(VP[0:m, t, :, HD:2 * HD], src[0:m, :].rearrange("p (h d) -> p h d", h=H),
                                 VP[0:m, t, :, 0:HD], pb_free)
                    elif kind[0] == "Q":
                        dve.scalar_tensor_tensor(out=qt[:, 1, :], in0=src[:, :], scalar=par("q_b1", int(kind[1:])),
                                                 in1=qt[:, 0, :].bitcast(F32), op0=ALU.add,
                                                 op1=ALU.subtract).then_inc(pb_free, 1)
                    else:
                        o, n = (S, C) if kind[1] == "C" else (0, S)
                        dve.scalar_tensor_tensor(out=kt[:, 1, o:o + n], in0=src[:, 0:n], scalar=par("k_b1", int(kind[-1])),
                                                 in1=kt[:, 0, o:o + n].bitcast(F32), op0=ALU.add,
                                                 op1=ALU.subtract).then_inc(pb_free, 1)

                def max_step(nb, c, i):
                    j, t = STEPS[i]
                    dve.wait_ge(mm_full, at(0, nb, BSTEP, NSTEP * c + i + 1))
                    if t < TT:
                        dve.tensor_reduce(nm_main[:, TT * j + t:TT * j + t + 1], bank[2 + i % 2][:, :], AX_X, ALU.max,
                                          negate=True).then_inc(mm_free, 1)
                    else:
                        dve.tensor_reduce(nm_ctx[:, TT * j:TT * j + TT],
                                          bank[2 + i % 2][:, 0:TT * C].rearrange("p (q n) -> p q n", q=TT),
                                          AX_X, ALU.max, negate=True).then_inc(mm_free, 1)

                def max_join(nb, c):
                    dve.wait_ge(mm_free, at(0, nb, BSTEP, NSTEP * (c + 1)))
                    dve.tensor_tensor(nm, nm_main, nm_ctx, ALU.min).then_inc(nm_ready, 1)

                def max_turned(b, u, nb, c, last=False, first=False):
                    n = use1(u, last, first)
                    dve.wait_ge(pb_full, at(0, b, USES, n + 1))
                    dve.wait_ge(maxed[c % 2], at(0, nb, 32, 16 * (c // 2)))
                    dve.tensor_copy(nT[:, c % 2, :], bank[n % 2][0:H, 0:P]).then_inc(pb_free, 1)

                def batch(b, last):
                    def lo_p(n):
                        if n < 0 or by_act(n):
                            return
                        m, r = C if STEPS[n % NSTEP][1] == TT else P, n % PRING
                        dve.wait_ge(p_hi, at(0, b, BSTEP - ACT_STEPS, kind_count(n)))
                        split_lo(pl[0:m, r, :], pf[0:m, r, :], ph[0:m, r, :], p_lo)

                    def o_sum(h):
                        j = h % HG
                        dve.wait_ge(sg_ready, at(0, b, H, h + 1))
                        dve.tensor_tensor(oa[HD * j:HD * j + HD, h // HG, :], bank[6 + h % 2][HD:2 * HD, :],
                                          sg[0:HD, h % 2, :], ALU.add).then_inc(o_free, 1)

                    for c in range(G):
                        at_step = {s0 + n + 1: u for s0, n, u in fillers(c, last)}
                        ahead = not (last and c == G - 1)
                        nb, nc_ = (b, c + 1) if c + 1 < G else (b + 1, 0)
                        for i in range(NSTEP):
                            if ahead:
                                for m in max_items(i):
                                    max_step(nb, nc_, m)
                                if i == TURN:
                                    max_turned(b, f"R{nc_}" if c + 1 < G else "nR0", nb, nc_, last)
                                if i == TURN - 1:
                                    max_join(nb, nc_)
                            if i:
                                lo_p(NSTEP * c + i - 1)
                            if i in at_step:
                                lo(b, at_step[i], last)
                            j, t = divmod(i - LAG - 2, TT + 1)
                            if t == TT and 0 <= j < HG - 1:
                                o_sum(HG * c + j)
                        lo_p(NSTEP * (c + 1) - 1)
                        o_sum(HG * c + HG - 1)

                    def inverse():
                        for r in range(2):
                            dve.wait_ge(o_moved[r], at(0, b, 128, 128))
                        dve.reciprocal(s16, s16).then_inc(r_ready, 1)
                    if not last:
                        lo(b, "nV0")
                        lo(b, "nV1")
                    inverse()
                    if not last:
                        for t in range(2, TT + 1):
                            lo(b, f"nV{t}")
                    for k in range(KT):
                        n = use1(f"B{k}", last)
                        dve.wait_ge(pb_full, at(0, b, USES, n + 1))
                        dve.tensor_tensor(oa[:, k, :], bank[n % 2][:, :], oa[:, k, :], ALU.mult).then_inc(pb_free, 1)
                    for t in range(TT + 1):
                        if t < TT:
                            dve.wait_ge(as_hi, at(0, b, TT, t + 1))
                            split_lo(AS[:, t % 2, 1, :, :], oa[:, :, t * P:(t + 1) * P], AS[:, t % 2, 0, :, :], as_lo)
                        if t:
                            n = use1(f"O{t - 1}", last)
                            dve.wait_ge(pb_full, at(0, b, USES, n + 1))
                            dve.wait_ge(xres_biased, at(0, b, TT, t))
                            dve.tensor_tensor(res[:, (t - 1) % 2, :], bank[n % 2][:, :], res[:, (t - 1) % 2, :],
                                              ALU.add).then_inc(pb_free, 1)

                for u in split_by_act(FIRST):
                    lo(0, u, first=True)
                    for slot, at_q, at_k in ((0, "nC", "nQ0"), (1, "nK0", "nKC0")):
                        if u == at_q:
                            dve.memset(QS[ROWMASK:P, slot, :, :].bitcast(F32), 1.0)
                        elif u == at_k:
                            link(dve.memset(KS[ROWMASK:P, slot, :, :].bitcast(F32), 1.0))
                            op = dve.memset(KS[ROWMASK:ROWMASK + 1, slot, :, 0:S].bitcast(F32), 0.0)
                    if u == "nKC0":
                        link(op)
                        dve.memset(VP[:, :, :, 2 * HD:VW].bitcast(F32), 1.0).then_inc(consts, 1)
                for i in range(NSTEP):
                    max_step(0, 0, i)
                max_join(0, 0)
                max_turned(0, "nR0", 0, 0, first=True)
                with dve.Fori(0, B - 1) as b:
                    batch(b, False)
                batch(B - 1, True)

            def mlp(L):
                per = 3 if L.index == 0 else 5
                n0 = 6 * B if L.index else 0

                def norm(nb, h, nt=nt):
                    def step(k):
                        return at(n0, nb, 2 * per, h * per + k)
                    dve.wait_ge(nt_loaded[h], at(base(L, 16), nb, 16, 16))
                    for t in range(HALF):
                        op = dve.bn_stats(stats[:, t, :], nt[:, t, :])
                    op.then_inc(normed, 1)
                    wait_apart(dve, (normed, step(1)))
                    for t in range(HALF):
                        op = dve.bn_aggr(mv[:, t, :], stats[:, t, :])
                    if L.index == 0:
                        op.then_inc(var_ready, 1)
                    else:
                        op.then_inc(normed, 1)
                        dve.wait_ge(normed, step(2))
                        dve.tensor_tensor(sdev[:, 0:HALF], mv[:, 0:HALF, 0], mv[:, 0:HALF, 0], ALU.mult).then_inc(normed, 1)
                        dve.wait_ge(normed, step(3))
                        dve.tensor_tensor(mv[:, 0:HALF, 1], mv[:, 0:HALF, 1], sdev[:, 0:HALF], ALU.add).then_inc(var_ready, 1)
                    dve.wait_ge(sd_ready, at(base(L, 2), nb, 2, h + 1))
                    dve.reciprocal(rstd[:, 0:HALF], sdev[:, 0:HALF]).then_inc(normed, 1)
                    dve.wait_ge(normed, step(per - 1))
                    for t in range(HALF):
                        if L.index == 0:
                            op = dve.tensor_scalar(nt[:, t, :], nt[:, t, :], mv[:, t, 0:1], rstd[:, t:t + 1],
                                                   ALU.subtract, ALU.mult)
                        else:
                            op = dve.tensor_scalar(nt[:, t, :], nt[:, t, :], rstd[:, t:t + 1], None, ALU.mult)
                    op.then_inc(normed, 1)

                def turned(nb, u, b3=3):
                    k, where = 2 * (u % 2), ds(nb * S + (u // 2) * HALF * P, HALF * P)
                    wait_apart(dve, (y_hi, at(base(L, 4), nb, 4, u + 1)))
                    split_lo(yT[:, 1, k:k + 2, where], bank[b3][:, :].rearrange("p (k n) -> p k n", k=2),
                             yT[:, 0, k:k + 2, where], y_ready)

                def batch(b, g, ahead):
                    n0_ = base(L, NGRP * NCH) + g * B * NCH

                    def gelu(i):
                        dve.wait_ge(g_act, b * NCH + (n0_ + i + 1 + ONE))
                        if i == 0:
                            dve.wait_ge(a_full, b * NCH + (n0_ + ONE))
                        dve.tensor_copy(gs[:, 0, i, :], gf[:, i % 2, :]).then_inc(g_hi, 1)
                        dve.wait_ge(g_hi, b * NCH + (n0_ + i + 1 + ONE))
                        split_lo(gs[:, 1, i, :], gf[:, i % 2, :], gs[:, 0, i, :], g_lo)
                    gelu(0)
                    if ahead:
                        norm(b + 1, 0)
                    gelu(1)
                    if ahead:
                        turned(b + 1, 0)
                    gelu(2)
                    if ahead:
                        turned(b + 1, 1)
                        norm(b + 1, 1)
                    gelu(3)
                    if ahead:
                        turned(b + 1, 2)
                        turned(b + 1, 3)
                    if g == 0:
                        dve.wait_ge(acc_loaded, 16 * B * (L.index + 1) + ONE)
                        dve.wait_ge(brow_loaded, 16 * (2 * L.index + 2) + ONE)
                        for t in range(TT):
                            a = acc_[:, ds(b * (TT * D) + t * D, D)]
                            dve.tensor_tensor(a, a, brow[:, :], ALU.add).then_inc(biased, 1)
                    for t in range(TT):
                        dve.wait_ge(a_full, b * NCH + (n0_ + t + 1 + ONE))
                        if g == 0:
                            dve.wait_ge(biased, at(base(L, TT), b, TT, t + 1))
                        a = acc_[:, ds(b * (TT * D) + t * D, D)]
                        dve.tensor_tensor(a, bank[4 + t][:, :], a, ALU.add).then_inc(acc_added, 1)

                norm(0, 0)
                turned(0, 0, 0)
                norm(0, 1, gf)
                for u in range(1, 4):
                    turned(0, u, u)
                with dve.Fori(0, B - 1) as b:
                    batch(b, 0, True)
                batch(B - 1, 0, False)
                for g in range(1, NGRP):
                    with dve.Fori(0, B) as b:
                        batch(b, g, False)

            attention0()
            mlp(LAYERS[0])
            attention1()
            mlp(LAYERS[1])

        @block.tensor
        def _(pe):
            HL = ((0, 0), (0, 1), (1, 0))

            pe.wait_ge(par_loaded, 16 * (len(order) + 2) + ONE)
            pe.wait_ge(ident_ready, 2 + ONE)
            pe.transpose(bank[7][:, 0:NPAR], par_rows, ident[0:NPAR, 0:NPAR]).then_inc(par_turned, 1)

            def attention0():
                def free(b, u, first=False, last=False):
                    n = use0(u, first=first, last=last)
                    pe.wait_ge(pb0_free, at(0, b, 16, n - 1))
                    return bank[n % 2]

                def turn_tokens(nb, b, first, ks):
                    pe.wait_ge(tok_normed, at(0, nb, 3, 3))
                    for k in ks:
                        dst = free(b, f"T{k}", first)
                        for t in range(TT):
                            last = pe.transpose(dst[:, t * P:(t + 1) * P], tok0[:, t, k * P:(k + 1) * P], ident[:, :])
                        last.then_inc(pb0_full, 1)

                def front(nb, b, first):
                    dst = free(b, "C", first)
                    pe.wait_ge(ctx_loaded, at(0, nb, 32, 32))
                    for k in range(KT):
                        last = pe.transpose(dst[:, k * P:(k + 1) * P], ctok0[:, k * P:(k + 1) * P], ident[:, :])
                    last.then_inc(pb0_full, 1)
                    if first:
                        pe.wait_ge(w0_kv, KT + ONE)
                    for i in range(2):
                        dst = free(b, f"K{i}", first)
                        pe.wait_ge(pb0_free, at(0, b, 16, use0("C", first=first) + 1))
                        for c in (2 * i, 2 * i + 1):
                            for k in range(KT):
                                for a, d in HL:
                                    last = pe.matmul(dst[:, (c % 2) * C:(c % 2) * C + C],
                                                     W[:, 1, a, k, c * P:(c + 1) * P], cT0[:, d, k, 0:C],
                                                     start=(k == 0 and a == 0 and d == 0),
                                                     stop=(k == KT - 1 and a == 1))
                        last.then_inc(pb0_full, 1)

                def values(b, first):
                    dst = free(b, "V", first)
                    for k in range(KT):
                        for a, d in HL:
                            last = pe.matmul(dst[:, :], cT0[:, a, k, :], W[:, 2, d, k, :],
                                             start=(k == 0 and a == 0 and d == 0),
                                             stop=(k == KT - 1 and a == 1))
                    last.then_inc(pb0_full, 1)

                def batch(b, last_batch):
                    def q_proj(c):
                        dst = free(b, f"Q{c}")
                        for k in range(KT):
                            for a, d in HL:
                                last = pe.matmul(dst[:, :], W[:, 0, a, k, c * P:(c + 1) * P], xT0[:, d, k, :],
                                                 start=(k == 0 and a == 0 and d == 0),
                                                 stop=(k == KT - 1 and a == 1))
                        last.then_inc(pb0_full, 1)

                    def scores(c):
                        pe.wait_ge(pb0_free, at(0, b, 16, use0(f"Q{c}") + 1))
                        if c == 0:
                            pe.wait_ge(k_spread, at(0, b, 2, 2))
                        for u in (2 * c, 2 * c + 1):
                            pe.wait_ge(s0_less, at(0, b, 2 * G, u - 1))
                            for i in range(2):
                                dst = bank[2 + u % 2][:, i * HG * C:(i + 1) * HG * C]
                                q = (2 * (u % 2) + i) * P
                                for a, d in HL:
                                    pe.matmul(dst, qg[:, c % 2, a, q:q + P], KB[:, d, c, :],
                                              start=(a == 0 and d == 0), stop=False)
                                last = pe.matmul(dst, first_[:, :], KM_[:, ds(b * (HG * C), HG * C)],
                                                 start=False, stop=True)
                            last.then_inc(s0_full, 1)

                    def turn(c):
                        pe.wait_ge(prob_ready, at(0, b, 2 * G, 2 * c + 2))
                        for a in range(PAIRS):
                            pe.wait_ge(pt_lo, at(0, b, 2 * G, 2 * c - 1 + a))
                            for q in range(TT):
                                o = (q % 2) * HG * C + a * P
                                last = pe.transpose(bank[4 + a][:, q * P:(q + 1) * P],
                                                    pn[:, (2 * c + q // 2) % 4, o:o + P], ident[:, :])
                            last.then_inc(pt_full, 1)

                    def out_(c):
                        pe.wait_ge(pt_lo, at(0, b, 2 * G, 2 * c + 2))
                        pe.wait_ge(o0_lo, at(0, b, G, c - 1))
                        for a in range(PAIRS):
                            for v, p in HL:
                                last = pe.matmul(bank[6 + c % 2][:, :], VB[:, v, c, a, :], PT[:, c % 2, a, p, :],
                                                 start=(a == 0 and v == 0 and p == 0),
                                                 stop=(a == PAIRS - 1 and v == 1))
                        last.then_inc(o0_full, 1)

                    q_proj(0)
                    q_proj(1)
                    scores(0)
                    for c in range(G):
                        if c + 2 < G:
                            q_proj(c + 2)
                        if c + 1 < G:
                            scores(c + 1)
                        turn(c)
                        if c:
                            out_(c - 1)
                    out_(G - 1)
                    pe.wait_ge(w0_qo, 2 * KT + ONE)
                    pe.wait_ge(o0_lo, at(0, b, G, G))
                    for t in range(TT):
                        dst = free(b, f"O{t}", last=last_batch)
                        for k in range(KT):
                            for a, d in HL:
                                last = pe.matmul(dst[:, :], aT[:, a, k, t * P:(t + 1) * P], W[:, 3, d, k, :],
                                                 start=(k == 0 and a == 0 and d == 0),
                                                 stop=(k == KT - 1 and a == 1))
                        last.then_inc(pb0_full, 1)
                        if not last_batch:
                            turn_tokens(b + 1, b, False, (t,))
                    if not last_batch:
                        front(b + 1, b, False)
                        values(b, False)

                turn_tokens(0, 0, True, range(KT))
                front(0, 0, True)
                pe.wait_ge(w0_kv, 2 * KT + ONE)
                values(0, True)
                pe.wait_ge(consts, 4 + ONE)
                pe.wait_ge(w0_qo, KT + ONE)
                with pe.Fori(0, B - 1) as b:
                    batch(b, False)
                batch(B - 1, True)

            def attention1():
                U = LAYERS[1].before

                def free(b, u, last, first):
                    n = use1(u, last, first)
                    pe.wait_ge(pb_free, at(0, b, USES, n - 1))
                    return bank[n % 2]

                def project(b, u, part, parts, last=False, first=False):
                    kind = u.lstrip("n")
                    nb = b if first else b + 1
                    n = use1(u, last, first)
                    dst = free(b, u, last, first) if part == 0 else bank[n % 2]
                    if kind[0] == "T":
                        k = int(kind[1:])
                        if k == 0:
                            wait_apart(pe, (x_loaded, at(0, nb, 16, 16)))
                        for t in range(TT):
                            op = pe.transpose(dst[:, t * P:(t + 1) * P], tok[:, t, k * P:(k + 1) * P], ident[:, :])
                    elif kind == "C":
                        wait_apart(pe, (c_loaded, at(0, nb, 16, 16)))
                        for k in range(KT):
                            op = pe.transpose(dst[:, k * C:(k + 1) * C], ctok[:, k * P:(k + 1) * P], ident[0:C, 0:C])
                    else:
                        if first:
                            pe.wait_ge(pb_free, use1("nC", first=True) + 1 + ONE)
                            pe.wait_ge(w_lo, U + {"Q": KT, "K": 3 * KT, "V": 5 * KT}[kind[0]] + ONE)
                        elif kind == "Q0":
                            wait_apart(pe, (pb_free, at(0, b, USES, use1("nC", last) + 1)))
                        mine = [(k, a, d) for k in range(KT) for a, d in HL]
                        mine = mine[len(mine) * part // parts:len(mine) * (part + 1) // parts]
                        for k, a, d in mine:
                            start, stop = (k, a, d) == (0, 0, 0), (k, a) == (KT - 1, 1)
                            if kind[0] == "V":
                                t = int(kind[1:])
                                m = C if t == TT else P
                                src = cT[:, a, k, :] if t == TT else xT[:, a, k, t * P:(t + 1) * P]
                                op = pe.matmul(dst[0:m, :], src, W[:, 2, d, k, :], start=start, stop=stop)
                            else:
                                c = int(kind[-1])
                                src, m = (cT, C) if kind[:2] == "KC" else (xT, S)
                                op = pe.matmul(dst[:, 0:m], W[:, "QK".index(kind[0]), a, k, c * P:(c + 1) * P],
                                               src[:, d, k, :], start=start, stop=stop)
                    if part == parts - 1:
                        op.then_inc(pb_full, 1)

                def max_step(nb, c, i):
                    j, t = STEPS[i]
                    if t == 0 and j % 2 == 0:
                        wait_apart(pe, (stacked[c % 2][j // 2], at(0, nb, STACK, stack_count(c))))
                    pe.wait_ge(mm_free, at(0, nb, BSTEP, NSTEP * c + i - 1))
                    if t < TT:
                        pe.matmul(bank[2 + i % 2][:, :], QS[0:ROWMAX, c % 2, j, t * P:(t + 1) * P],
                                  KS[0:ROWMAX, c % 2, j, 0:S], start=True, stop=True).then_inc(mm_full, 1)
                    else:
                        for q in range(TT):
                            op = pe.matmul(bank[2 + i % 2][:, q * C:(q + 1) * C], QS[0:ROWMAX, c % 2, j, q * P:(q + 1) * P],
                                           KS[0:ROWMAX, c % 2, j, S:NK], start=True, stop=True)
                        op.then_inc(mm_full, 1)

                def max_turn(b, u, nb, c, last=False, first=False):
                    dst = free(b, u, last, first)
                    wait_apart(pe, (nm_ready, at(0, nb, G, c + 1)))
                    pe.transpose(dst[0:H, 0:P], nm, ident[:, :]).then_inc(pb_full, 1)

                def batch(b, last):
                    def scores(n):
                        c, i = divmod(n, NSTEP)
                        j, t = STEPS[i]
                        if i == 0:
                            wait_apart(pe, (maxed[c % 2], at(0, b, 32, 16 * (c // 2 + 1))))
                        pe.wait_ge(p_exp, at(0, b, BSTEP, n - 1))
                        m = C if t == TT else P
                        pe.matmul(bank[4 + n % 2][0:m, :], KS[0:ROWMAX + 1, c % 2, j, t * P:t * P + m],
                                  QS[0:ROWMAX + 1, c % 2, j, :], start=True, stop=True).then_inc(s_full, 1)

                    def values(n):
                        j, t = STEPS[n % NSTEP]
                        h = HG * (n // NSTEP) + j
                        m = C if t == TT else P
                        if t == 0:
                            wait_apart(pe, (o_free, at(0, b, H, h - 1)))
                        if by_act(n):
                            pe.wait_ge(p_lo_pool, at(0, b, ACT_STEPS, kind_count(n)))
                        else:
                            pe.wait_ge(p_lo, at(0, b, BSTEP - ACT_STEPS, kind_count(n)))
                        v = VP[0:m, t, h, 0:2 * HD + 1]
                        o = bank[6 + h % 2][0:2 * HD + 1, :]
                        pe.matmul(o, v, ph[0:m, n % PRING, :], start=(t == 0), stop=False)
                        pe.matmul(o, v, pl[0:m, n % PRING, :], start=False, stop=(t == TT)).then_inc(pv_step, 1)

                    for c in range(G):
                        at_step = {s0 + part: (u, part, n) for s0, n, u in fillers(c, last) for part in range(n)}
                        ahead = not (last and c == G - 1)
                        nb, nc_ = (b, c + 1) if c + 1 < G else (b + 1, 0)
                        for i in range(NSTEP):
                            scores(NSTEP * c + i)
                            if ahead:
                                for m in max_items(i):
                                    max_step(nb, nc_, m)
                            if i >= LAG:
                                values(NSTEP * c + i - LAG)
                            if i in at_step:
                                u, part, n = at_step[i]
                                project(b, u, part, n, last)
                            if ahead and i == TURN:
                                max_turn(b, f"R{nc_}" if c + 1 < G else "nR0", nb, nc_, last)
                        for i in range(NSTEP - LAG, NSTEP):
                            values(NSTEP * c + i)
                    if not last:
                        for t in range(TT + 1):
                            project(b, f"nV{t}", 0, 1)
                    for k in range(KT):
                        dst = free(b, f"B{k}", last, False)
                        if k == 0:
                            wait_apart(pe, (r_ready, at(0, b, 1, 1)))
                        pe.matmul(dst[:, :], pick[:, k * P:(k + 1) * P], s16, start=True, stop=True).then_inc(pb_full, 1)
                    for t in range(TT):
                        dst = free(b, f"O{t}", last, False)
                        wait_apart(pe, (as_lo, at(0, b, TT, t + 1)))
                        for k in range(KT):
                            for a, d in HL:
                                op = pe.matmul(dst[:, :], AS[:, t % 2, a, k, :], W[:, 3, d, k, :],
                                               start=(k == 0 and a == 0 and d == 0),
                                               stop=(k == KT - 1 and a == 1))
                        op.then_inc(pb_full, 1)

                for u in FIRST[:-1]:
                    if u == "nV0":
                        pe.wait_ge(consts, 5 + ONE)
                    project(0, u, 0, 1, first=True)
                for i in range(NSTEP):
                    max_step(0, 0, i)
                max_turn(0, "nR0", 0, 0, first=True)
                pe.wait_ge(w_lo, U + 6 * KT + ONE)
                with pe.Fori(0, B - 1) as b:
                    batch(b, False)
                batch(B - 1, True)

            def mlp(L):
                per = 3 if L.index == 0 else 5
                n0 = 6 * B if L.index else 0

                def turn(nb, u, nt=nt, b3=3):
                    wait_apart(pe, (normed, at(n0, nb, 2 * per, (u // 2 + 1) * per)))
                    if nt is not gf and b3 == 3:
                        wait_apart(pe, (y_ready, at(base(L, 4), nb, 4, u)))
                    for i in range(2):
                        k = 2 * (u % 2) + i
                        for t in range(HALF):
                            op = pe.transpose(bank[b3][:, (i * HALF + t) * P:(i * HALF + t + 1) * P],
                                              nt[:, t, k * P:(k + 1) * P], ident[:, :])
                    op.then_inc(t_full, 1)

                def batch(b, g, ahead):
                    n = base(L, NGRP * NCH) + g * B * NCH
                    slot = 2 * (g % 2)

                    def fc1(i):
                        if i == 0 and g == 0:
                            wait_apart(pe, (y_ready, at(base(L, 4), b, 4, 4)))
                        if i in (0, 3):
                            wait_apart(pe, (g_act, b * NCH + (n + (i == 3) + ONE)))
                        for k in range(KT):
                            for a, d in HL:
                                op = pe.matmul(bank[FC1_BANK[i]][:, :], W[:, slot, a, k, i * P:(i + 1) * P],
                                               yT[:, d, k, ds(b * S, S)],
                                               start=(k == 0 and a == 0 and d == 0),
                                               stop=(k == KT - 1 and a == 1))
                        op.then_inc(f_full, 1)

                    def fc2(i):
                        if i == 0:
                            wait_apart(pe, (acc_added, b * NCH + (n + ONE)))
                        pe.wait_ge(g_lo, b * NCH + (n + i + 1 + ONE))
                        for t in range(TT):
                            for a, d in HL:
                                op = pe.matmul(bank[4 + t][:, :], gs[:, a, i, t * P:(t + 1) * P],
                                               W[:, slot + 1, d, i, :],
                                               start=(i == 0 and a == 0 and d == 0),
                                               stop=(i == NCH - 1 and a == 1))
                            if i == NCH - 1:
                                op.then_inc(a_full, 1)
                    fc1(0)
                    fc1(1)
                    fc2(0)
                    if ahead:
                        turn(b + 1, 0)
                    fc1(2)
                    if ahead:
                        turn(b + 1, 1)
                    fc2(1)
                    fc1(3)
                    if ahead:
                        turn(b + 1, 2)
                    fc2(2)
                    if ahead:
                        turn(b + 1, 3)
                    fc2(3)

                for u in range(4):
                    turn(0, u, (nt, gf)[u // 2], u)
                pe.wait_ge(w_lo, L.before + L.units + 2 * KT + ONE)
                with pe.Fori(0, B - 1) as b:
                    batch(b, 0, True)
                batch(B - 1, 0, False)
                for g in range(1, NGRP):
                    pe.wait_ge(w_lo, L.before + L.units + (g + 1) * 2 * KT + ONE)
                    with pe.Fori(0, B) as b:
                        batch(b, g, False)

            attention0()
            mlp(LAYERS[0])
            attention1()
            mlp(LAYERS[1])


_WEIGHTS = {
    "ln1_w": "L0_xattn_ln1_w", "ln1_b": "L0_xattn_ln1_b", "q_w": "L0_xattn_q_w", "q_b": "L0_xattn_q_b",
    "k_w": "L0_xattn_k_w", "k_b": "L0_xattn_k_b", "v_w": "L0_xattn_v_w", "v_b": "L0_xattn_v_b",
    "cproj_w": "L0_xattn_cproj_w", "cproj_b": "L0_xattn_cproj_b", "ln2_w": "L0_xattn_ln2_w",
    "ln2_b": "L0_xattn_ln2_b", "fc_w": "L0_xattn_fc_w", "fc_b": "L0_xattn_fc_b",
    "proj_w": "L0_xattn_proj_w", "proj_b": "L0_xattn_proj_b", "q_w1": "L1_xattn_q_w",
    "q_b1": "L1_xattn_q_b", "kv_w": "L1_xattn_kv_w", "kv_b": "L1_xattn_kv_b", "out_w": "L1_xattn_out_w",
    "out_b": "L1_xattn_out_b", "post_w": "L1_xattn_postnorm_w", "mlp_w1": "L1_xattn_mlp_w1",
    "mlp_b1": "L1_xattn_mlp_b1", "mlp_w2": "L1_xattn_mlp_w2", "mlp_b2": "L1_xattn_mlp_b2",
}


def kernel(**inputs):
    import numpy as np
    import concourse.bacc as bacc
    from concourse.bass_utils import run_bass_kernel_spmd

    nc = bacc.Bacc("TRN2", target_bir_lowering=False, num_devices=1)
    arrays = {}

    def dram_in(name):
        a = np.ascontiguousarray(inputs[name])
        if a.dtype == np.bool_:
            a = a.view(np.uint8)
        arrays[f"in_{name}_dram"] = a
        return nc.dram_tensor(f"in_{name}_dram", a.shape, mybir.dt.from_np(a.dtype), kind="ExternalInput").ap()

    main = [dram_in(n) for n in ("x", "ctx_2048", "mask_BxS2_bf1", "mask_BxS2_ik0")]
    weights = {k: dram_in(v) for k, v in _WEIGHTS.items()}
    between = [nc.dram_tensor(n, (B, S, D), F32, kind="Internal").ap() for n in ("after_att0", "after_layer0", "after_att1")]
    out = nc.dram_tensor("out_0_dram", (B, S, D), F32, kind="ExternalOutput").ap()
    parts = [nc.dram_tensor(n, (2, P, 2, m), F32, kind="Internal").ap() for n, m in (("q_parts", S), ("k_parts", NK))]
    program(nc, *main, weights, *between, *parts, out)
    r = run_bass_kernel_spmd(nc, [arrays], core_ids=[0])
    return r.results[0]["out_0_dram"]
```
